# Optimizing a Trainium2 kernel written in Bass

```python
import numpy as np
import jax
import jax.numpy as jnp

def _softmax(x, axis=-1):
    return jax.nn.softmax(x, axis=axis)

def _gelu(x):
    return jax.nn.gelu(x, approximate=True)

def _silu(x):
    return jax.nn.silu(x)

def _sigmoid(x):
    return jax.nn.sigmoid(x)

def _layernorm(x, axis=-1, eps=1e-05):
    m = jnp.mean(x, axis=axis, keepdims=True)
    v = jnp.var(x, axis=axis, keepdims=True)
    return (x - m) / jnp.sqrt(v + eps)

def _scatter_add(tgt, idx, src, axis=0):
    return tgt.at[idx].add(src)

def _segment_sum(src, seg, n):
    return jax.ops.segment_sum(src, seg, n)
kernel_name = 'mk_sandwich_d2_jaxref_r8_8ca83f'

def setup_inputs(seed: int=0):
    np.random.seed(seed)
    _w = jnp.asarray

    def _L0_attn_setup():
        import jax, jax.numpy as jnp
        import numpy as np
        from jax.scipy.linalg import solve_triangular
        B, L, D, H = (1, 256, 128, 4)
        DK = DV = D // H
        CONV = 4
        FIR_S, FIR_M, FIR_L = (3, 15, 63)
        CHUNK = 32

        def _l2norm(x):
            return x * jax.lax.rsqrt(jnp.sum(x * x, -1, keepdims=True) + 1e-06)

        def _short_conv(x, w):
            K = w.shape[-1]
            l = x.shape[1]
            xp = jnp.pad(x, ((0, 0), (K - 1, 0), (0, 0)))
            y = sum((xp[:, j:j + l, :] * w[:, j] for j in range(K)))
            return jax.nn.silu(y)

        def _fir(x, filt):
            b, l, h, d = x.shape
            K = filt.shape[-1]
            xf = jnp.transpose(x.reshape(b, l, h * d), (0, 2, 1))
            y = jax.lax.conv_general_dilated(xf, filt.reshape(h * d, 1, K), (1,), [(K - 1, 0)], feature_group_count=h * d)
            return jnp.transpose(y, (0, 2, 1)).reshape(b, l, h, d)

        def _delta_rule_chunkwise(q, k, v, beta):
            b, h, Lq, dk = q.shape
            c = CHUNK
            n = Lq // c
            q = _l2norm(q)
            k = _l2norm(k)
            v = v * beta[..., None]
            kb = k * beta[..., None]
            rs = lambda t: t.reshape(b, h, n, c, t.shape[-1])
            qc, kc, vc, kbc = (rs(q), rs(k), rs(v), rs(kb))
            tri_strict = jnp.tril(jnp.ones((c, c), bool), -1)
            A = jnp.where(tri_strict, -(kbc @ jnp.swapaxes(kc, -1, -2)), 0.0)
            eye = jnp.eye(c, dtype=q.dtype)
            M = eye - A
            T = solve_triangular(M, jnp.broadcast_to(eye, M.shape), lower=True)
            u = T @ vc
            w = T @ kbc
            causal = jnp.tril(jnp.ones((c, c), bool))

            def step(S, inp):
                q_i, k_i, u_i, w_i = inp
                attn = jnp.where(causal, q_i @ jnp.swapaxes(k_i, -1, -2), 0.0)
                u_adj = u_i - w_i @ S
                o_i = q_i @ S + attn @ u_adj
                return (S + jnp.swapaxes(k_i, -1, -2) @ u_adj, o_i)
            S0 = jnp.zeros((b, h, dk, v.shape[-1]), q.dtype)
            mv = lambda t: jnp.moveaxis(t, 2, 0)
            _, o = jax.lax.scan(step, S0, (mv(qc), mv(kc), mv(u), mv(w)))
            return jnp.moveaxis(o, 0, 2).reshape(b, h, Lq, -1)

        def _rmsnorm(x, w, eps=1e-05):
            return x * jax.lax.rsqrt(jnp.mean(x * x, -1, keepdims=True) + eps) * w
        key = jax.random.key(seed)
        ks = jax.random.split(key, 16)
        wn = lambda k, shape, s: jax.random.normal(k, shape, jnp.float32) * s

        def fir_init(k, K):
            f = jnp.zeros((H, DV, K), jnp.float32).at[..., -1].set(1.0)
            return f + wn(k, (H, DV, K), 0.01)
        return {'hidden_states': jax.random.normal(ks[0], (B, L, D), jnp.float32), 'Wq': wn(ks[1], (D, D), 0.02), 'Wk': wn(ks[2], (D, D), 0.02), 'Wv': wn(ks[3], (D, D), 0.02), 'Wb': wn(ks[4], (H, D), 0.02), 'conv_q': wn(ks[5], (D, CONV), 0.1), 'conv_k': wn(ks[6], (D, CONV), 0.1), 'conv_v': wn(ks[7], (D, CONV), 0.1), 'fir_s': fir_init(ks[8], FIR_S), 'fir_m': fir_init(ks[9], FIR_M), 'fir_l': fir_init(ks[10], FIR_L), 'gate_w': wn(ks[11], (H, 5, D), 1.0 / np.sqrt(D)), 'gate_b': jnp.zeros((H, 5), jnp.float32), 'log_temp': jnp.zeros((H, 1), jnp.float32), 'eps_param': jnp.full((H, 1), 0.02, jnp.float32), 'norm_w': jnp.ones((DV,), jnp.float32), 'Wo': wn(ks[12], (D, D), 0.02)}
    _L0_attn_in = _L0_attn_setup()

    def _L0_ffn_setup():
        import jax, jax.numpy as jnp
        import numpy as np
        TOP_K = 2
        EPS = 1e-05

        def layer_norm(x, g, b):
            mu = jnp.mean(x, axis=-1, keepdims=True)
            var = jnp.mean(jnp.square(x - mu), axis=-1, keepdims=True)
            return (x - mu) * jax.lax.rsqrt(var + EPS) * g + b
        key = jax.random.key(seed)
        ks = jax.random.split(key, 12)
        B, S, D, F, E = (2, 256, 128, 512, 8)
        std = 0.02
        return {'x': jax.random.normal(ks[0], (B, S, D), jnp.float32), 'g1': jnp.ones((D,), jnp.float32), 'be1': jnp.zeros((D,), jnp.float32), 'mix_w': jax.random.normal(ks[1], (D, D), jnp.float32) * std, 'mix_b': jnp.zeros((D,), jnp.float32), 'g2': jnp.ones((D,), jnp.float32), 'be2': jnp.zeros((D,), jnp.float32), 'router_w': jax.random.normal(ks[2], (D, E), jnp.float32) * std, 'w1': jax.random.normal(ks[3], (E, D, F), jnp.float32) * std, 'b1': jnp.zeros((E, F), jnp.float32), 'w2': jax.random.normal(ks[4], (E, F, D), jnp.float32) * std, 'b2': jnp.zeros((E, D), jnp.float32)}
    _L0_ffn_in = _L0_ffn_setup()

    def _L1_attn_setup():
        import jax, jax.numpy as jnp
        import numpy as np
        B, S, D = (2, 512, 128)
        EPS = 1e-05

        def _rmsnorm(x, gamma):
            ss = jnp.sum(jnp.square(x), axis=-1, keepdims=True)
            inv = jax.lax.rsqrt(ss + EPS)
            return inv * x * gamma * x.shape[-1] ** 0.5

        def _gate_loop_operator(kv, q, a):

            def binop(e_i, e_j):
                a_i, kv_i = e_i
                a_j, kv_j = e_j
                return (a_j * a_i, a_j * kv_i + kv_j)
            _, y = jax.lax.associative_scan(binop, (a, kv), axis=1)
            return q * y
        key = jax.random.key(seed)
        ks = jax.random.split(key, 7)
        x = jax.random.normal(ks[0], (B, S, D), dtype=jnp.float32)
        gamma = jnp.ones((D,), dtype=jnp.float32)
        wq, wk, wv, wa, wg, wo = (jax.random.normal(k, (D, D), dtype=jnp.float32) for k in ks[1:7])
        return {'x': x, 'gamma': gamma, 'wq': wq, 'wk': wk, 'wv': wv, 'wa': wa, 'wg': wg, 'wo': wo}
    _L1_attn_in = _L1_attn_setup()

    def _L1_ffn_setup():
        import jax, jax.numpy as jnp
        import numpy as np
        B, S, D_MODEL, D_FF = (4, 256, 128, 512)

        def _quantum_transform(hidden, theta, w_real, w_imag):
            imag = w_imag * jnp.sin(theta + hidden * 0.1)
            quantum_phase = jnp.cos(theta) * w_real + jnp.sin(theta) * w_imag
            return hidden + quantum_phase * imag * 0.1
        key = jax.random.key(seed)
        ks = jax.random.split(key, 8)
        return {'x': jax.random.normal(ks[0], (B, S, D_MODEL), dtype=jnp.float32), 'W1': jax.random.normal(ks[1], (D_MODEL, D_FF), dtype=jnp.float32) * (1.0 / np.sqrt(D_MODEL)), 'b1': jnp.zeros((D_FF,), dtype=jnp.float32), 'quantum_phases': jax.random.normal(ks[2], (D_FF,), dtype=jnp.float32) * (2.0 * np.pi), 'quantum_weights_real': jax.random.normal(ks[3], (D_FF,), dtype=jnp.float32) * 0.1, 'quantum_weights_imag': jax.random.normal(ks[4], (D_FF,), dtype=jnp.float32) * 0.1, 'W2': jax.random.normal(ks[5], (D_FF, D_MODEL), dtype=jnp.float32) * (1.0 / np.sqrt(D_FF)), 'b2': jnp.zeros((D_MODEL,), dtype=jnp.float32)}
    _L1_ffn_in = _L1_ffn_setup()
    _d = {'L0_attn_hidden_states': _L0_attn_in['hidden_states'], 'L0_attn_Wq': _L0_attn_in['Wq'], 'L0_attn_Wk': _L0_attn_in['Wk'], 'L0_attn_Wv': _L0_attn_in['Wv'], 'L0_attn_Wb': _L0_attn_in['Wb'], 'L0_attn_conv_q': _L0_attn_in['conv_q'], 'L0_attn_conv_k': _L0_attn_in['conv_k'], 'L0_attn_conv_v': _L0_attn_in['conv_v'], 'L0_attn_fir_s': _L0_attn_in['fir_s'], 'L0_attn_fir_m': _L0_attn_in['fir_m'], 'L0_attn_fir_l': _L0_attn_in['fir_l'], 'L0_attn_gate_w': _L0_attn_in['gate_w'], 'L0_attn_gate_b': _L0_attn_in['gate_b'], 'L0_attn_log_temp': _L0_attn_in['log_temp'], 'L0_attn_eps_param': _L0_attn_in['eps_param'], 'L0_attn_norm_w': _L0_attn_in['norm_w'], 'L0_attn_Wo': _L0_attn_in['Wo'], 'L0_ffn_g1': _L0_ffn_in['g1'], 'L0_ffn_be1': _L0_ffn_in['be1'], 'L0_ffn_mix_w': _L0_ffn_in['mix_w'], 'L0_ffn_mix_b': _L0_ffn_in['mix_b'], 'L0_ffn_g2': _L0_ffn_in['g2'], 'L0_ffn_be2': _L0_ffn_in['be2'], 'L0_ffn_router_w': _L0_ffn_in['router_w'], 'L0_ffn_w1': _L0_ffn_in['w1'], 'L0_ffn_b1': _L0_ffn_in['b1'], 'L0_ffn_w2': _L0_ffn_in['w2'], 'L0_ffn_b2': _L0_ffn_in['b2'], 'L1_attn_gamma': _L1_attn_in['gamma'], 'L1_attn_wq': _L1_attn_in['wq'], 'L1_attn_wk': _L1_attn_in['wk'], 'L1_attn_wv': _L1_attn_in['wv'], 'L1_attn_wa': _L1_attn_in['wa'], 'L1_attn_wg': _L1_attn_in['wg'], 'L1_attn_wo': _L1_attn_in['wo'], 'L1_ffn_W1': _L1_ffn_in['W1'], 'L1_ffn_b1': _L1_ffn_in['b1'], 'L1_ffn_quantum_phases': _L1_ffn_in['quantum_phases'], 'L1_ffn_quantum_weights_real': _L1_ffn_in['quantum_weights_real'], 'L1_ffn_quantum_weights_imag': _L1_ffn_in['quantum_weights_imag'], 'L1_ffn_W2': _L1_ffn_in['W2'], 'L1_ffn_b2': _L1_ffn_in['b2']}
    _x0 = _d['L0_attn_hidden_states']
    _d['L0_attn_hidden_states'] = jax.random.normal(jax.random.fold_in(jax.random.key(seed), 1), (16, 512, 128), dtype=_x0.dtype)
    del _x0
    return _d

def reference(L0_attn_hidden_states, L0_attn_Wq, L0_attn_Wk, L0_attn_Wv, L0_attn_Wb, L0_attn_conv_q, L0_attn_conv_k, L0_attn_conv_v, L0_attn_fir_s, L0_attn_fir_m, L0_attn_fir_l, L0_attn_gate_w, L0_attn_gate_b, L0_attn_log_temp, L0_attn_eps_param, L0_attn_norm_w, L0_attn_Wo, L0_ffn_g1, L0_ffn_be1, L0_ffn_mix_w, L0_ffn_mix_b, L0_ffn_g2, L0_ffn_be2, L0_ffn_router_w, L0_ffn_w1, L0_ffn_b1, L0_ffn_w2, L0_ffn_b2, L1_attn_gamma, L1_attn_wq, L1_attn_wk, L1_attn_wv, L1_attn_wa, L1_attn_wg, L1_attn_wo, L1_ffn_W1, L1_ffn_b1, L1_ffn_quantum_phases, L1_ffn_quantum_weights_real, L1_ffn_quantum_weights_imag, L1_ffn_W2, L1_ffn_b2):

    def _L0_attn_ref(hidden_states, Wq, Wk, Wv, Wb, conv_q, conv_k, conv_v, fir_s, fir_m, fir_l, gate_w, gate_b, log_temp, eps_param, norm_w, Wo):
        import jax, jax.numpy as jnp
        import numpy as np
        from jax.scipy.linalg import solve_triangular
        B, L, D, H = (1, 256, 128, 4)
        DK = DV = D // H
        CONV = 4
        FIR_S, FIR_M, FIR_L = (3, 15, 63)
        CHUNK = 32

        def _l2norm(x):
            return x * jax.lax.rsqrt(jnp.sum(x * x, -1, keepdims=True) + 1e-06)

        def _short_conv(x, w):
            K = w.shape[-1]
            l = x.shape[1]
            xp = jnp.pad(x, ((0, 0), (K - 1, 0), (0, 0)))
            y = sum((xp[:, j:j + l, :] * w[:, j] for j in range(K)))
            return jax.nn.silu(y)

        def _fir(x, filt):
            b, l, h, d = x.shape
            K = filt.shape[-1]
            xf = jnp.transpose(x.reshape(b, l, h * d), (0, 2, 1))
            y = jax.lax.conv_general_dilated(xf, filt.reshape(h * d, 1, K), (1,), [(K - 1, 0)], feature_group_count=h * d)
            return jnp.transpose(y, (0, 2, 1)).reshape(b, l, h, d)

        def _delta_rule_chunkwise(q, k, v, beta):
            b, h, Lq, dk = q.shape
            c = CHUNK
            n = Lq // c
            q = _l2norm(q)
            k = _l2norm(k)
            v = v * beta[..., None]
            kb = k * beta[..., None]
            rs = lambda t: t.reshape(b, h, n, c, t.shape[-1])
            qc, kc, vc, kbc = (rs(q), rs(k), rs(v), rs(kb))
            tri_strict = jnp.tril(jnp.ones((c, c), bool), -1)
            A = jnp.where(tri_strict, -(kbc @ jnp.swapaxes(kc, -1, -2)), 0.0)
            eye = jnp.eye(c, dtype=q.dtype)
            M = eye - A
            T = solve_triangular(M, jnp.broadcast_to(eye, M.shape), lower=True)
            u = T @ vc
            w = T @ kbc
            causal = jnp.tril(jnp.ones((c, c), bool))

            def step(S, inp):
                q_i, k_i, u_i, w_i = inp
                attn = jnp.where(causal, q_i @ jnp.swapaxes(k_i, -1, -2), 0.0)
                u_adj = u_i - w_i @ S
                o_i = q_i @ S + attn @ u_adj
                return (S + jnp.swapaxes(k_i, -1, -2) @ u_adj, o_i)
            S0 = jnp.zeros((b, h, dk, v.shape[-1]), q.dtype)
            mv = lambda t: jnp.moveaxis(t, 2, 0)
            _, o = jax.lax.scan(step, S0, (mv(qc), mv(kc), mv(u), mv(w)))
            return jnp.moveaxis(o, 0, 2).reshape(b, h, Lq, -1)

        def _rmsnorm(x, w, eps=1e-05):
            return x * jax.lax.rsqrt(jnp.mean(x * x, -1, keepdims=True) + eps) * w
        b, l, d = hidden_states.shape
        q = _short_conv(hidden_states @ Wq.T, conv_q).reshape(b, l, H, DK)
        k = _short_conv(hidden_states @ Wk.T, conv_k).reshape(b, l, H, DK)
        v_direct = _short_conv(hidden_states @ Wv.T, conv_v).reshape(b, l, H, DV)
        beta = jax.nn.sigmoid(hidden_states @ Wb.T)
        tp = lambda t: jnp.transpose(t, (0, 2, 1, 3))
        delta_out = tp(_delta_rule_chunkwise(tp(q), tp(k), tp(v_direct), jnp.transpose(beta, (0, 2, 1))))
        local_s = _fir(v_direct, fir_s)
        local_m = _fir(v_direct, fir_m)
        local_l = _fir(v_direct, fir_l)
        logits = jnp.einsum('bld,hpd->blhp', hidden_states, gate_w) + gate_b
        temp = jnp.exp(log_temp).reshape(1, 1, H, 1)
        probs = jax.nn.softmax(logits / temp, -1)
        eps = jnp.clip(eps_param, 0.0, 0.2).reshape(1, 1, H, 1)
        probs = probs * (1.0 - 5.0 * eps) + eps
        o = probs[..., 0:1] * local_s + probs[..., 1:2] * local_m + probs[..., 2:3] * local_l + probs[..., 3:4] * delta_out + probs[..., 4:5] * v_direct
        o = _rmsnorm(o, norm_w)
        return o.reshape(b, l, H * DV) @ Wo.T

    def _L0_ffn_ref(x, g1, be1, mix_w, mix_b, g2, be2, router_w, w1, b1, w2, b2):
        import jax, jax.numpy as jnp
        import numpy as np
        TOP_K = 2
        EPS = 1e-05

        def layer_norm(x, g, b):
            mu = jnp.mean(x, axis=-1, keepdims=True)
            var = jnp.mean(jnp.square(x - mu), axis=-1, keepdims=True)
            return (x - mu) * jax.lax.rsqrt(var + EPS) * g + b
        res = x
        n = layer_norm(x, g1, be1)
        x = res + n + (n @ mix_w + mix_b)
        res = x
        n = layer_norm(x, g2, be2)
        B, S, D = n.shape
        E = w1.shape[0]
        flat = n.reshape(-1, D)
        probs = jax.nn.softmax(flat @ router_w, axis=-1)
        topw, topi = jax.lax.top_k(probs, TOP_K)
        combine = jnp.sum(jax.nn.one_hot(topi, E, dtype=flat.dtype) * topw[..., None], axis=1)
        h = jax.nn.silu(jnp.einsum('td,edf->tef', flat, w1) + b1)
        y = jnp.einsum('tef,efd->ted', h, w2) + b2
        out = jnp.einsum('te,ted->td', combine, y)
        return res + out.reshape(B, S, D)

    def _L1_attn_ref(x, gamma, wq, wk, wv, wa, wg, wo):
        import jax, jax.numpy as jnp
        import numpy as np
        B, S, D = (2, 512, 128)
        EPS = 1e-05

        def _rmsnorm(x, gamma):
            ss = jnp.sum(jnp.square(x), axis=-1, keepdims=True)
            inv = jax.lax.rsqrt(ss + EPS)
            return inv * x * gamma * x.shape[-1] ** 0.5

        def _gate_loop_operator(kv, q, a):

            def binop(e_i, e_j):
                a_i, kv_i = e_i
                a_j, kv_j = e_j
                return (a_j * a_i, a_j * kv_i + kv_j)
            _, y = jax.lax.associative_scan(binop, (a, kv), axis=1)
            return q * y
        x = _rmsnorm(x, gamma)
        q = x @ wq
        k = x @ wk
        v = x @ wv
        a = jax.nn.sigmoid(x @ wa)
        g = x @ wg
        kv = k * v
        y = _gate_loop_operator(kv, q, a)
        y = y * jax.nn.silu(g)
        return y @ wo

    def _L1_ffn_ref(x, W1, b1, quantum_phases, quantum_weights_real, quantum_weights_imag, W2, b2):
        import jax, jax.numpy as jnp
        import numpy as np
        B, S, D_MODEL, D_FF = (4, 256, 128, 512)

        def _quantum_transform(hidden, theta, w_real, w_imag):
            imag = w_imag * jnp.sin(theta + hidden * 0.1)
            quantum_phase = jnp.cos(theta) * w_real + jnp.sin(theta) * w_imag
            return hidden + quantum_phase * imag * 0.1
        hidden = jnp.einsum('bsd,df->bsf', x, W1) + b1
        q = _quantum_transform(hidden, quantum_phases, quantum_weights_real, quantum_weights_imag)
        act = jax.nn.relu(q)
        return jnp.einsum('bsf,fd->bsd', act, W2) + b2
    x = L0_attn_hidden_states
    x = x + _layernorm(_L0_attn_ref(_layernorm(x, axis=-1), L0_attn_Wq, L0_attn_Wk, L0_attn_Wv, L0_attn_Wb, L0_attn_conv_q, L0_attn_conv_k, L0_attn_conv_v, L0_attn_fir_s, L0_attn_fir_m, L0_attn_fir_l, L0_attn_gate_w, L0_attn_gate_b, L0_attn_log_temp, L0_attn_eps_param, L0_attn_norm_w, L0_attn_Wo), axis=-1)
    x = x + _layernorm(_L0_ffn_ref(_layernorm(x, axis=-1), L0_ffn_g1, L0_ffn_be1, L0_ffn_mix_w, L0_ffn_mix_b, L0_ffn_g2, L0_ffn_be2, L0_ffn_router_w, L0_ffn_w1, L0_ffn_b1, L0_ffn_w2, L0_ffn_b2), axis=-1)
    x = x + _layernorm(_L1_attn_ref(_layernorm(x, axis=-1), L1_attn_gamma, L1_attn_wq, L1_attn_wk, L1_attn_wv, L1_attn_wa, L1_attn_wg, L1_attn_wo), axis=-1)
    x = x + _layernorm(_L1_ffn_ref(_layernorm(x, axis=-1), L1_ffn_W1, L1_ffn_b1, L1_ffn_quantum_phases, L1_ffn_quantum_weights_real, L1_ffn_quantum_weights_imag, L1_ffn_W2, L1_ffn_b2), axis=-1)
    return x

_drawn_inputs = setup_inputs


def setup_inputs(seed=0):
    import zlib

    import numpy as np

    out = dict(_drawn_inputs(seed))
    spreads = {'L0_attn_gate_b': (0.0, 0.1),
     'L0_attn_log_temp': (0.0, 0.451),
     'L0_attn_eps_param': (0.019999999552965164, 0.6),
     'L0_attn_norm_w': (1.0, 0.2),
     'L0_ffn_g1': (1.0, 0.2),
     'L0_ffn_be1': (0.0, 0.1),
     'L0_ffn_mix_b': (0.0, 0.277),
     'L0_ffn_g2': (1.0, 0.6),
     'L0_ffn_be2': (0.0, 0.8),
     'L0_ffn_b1': (0.0, 0.8),
     'L0_ffn_b2': (0.0, 0.8),
     'L1_attn_gamma': (1.0, 0.2),
     'L1_ffn_b1': (0.0, 0.1),
     'L1_ffn_b2': (0.0, 0.1)}
    factors = {'L0_attn_fir_s': 8.0,
     'L0_ffn_router_w': 8.0,
     'L0_ffn_w1': 8.0,
     'L0_ffn_w2': 8.0,
     'L1_ffn_quantum_phases': 25.668,
     'L1_ffn_quantum_weights_real': 50.398,
     'L1_ffn_quantum_weights_imag': 8.0}
    for name, (base, spread) in spreads.items():
        noise = np.random.default_rng([zlib.crc32(name.encode()), seed]).standard_normal(out[name].shape)
        drawn = base * np.exp(spread * noise) if base else spread * noise
        out[name] = jnp.asarray(drawn.astype(out[name].dtype))
    for name, factor in factors.items():
        out[name] = (out[name] * factor).astype(out[name].dtype)
    return out
```

```python
import concourse.bass as bass
from concourse import mybir
from contextlib import ExitStack

FP32 = mybir.dt.float32
ALU = mybir.AluOpType
ACT = mybir.ActivationFunctionType
AX = mybir.AxisListType

BATCH, SEQ, D = 16, 512, 128
P = 128
TPS = SEQ // P
NT = BATCH * TPS
H, DH = 4, 32
CH = 32
CPT = P // CH
CPS = SEQ // CH
TAPS = 4
FIRS = (3, 15, 63)
WIN = 64
NWIN = SEQ // WIN
NGATE = 5
NE, FF = 8, 512
FC = FF // P
PADW = 2 * WIN + WIN - 1


class Chain:

    def __init__(self, eng, sem, turn=0, per_turn=0, start=0, waits=None):
        self.sem_of_waits = waits
        self.eng, self.sem, self.base, self.per_turn, self.n = eng, sem, turn * per_turn, per_turn, start

    def __call__(self, ins):
        self.n += 1
        ins.then_inc(self.sem, 1)
        self.eng.wait_ge(self.sem, self.base + self.n)

    def apart(self, ins):
        self(ins)
        self.eng.sem_inc(self.sem_of_waits, 1)

    def end(self):
        assert self.n == self.per_turn, (self.n, self.per_turn)


def wait_apart(eng, sem, value, waits):
    eng.wait_ge(sem, value)
    eng.sem_inc(waits, 1)


def tensors(nc, ctx, tag):
    ctx.callback(nc.all_engine_barrier)

    def sb(name, shape, dt=FP32):
        return ctx.enter_context(nc.sbuf_tensor(f"{tag}_{name}", shape, dt))

    def pb(name, shape, dt=FP32):
        return ctx.enter_context(nc.psum_tensor(f"{tag}_{name}", shape, dt))

    def sem(name):
        held = ctx.enter_context(nc.semaphore(f"{tag}_{name}"))
        ctx.callback(nc.gpsimd.sem_clear, held)
        return held

    return sb, pb, sem


def heads(ap):
    return ap.rearrange("p t (h d) -> p (t h) d", h=H)


def flat(ap):
    return ap.rearrange("p t d -> p (t d)")


def over(ap, n):
    return ap.unsqueeze(2).to_broadcast([ap.shape[0], ap.shape[1], n])


def row_stats(dve, link, x, st, mv):
    for t in range(TPS):
        ins = dve.bn_stats(st[:, t, :], x[:, t, :])
        if t == TPS - 1:
            link.apart(ins)
    for t in range(TPS):
        last = dve.bn_aggr(mv[:, t, :], st[:, t, :])
    return last


def delta_inputs(nc, x, w, scr, res):
    with ExitStack() as ctx:
        sb, pb, sem = tensors(nc, ctx, "di")
        wq, wk, wv = (sb(n, [D, D]) for n in ("wq", "wk", "wv"))
        wg = sb("wg", [D, H * NGATE + H])
        taps = sb("taps", [D, 3, TAPS])
        gate_b = sb("gate_b", [P, H * NGATE])
        log_temp = sb("log_temp", [P, H])
        mhalf = sb("mhalf", [P, H * TPS])
        lower = sb("lower", [P, CH])
        upper = sb("upper", [P, CH])
        zrow = sb("zrow", [WIN, D])
        st, mv, rstd = sb("st", [P, TPS, 6]), sb("mv", [P, TPS, 2]), sb("rstd", [P, TPS])
        xn = sb("xn", [P, TPS, D])
        xnT = sb("xnT", [D, SEQ])
        conv = [sb(f"conv{n}", [D, SEQ]) for n in range(3)]
        sig = [sb(f"sig{n}", [D, SEQ]) for n in range(3)]
        act = [sb(f"act{n}", [D, SEQ]) for n in range(3)]
        sq = [sb(f"sq{n}", [P, TPS, D]) for n in range(2)]
        ss = [sb(f"ss{n}", [P, TPS * H]) for n in range(2)]
        rn = [sb(f"rn{n}", [P, TPS * H]) for n in range(2)]
        qt, kt, kb, vt, vb = (sb(n, [P, TPS, D]) for n in ("qt", "kt", "kb", "vt", "vb"))
        qT, kT = sb("qT", [D, SEQ]), sb("kT", [D, SEQ])
        beta = sb("beta", [P, TPS * H])
        am, at = sb("am", [P, H, TPS, CH]), sb("at", [P, H, TPS, CH])
        A, B = pb("A", [P, 4, 512]), pb("B", [P, 4, 512])

        loaded, consts = sem("loaded"), sem("consts")
        stats_ready, eps_added, rstd_ready, xn_ready = sem("stats_ready"), sem("eps_added"), sem("rstd_ready"), sem("xn_ready")
        xT_done, xnT_ready, proj_done, gates_done, tap_done = sem("xT_done"), sem("xnT_ready"), sem("proj_done"), sem("gates_done"), sem("tap_done")
        conv_ready, sig_ready, act_ready = sem("conv_ready"), sem("sig_ready"), sem("act_ready")
        tok_done, sq_ready, ss_ready, ss_eps, rn_ready = sem("tok_done"), sem("sq_ready"), sem("ss_ready"), sem("ss_eps"), sem("rn_ready")
        tok_ready, back_done, back_ready, beta_ready = sem("tok_ready"), sem("back_done"), sem("back_ready"), sem("beta_ready")
        gram_done, am_ready, own, glog = sem("gram_done"), sem("am_ready"), sem("own"), sem("glog")
        stored, drained, zst, lt = sem("stored"), sem("drained"), sem("zst"), sem("lt")
        pool_waits, dve_waits, pe_waits = sem("pool_waits"), sem("dve_waits"), sem("pe_waits")
        block = ctx.enter_context(nc.Block())
        X, ident = res["x"], res["ident"]
        STORES = 7

        @block.sync
        def _(sp):
            sp.dma_start(X[:, :, :], x.rearrange("b (t p) d -> p (b t) d", p=P)).then_inc(loaded, 16)
            for dst, src in ((wq, "wqT"), (wk, "wkT"), (wv, "wvT"), (wg, "gatesT")):
                sp.dma_start(dst[:, :], w[src]).then_inc(loaded, 16)
            sp.dma_start(taps[:, :, :], w["taps"]).then_inc(loaded, 16)
            sp.dma_start(gate_b[:, :], w["gate_b"].partition_broadcast(P)).then_inc(loaded, 16)
            sp.dma_start(log_temp[:, :], w["log_temp"].partition_broadcast(P)).then_inc(loaded, 16)
            sp.dma_start(res["eps"][:, :], w["eps"].partition_broadcast(P)).then_inc(loaded, 16)
            sp.wait_ge(consts, 1)
            for b in range(BATCH):
                sp.dma_start(scr["v"][b, 0:WIN, :], zrow[:, :]).then_inc(zst, 16)
            sp.sem_inc(drained, 1)
            with sp.Fori(0, BATCH) as b:
                sp.wait_ge(tok_ready, 2 * b + 2)
                for name, src in (("k", kt), ("kb", kb), ("vb", vb)):
                    sp.dma_start(scr[name][b], flat(src[:, :, :])).then_inc(stored, 16)
                sp.dma_start(scr["v"][b, WIN:WIN + SEQ, :].rearrange("(t p) d -> p t d", p=P), vt[:, :, :]).then_inc(stored, 16)
                sp.wait_ge(back_ready, 2 * b + 2)
                sp.dma_start(scr["qT"][b], qT[:, :]).then_inc(stored, 16)
                sp.wait_ge(am_ready, 2 * b + 2)
                sp.dma_start(scr["A"][b], am[:, :, :, :].rearrange("p h t c -> p (h t c)")).then_inc(stored, 16)
                sp.dma_start(scr["attnT"][b], at[:, :, :, :].rearrange("p h t c -> p (h t c)")).then_inc(stored, 16)
                sp.wait_ge(stored, (b + 1) * (16 * STORES))
                sp.sem_inc(drained, 1)
            sp.wait_ge(zst, 16 * BATCH)

        @block.gpsimd
        def _(pool):
            const = Chain(pool, consts)
            for dst, value in ((zrow, 0.0), (ident, 0.0), (lower, 1.0), (upper, 1.0), (mhalf, -0.5)):
                const(pool.memset(dst[:, :], value))
            const(pool.affine_select(out=ident[:, :], in_=ident[:, :], compare_op=ALU.not_equal, fill=1.0,
                                     base=0, pattern=[[-1, P]], channel_multiplier=1))
            for c in range(CPT):
                rows = slice(CH * c, CH * c + CH)
                const(pool.affine_select(out=lower[rows, :], in_=lower[rows, :], compare_op=ALU.is_gt, fill=0.0,
                                         base=0, pattern=[[-1, CH]], channel_multiplier=1))
                const(pool.affine_select(out=upper[rows, :], in_=upper[rows, :], compare_op=ALU.is_ge, fill=0.0,
                                         base=0, pattern=[[1, CH]], channel_multiplier=-1))
            with pool.Fori(0, BATCH) as b:
                wait_apart(pool, stats_ready, b + 1, pool_waits)
                pool.tensor_scalar(rstd[:, :], mv[:, :, 1], 1e-5, None, ALU.add).then_inc(eps_added, 1)
                pool.wait_ge(eps_added, b + 1)
                pool.tensor_tensor(rstd[:, :], rstd[:, :], mhalf[:, 0:TPS], ALU.pow).then_inc(rstd_ready, 1)
                for n in range(2):
                    wait_apart(pool, ss_ready, 2 * b + n + 1, pool_waits)
                    pool.tensor_scalar(rn[n][:, :], ss[n][:, :], 1e-6, None, ALU.add).then_inc(ss_eps, 1)
                    pool.wait_ge(ss_eps, 2 * b + n + 1)
                    pool.tensor_tensor(rn[n][:, :], rn[n][:, :], mhalf[:, :], ALU.pow).then_inc(rn_ready, 1)

        @block.vector
        def _(dve):
            K = 11
            dve.wait_ge(loaded, 16 * 9)
            dve.wait_ge(consts, 6 + 2 * CPT)
            with dve.Fori(0, BATCH) as b:
                link = Chain(dve, own, b, K, waits=dve_waits)
                for t in range(TPS):
                    ins = dve.bn_stats(st[:, t, :], X[:, bass.ds(b * TPS + t, 1), :].rearrange("p a d -> p (a d)"))
                link.apart(ins)
                for t in range(TPS):
                    ins = dve.bn_aggr(mv[:, t, :], st[:, t, :])
                ins.then_inc(stats_ready, 1)
                dve.wait_ge(rstd_ready, b + 1)
                for t in range(TPS):
                    ins = dve.tensor_scalar(xn[:, t, :], X[:, bass.ds(b * TPS + t, 1), :].rearrange("p a d -> p (a d)"),
                                            mv[:, t, 0:1], rstd[:, t:t + 1], ALU.subtract, ALU.mult)
                ins.then_inc(xn_ready, 1)
                for n in range(3):
                    dve.wait_ge(tap_done, 3 * b + n + 1)
                    for j in range(TAPS - 1):
                        s = TAPS - 1 - j
                        ins = dve.scalar_tensor_tensor(conv[n][:, s:], A[:, 1 + n, 0:SEQ - s], taps[:, n, j:j + 1],
                                                       conv[n][:, s:], ALU.mult, ALU.add)
                        if j < TAPS - 2:
                            link(ins)
                    ins.then_inc(conv_ready, 1)
                for n in range(3):
                    dve.wait_ge(sig_ready, 3 * b + n + 1)
                    dve.tensor_tensor(act[n][:, :], conv[n][:, :], sig[n][:, :], ALU.mult).then_inc(act_ready, 1)
                dve.wait_ge(beta_ready, b + 1)
                dve.tensor_tensor(res["logits"][:, bass.ds(b * TPS, TPS), :], B[:, 0, 0:96].rearrange("p (t g) -> p t g", t=TPS)[:, :, 0:20],
                                  gate_b[:, :].unsqueeze(1).to_broadcast([P, TPS, 20]), ALU.add).then_inc(glog, 1)
                for n in range(2):
                    dve.wait_ge(sq_ready, 2 * b + n + 1)
                    dve.reduce_sum(ss[n][:, :], heads(sq[n][:, :, :]), axis=AX.X).then_inc(ss_ready, 1)
                dve.wait_ge(drained, b + 1)
                dve.wait_ge(tok_done, 3 * b + 3)
                dve.tensor_copy(flat(vt[:, :, :]), B[:, 3, :]).then_inc(own, 1)
                link.n += 1
                link(dve.tensor_tensor(heads(vb[:, :, :]), B[:, 3, :].rearrange("p (g d) -> p g d", d=DH), over(beta[:, :], DH), ALU.mult))
                for n, dst in enumerate((qt, kt)):
                    dve.wait_ge(rn_ready, 2 * b + n + 1)
                    ins = dve.tensor_tensor(heads(dst[:, :, :]), B[:, 1 + n, :].rearrange("p (g d) -> p g d", d=DH), over(rn[n][:, :], DH), ALU.mult)
                    if n == 0:
                        ins.then_inc(tok_ready, 1)
                    else:
                        link(ins)
                dve.tensor_tensor(heads(kb[:, :, :]), heads(kt[:, :, :]), over(beta[:, :], DH), ALU.mult).then_inc(tok_ready, 1)
                dve.wait_ge(gram_done, b + 1)
                gh = lambda lo: A[:, :, lo:lo + TPS * CH].rearrange("p h (t c) -> p h t c", t=TPS)
                lw = lower[:, :].unsqueeze(1).to_broadcast([P, H * TPS, CH])
                up = upper[:, :].unsqueeze(1).to_broadcast([P, TPS, CH])
                bt = beta[:, :].rearrange("p (t h) -> p h t", t=TPS).unsqueeze(3).to_broadcast([P, H, TPS, CH])
                link(dve.tensor_tensor(am[:, :, :, :], gh(0), bt, ALU.mult))
                amf = am[:, :, :, :].rearrange("p h t c -> p (h t) c")
                dve.scalar_tensor_tensor(amf, amf, -1.0, lw, ALU.mult, ALU.mult).then_inc(am_ready, 1)
                for h in range(H):
                    ins = dve.tensor_tensor(at[:, h, :, :], A[:, h, 128:256].rearrange("p (t c) -> p t c", t=TPS), up, ALU.mult)
                ins.then_inc(am_ready, 1)
                link.end()

        @block.scalar
        def _(act_e):
            act_e.wait_ge(loaded, 16 * 9)
            act_e.activation(res["inv_temp"][:, :], log_temp[:, :], ACT.Exp, scale=-1.0).then_inc(lt, 1)
            with act_e.Fori(0, BATCH) as b:
                act_e.wait_ge(xT_done, b + 1)
                act_e.activation(xnT[:, :], A[:, 0, :], ACT.Copy).then_inc(xnT_ready, 1)
                for n in range(3):
                    act_e.wait_ge(proj_done, 3 * b + n + 1)
                    act_e.activation(conv[n][:, :], A[:, 1 + n, :], ACT.Copy, scale=taps[:, n, TAPS - 1:TAPS]).then_inc(tap_done, 1)
                act_e.wait_ge(gates_done, b + 1)
                act_e.activation(beta[:, :].rearrange("p (t h) -> p t h", t=TPS), B[:, 0, 0:96].rearrange("p (t g) -> p t g", t=TPS)[:, :, 20:24],
                                 ACT.Sigmoid).then_inc(beta_ready, 1)
                for n in range(3):
                    act_e.wait_ge(conv_ready, 3 * b + n + 1)
                    act_e.activation(sig[n][:, :], conv[n][:, :], ACT.Sigmoid).then_inc(sig_ready, 1)
                for n in range(2):
                    act_e.wait_ge(tok_done, 3 * b + n + 1)
                    act_e.activation(flat(sq[n][:, :, :]), B[:, 1 + n, :], ACT.Square).then_inc(sq_ready, 1)
                for n, dst in enumerate((qT, kT)):
                    act_e.wait_ge(back_done, 2 * b + n + 1)
                    act_e.activation(dst[:, :], B[:, 1 + n, :], ACT.Copy).then_inc(back_ready, 1)

        @block.tensor
        def _(pe):
            pe.wait_ge(loaded, 16 * 9)
            pe.wait_ge(consts, 6 + 2 * CPT)
            with pe.Fori(0, BATCH) as b:
                pe.wait_ge(xn_ready, b + 1)
                for t in range(TPS):
                    ins = pe.transpose(A[:, 0, t * P:(t + 1) * P], xn[:, t, :], ident[:, :])
                ins.then_inc(xT_done, 1)
                pe.wait_ge(xnT_ready, b + 1)
                for n, wt in enumerate((wq, wk, wv)):
                    pe.matmul(A[:, 1 + n, :], wt[:, :], xnT[:, :], start=True, stop=True).then_inc(proj_done, 1)
                for t in range(TPS):
                    ins = pe.matmul(B[:, 0, t * 24:(t + 1) * 24], xnT[:, t * P:(t + 1) * P], wg[:, :], start=True, stop=True)
                ins.then_inc(gates_done, 1)
                for n in range(3):
                    pe.wait_ge(act_ready, 3 * b + n + 1)
                    for t in range(TPS):
                        ins = pe.transpose(B[:, 1 + n, t * P:(t + 1) * P], act[n][:, t * P:(t + 1) * P], ident[:, :])
                    ins.then_inc(tok_done, 1)
                for n, src in enumerate((qt, kt)):
                    pe.wait_ge(tok_ready, 2 * b + n + 1)
                    for t in range(TPS):
                        ins = pe.transpose(B[:, 1 + n, t * P:(t + 1) * P], src[:, t, :], ident[:, :])
                    ins.then_inc(back_done, 1)
                wait_apart(pe, back_ready, 2 * b + 2, pe_waits)
                for lo, right in ((0, kT), (P, qT)):
                    for t in range(TPS):
                        for c in range(CPT):
                            cols = slice(t * P + c * CH, t * P + (c + 1) * CH)
                            for h in range(H):
                                rows = slice(DH * h, DH * h + DH)
                                ins = pe.matmul(A[CH * c:CH * c + CH, h, lo + t * CH:lo + (t + 1) * CH],
                                                kT[rows, cols], right[rows, cols], start=True, stop=True)
                ins.then_inc(gram_done, 1)


def fir_and_inverses(nc, w, scr, res):
    with ExitStack() as ctx:
        sb, pb, sem = tensors(nc, ctx, "fi")
        NG = H * NGATE
        GC = 4
        F3 = len(FIRS)
        vwin = sb("vwin", [P, BATCH, NWIN, D])
        vst = [sb(f"vst{n}", [P, GC, P]) for n in range(2)]
        toep = [sb(f"toep{n}", [P, GC * F3, WIN]) for n in range(2)]
        tmp = [sb(f"tmp{n}", [P, 2, F3, WIN]) for n in range(2)]
        pw = sb("pw", [P, WIN, NG])
        pf = sb("pf", [P, H, F3, WIN])
        oc = sb("oc", [P, WIN, D])
        mx, sm = sb("mx", [P, NT * H]), sb("sm", [P, NT * H])
        gain = sb("gain", [P, H])
        GP = 2
        POOL_GROUPS = 3
        groups = BATCH // GP
        am = {e: sb(f"am_{e}", [P, CH, CH]) for e in ("pool", "dve")}
        um = {e: sb(f"um_{e}", [P, CH, CH]) for e in ("pool", "dve")}
        pr = {e: sb(f"pr_{e}", [P, CH * CH // 4 + CH]) for e in ("pool", "dve")}
        F = [pb(f"F{n}", [P, 2, 512]) for n in range(2)]
        win_in, own, pown, toep_in = sem("win_in"), sem("own"), sem("pown"), [sem("toep_in0"), sem("toep_in1")]
        down, fir_summed = sem("down"), sem("fir_summed")
        vst_ready, fir_done, fir_read, exps, prb, pw_out, pw_in, oc_out = (
            sem(n) for n in ("vst_ready", "fir_done", "fir_read", "exps", "prb", "pw_out", "pw_in", "oc_out"))
        mats_in = {e: sem(f"mats_in_{e}") for e in ("pool", "dve")}
        mats_out = {e: sem(f"mats_out_{e}") for e in ("pool", "dve")}
        solved = {e: sem(f"solved_{e}") for e in ("pool", "dve")}
        sub, pf_ready = sem("sub"), sem("pf_ready")
        pool_waits, dve_waits, pe_waits = sem("pool_waits"), sem("dve_waits"), sem("pe_waits")
        block = ctx.enter_context(nc.Block())
        L, PR, eps = res["logits"], res["probs"], res["eps"]
        L4 = L[:, :, :].rearrange("p t (h g) -> p (t h) g", h=H)
        P4 = PR[:, :, :].rearrange("p t (h g) -> p (t h) g", h=H)

        @block.sync
        def _(sp):
            for b in range(BATCH):
                sp.dma_start(vwin[:, b, :, :], bass.AP(tensor=scr["v"].tensor, offset=b * (SEQ + WIN) * D,
                                                       ap=[[D, P], [WIN * D, NWIN], [1, D]])).then_inc(win_in, 16)
            with sp.Fori(0, D // GC // 2) as i:
                for u in range(2):
                    sp.wait_ge(fir_done, 2 * i + u + 1)
                    rows = w["fir_pad"][bass.ds((2 * i + u) * (GC * F3), GC * F3), :]
                    src = bass.AP(tensor=rows.tensor, offset=rows.offset, ap=[[1, P], [PADW, GC * F3], [1, WIN]])
                    sp.dma_start(toep[u][:, :, :], src).then_inc(toep_in[u], 16)
            sp.wait_ge(fir_summed, D // GC)
            sp.dma_start(scr["ofir"].rearrange("b (j t) d -> (b j) t d", t=WIN), oc[:, :, :]).then_inc(oc_out, 16)
            sp.wait_ge(oc_out, 16)

        def matrices(eng, e, g):
            for b in range(GP):
                for c in range(CPT):
                    src = scr["A"][bass.ds(g * GP + b, 1), c * CH:(c + 1) * CH, :].rearrange("a i (x j) -> (a x) i j", j=CH)
                    p0 = b * 64 + c * 16
                    eng.dma_start(am[e][p0:p0 + 16, :, :], src).then_inc(mats_in[e], 16)

        def solve(eng, e, chain, turn, g):
            A_, U, R = am[e], um[e], pr[e]
            eng.sem_inc(pool_waits if e == "pool" else dve_waits, 1)
            chain.apart(eng.memset(U[:, :, :], 0.0))
            chain(eng.memset(U[:, :, :].rearrange("p a b -> p (a b)")[:, 0:CH * CH:CH + 1], 1.0))
            eng.wait_ge(mats_in[e], (turn + 1) * (16 * GP * CPT))
            for j in range(CH - 1):
                n, m = j + 1, CH - 1 - j
                prod = R[:, 0:n * m].rearrange("p (a b) -> p a b", a=n)
                chain(eng.tensor_tensor(prod, U[:, 0:n, j:j + 1].to_broadcast([P, n, m]),
                                        A_[:, j + 1:, j].unsqueeze(1).to_broadcast([P, n, m]), ALU.mult))
                ins = eng.tensor_tensor(U[:, 0:n, j + 1:], U[:, 0:n, j + 1:], prod, ALU.add)
                if j < CH - 2:
                    chain(ins)
            ins.then_inc(solved[e], 1)

        SOLVE = 2 + 2 * (CH - 1) - 1

        @block.gpsimd
        def _(pool):
            with pool.Fori(0, POOL_GROUPS) as g:
                matrices(pool, "pool", g)
                chain = Chain(pool, pown, g, SOLVE, waits=pool_waits)
                solve(pool, "pool", chain, g, g)
                chain.end()
                pool.wait_ge(solved["pool"], g + 1)
                pool.dma_start(scr["T"][bass.ds(g, 1), :, :].rearrange("a p n -> (a p) n"),
                               um["pool"][:, :, :].rearrange("p a b -> p (a b)")).then_inc(mats_out["pool"], 16)
                pool.wait_ge(mats_out["pool"], (g + 1) * 16)

        @block.vector
        def _(dve):
            SOFT = 8
            link = Chain(dve, own, 0, SOFT)
            temp = res["inv_temp"][:, :].unsqueeze(1).to_broadcast([P, NT, H])
            L_h = lambda g: L[:, :, :].rearrange("p t (h g) -> p t h g", h=H)[:, :, :, g]
            for g in range(NGATE):
                ins = dve.tensor_tensor(L_h(g), L_h(g), temp, ALU.mult)
            link(ins)
            link(dve.reduce_max(mx[:, :], L4, axis=AX.X))
            dve.tensor_tensor(L4, L4, over(mx[:, :], NGATE), ALU.subtract).then_inc(sub, 1)
            link(dve.tensor_scalar(eps[:, :], eps[:, :], 0.0, 0.2, ALU.max, ALU.min))
            link(dve.tensor_scalar(gain[:, :], eps[:, :], -5.0, 1.0, ALU.mult, ALU.add))
            dve.wait_ge(exps, 1)
            link(dve.reduce_sum(sm[:, :], P4, axis=AX.X))
            link(dve.reciprocal(sm[:, :], sm[:, :]))
            smh = sm[:, :].rearrange("p (t h) -> p t h", h=H)
            link(dve.tensor_tensor(smh, smh, gain[:, :].unsqueeze(1).to_broadcast([P, NT, H]), ALU.mult))
            link(dve.tensor_tensor(P4, P4, over(sm[:, :], NGATE), ALU.mult))
            ev = eps[:, :].unsqueeze(1).to_broadcast([P, NT, H])
            for g in range(NGATE):
                pg = PR[:, :, :].rearrange("p t (h g) -> p t h g", h=H)[:, :, :, g]
                ins = dve.tensor_tensor(pg, pg, ev, ALU.add)
            ins.then_inc(prb, 1)
            dve.wait_ge(pw_in, 16)
            for h in range(H):
                for f in range(F3):
                    ins = dve.tensor_copy(pf[:, h, f, :], pw[:, ::-1, h * NGATE + f])
            ins.then_inc(pf_ready, 1)
            dve.wait_ge(pf_ready, 1)
            for u in range(2):
                dve.sem_inc(fir_read, 1)
            with dve.Fori(0, H) as h:
                with dve.Fori(0, DH // GC // 2) as k:
                    for u in range(2):
                        grp = h * (DH // GC) + k * 2 + u
                        dve.wait_ge(fir_done, grp + 3)
                        wgt = pf[:, bass.ds(h, 1), :, :].rearrange("p a f t -> p (a f) t").unsqueeze(1).to_broadcast([P, 2, F3, WIN])
                        for c2 in range(2):
                            ins = dve.tensor_tensor(tmp[c2][:, :, :, :], F[u][:, c2, 0:2 * F3 * WIN].rearrange("p (c f t) -> p c f t", c=2, f=F3),
                                                    wgt, ALU.mult)
                        ins.then_inc(fir_read, 1)
                        dve.wait_ge(fir_read, grp + 3)
                        for c2 in range(2):
                            out = oc[:, :, bass.ds(grp * GC + 2 * c2, 2)].rearrange("p t c -> p c t")
                            ins = dve.reduce_sum(out, tmp[c2][:, :, :, ::-1].rearrange("p c f t -> p c t f"), axis=AX.X)
                        ins.then_inc(fir_summed, 1)
                        dve.wait_ge(fir_summed, grp + 1)
            with dve.Fori(0, groups - POOL_GROUPS) as g:
                chain = Chain(dve, down, g, SOLVE, waits=dve_waits)
                solve(dve, "dve", chain, g, g)
                chain.end()
                dve.wait_ge(mats_out["dve"], (g + 1) * 16)
            link.end()

        @block.scalar
        def _(act_e):
            act_e.wait_ge(sub, 1)
            act_e.activation(PR[:, :, :], L[:, :, :], ACT.Exp).then_inc(exps, 1)
            act_e.wait_ge(prb, 1)
            act_e.dma_start(scr["probs"].rearrange("(t p) g -> p t g", p=P), PR[:, :, :]).then_inc(pw_out, 16)
            act_e.wait_ge(pw_out, 16)
            act_e.dma_start(pw[:, :, :], scr["probs"].rearrange("(w t) g -> w t g", t=WIN)).then_inc(pw_in, 16)
            act_e.wait_ge(win_in, 16 * BATCH)
            vw = vwin[:, :, :, :].rearrange("p b j d -> p (b j) d")
            with act_e.Fori(0, D // GC // 2) as i:
                for u in range(2):
                    act_e.wait_ge(fir_done, 2 * i + u + 1)
                    act_e.activation(vst[u][:, :, :], vw[:, :, bass.ds((2 * i + u) * GC, GC)].rearrange("p w c -> p c w"), ACT.Copy)\
                         .then_inc(vst_ready, 1)
            with act_e.Fori(0, groups - POOL_GROUPS) as g:
                matrices(act_e, "dve", g + POOL_GROUPS)
                act_e.wait_ge(solved["dve"], g + 1)
                act_e.dma_start(scr["T"][bass.ds(g + POOL_GROUPS, 1), :, :].rearrange("a p n -> (a p) n"),
                                um["dve"][:, :, :].rearrange("p a b -> p (a b)")).then_inc(mats_out["dve"], 16)
                act_e.wait_ge(mats_out["dve"], (g + 1) * 16)

        @block.tensor
        def _(pe):
            for u in range(2):
                pe.sem_inc(fir_done, 1)
            with pe.Fori(0, D // GC // 2) as i:
                for u in range(2):
                    pe.wait_ge(vst_ready, 2 * i + u + 1)
                    pe.wait_ge(toep_in[u], 16 * (i + 1))
                    pe.wait_ge(fir_read, 2 * i + u + 1)
                    for c in range(GC):
                        ins = pe.matmul(F[u][:, c // 2, (c % 2) * F3 * WIN:(c % 2 + 1) * F3 * WIN], vst[u][:, c, :],
                                        toep[u][:, c * F3:(c + 1) * F3, :], start=True, stop=True)
                    ins.then_inc(fir_done, 1)


def delta_rule(nc, scr, res):
    with ExitStack() as ctx:
        sb, pb, sem = tensors(nc, ctx, "dr")
        GB = 4
        X2 = TPS * H
        tT = [sb(f"tT{b}", [P, X2, P]) for b in range(GB)]
        aT = [sb(f"aT{b}", [P, X2, P]) for b in range(GB)]
        kk, kb, vb = ([sb(f"{n}{b}", [P, TPS, D]) for b in range(GB)] for n in ("kk", "kb", "vb"))
        qT = [sb(f"qT{b}", [D, SEQ]) for b in range(GB)]
        us = sb("us", [P, GB, TPS, D])
        wT = [sb(f"wT{b}", [D, SEQ]) for b in range(GB)]
        S = sb("S", [D, GB, D])
        diag = sb("diag", [D, D])
        PAIRS, PB = 2, GB // 2
        W, SP_ = ([pb(f"{n}{k}", [P, 512]) for k in range(PAIRS)] for n in ("W", "SP"))
        O = [pb(f"O{b}", [P, TPS, D]) for b in range(GB)]
        consts, loads, zeroed, u_done, u_ready, state_zero = (sem(n) for n in ("consts", "loads", "zeroed", "u_done", "u_ready", "state_zero"))
        ws_done, ua_ready, s_done, s_ready, o_done, o_ready, stored, turn_done = (
            sem(n) for n in ("ws_done", "ua_ready", "s_done", "s_ready", "o_done", "o_ready", "stored", "turn_done"))
        block = ctx.enter_context(nc.Block())
        LOADS = (4 + 2 * CPT) * GB
        NS = CPS * PAIRS

        @block.sync
        def _(sp):
            sp.wait_ge(zeroed, 2 * GB)
            with sp.Fori(0, BATCH // GB) as g:
                for b in range(GB):
                    bb = bass.ds(g * GB + b, 1)
                    one = lambda name: scr[name][bb, :, :].rearrange("a p n -> (a p) n")
                    for c in range(CPT):
                        r = slice(c * CH, (c + 1) * CH)
                        tsrc = scr["T"][bass.ds(g * (GB // 2) + b // 2, 1), (b % 2) * 64 + c * 16:(b % 2) * 64 + c * 16 + 16, :]
                        sp.dma_start(tT[b][r, :, r], tsrc.rearrange("a x (j i) -> j (a x) i", i=CH)).then_inc(loads, 16)
                        sp.dma_start(aT[b][r, :, r], scr["attnT"][bb, r, :].rearrange("a j (x i) -> (a j) x i", i=CH)).then_inc(loads, 16)
                    for name, dst in (("k", kk), ("kb", kb), ("vb", vb)):
                        sp.dma_start(flat(dst[b][:, :, :]), one(name)).then_inc(loads, 16)
                    sp.dma_start(qT[b][:, :], one("qT")).then_inc(loads, 16)
                for b in range(GB):
                    sp.wait_ge(o_ready, g * GB + b + 1)
                    sp.dma_start(scr["o"][bass.ds(g * GB + b, 1), :, :].rearrange("a p n -> (a p) n"), flat(us[:, b, :, :])).then_inc(stored, 16)
                sp.wait_ge(stored, (g + 1) * (16 * GB))
                sp.sem_inc(turn_done, 1)

        @block.gpsimd
        def _(pool):
            const, clear = Chain(pool, consts), Chain(pool, zeroed)
            for b in range(GB):
                clear(pool.memset(tT[b][:, :, :], 0.0))
                clear(pool.memset(aT[b][:, :, :], 0.0))
            const(pool.memset(diag[:, :], 0.0))
            for h in range(H):
                r = slice(h * DH, (h + 1) * DH)
                const(pool.memset(diag[r, r], 1.0))

        @block.tensor
        def _(pe):
            pe.sem_inc(turn_done, 1)
            with pe.Fori(0, BATCH // GB) as g:
                pe.wait_ge(loads, (g + 1) * (16 * LOADS))
                pe.wait_ge(turn_done, g + 1)
                for b in range(GB):
                    if b >= 2:
                        pe.wait_ge(u_ready, 2 * GB * g + 2 * b - 3)
                    for h in range(H):
                        for t in range(TPS):
                            ins = pe.matmul(O[2 * (b % 2)][:, t, h * DH:(h + 1) * DH], tT[b][:, h * TPS + t, :], vb[b][:, t, h * DH:(h + 1) * DH],
                                            start=True, stop=True)
                    ins.then_inc(u_done, 1)
                    if b >= 2:
                        pe.wait_ge(u_ready, 2 * GB * g + 2 * b - 2)
                    for h in range(H):
                        for t in range(TPS):
                            ins = pe.matmul(O[2 * (b % 2) + 1][h * DH:(h + 1) * DH, t, :], kb[b][:, t, h * DH:(h + 1) * DH], tT[b][:, h * TPS + t, :],
                                            start=True, stop=True)
                    ins.then_inc(u_done, 1)
                pe.wait_ge(u_ready, 2 * GB * (g + 1))
                pe.wait_ge(state_zero, g + 1)
                for n in range(CPS):
                    t, c = n // CPT, n % CPT
                    r = slice(c * CH, (c + 1) * CH)
                    cols = slice(n * CH, (n + 1) * CH)
                    for k in range(PAIRS):
                        if n:
                            pe.wait_ge(s_ready, g * NS + (n - 1) * PAIRS + k + 1)
                        for b in range(PB * k, PB * (k + 1)):
                            ins = pe.matmul(W[k][r, (b % PB) * D:(b % PB + 1) * D], wT[b][:, cols], S[:, b, :], start=True, stop=True)
                        ins.then_inc(ws_done, 1)
                    for b in range(GB):
                        pe.matmul(O[b][r, t, :], qT[b][:, cols], S[:, b, :], start=(t == 0), stop=False, skip_group_check=True)
                    for k in range(PAIRS):
                        pe.wait_ge(ua_ready, g * NS + n * PAIRS + k + 1)
                        for b in range(PB * k, PB * (k + 1)):
                            ins = pe.matmul(SP_[k][:, (b % PB) * D:(b % PB + 1) * D], kk[b][r, t, :], us[r, b, t, :], start=(n == 0 and b % PB == 0),
                                            stop=False, skip_group_check=True)
                        ins.then_inc(s_done, 1)
                    if c == CPT - 1:
                        for b in range(GB):
                            for h in range(H):
                                ins = pe.matmul(O[b][:, t, h * DH:(h + 1) * DH], aT[b][:, h * TPS + t, :], us[:, b, t, h * DH:(h + 1) * DH],
                                                start=False, stop=True, skip_group_check=True)
                            if t == TPS - 1:
                                ins.then_inc(o_done, 1)

        @block.vector
        def _(dve):
            dve.wait_ge(consts, 1 + H)
            with dve.Fori(0, BATCH // GB) as g:
                dve.memset(S[:, :, :], 0.0).then_inc(state_zero, 1)
                for n in range(CPS):
                    t, c = n // CPT, n % CPT
                    r = slice(c * CH, (c + 1) * CH)
                    two = lambda ap: ap.rearrange("p (b d) -> p b d", b=PB)
                    for k in range(PAIRS):
                        u = us[r, PB * k:PB * (k + 1), t, :]
                        dve.wait_ge(ws_done, g * NS + n * PAIRS + k + 1)
                        dve.tensor_tensor(u, u, two(W[k][r, 0:PB * D]), ALU.subtract).then_inc(ua_ready, 1)
                    for k in range(PAIRS):
                        dve.wait_ge(s_done, g * NS + n * PAIRS + k + 1)
                        dve.tensor_tensor(S[:, PB * k:PB * (k + 1), :], two(SP_[k][:, 0:PB * D]), diag[:, :].unsqueeze(1).to_broadcast([D, PB, D]),
                                          ALU.mult).then_inc(s_ready, 1)
                dve.wait_ge(s_ready, (g + 1) * NS)

        @block.scalar
        def _(act_e):
            with act_e.Fori(0, BATCH // GB) as g:
                act_e.wait_ge(turn_done, g + 1)
                for b in range(GB):
                    for n, (src, dst) in enumerate(((O[2 * (b % 2)], flat(us[:, b, :, :])), (O[2 * (b % 2) + 1], wT[b][:, :]))):
                        act_e.wait_ge(u_done, 2 * (GB * g + b) + n + 1)
                        act_e.activation(dst, src[:, :, :].rearrange("p t d -> p (t d)"), ACT.Copy).then_inc(u_ready, 1)
                for b in range(GB):
                    act_e.wait_ge(o_done, g * GB + b + 1)
                    act_e.activation(flat(us[:, b, :, :]), O[b][:, :, :].rearrange("p t d -> p (t d)"), ACT.Copy).then_inc(o_ready, 1)


def attention_output(nc, w, scr, res):
    with ExitStack() as ctx:
        sb, pb, sem = tensors(nc, ctx, "ao")
        wo, mix, rw = sb("wo", [D, D]), sb("mix", [D, D]), sb("rw", [D, NE])
        cols = sb("cols", [D, 5])
        mix_b = sb("mix_b", [P, D])
        mhalf = sb("mhalf", [P, TPS * H])
        of, dl, vt = ([sb(f"{n}{u}", [P, TPS, D]) for u in range(2)] for n in ("of", "dl", "vt"))
        o, t1, h0, c1 = (sb(n, [P, TPS, D]) for n in ("o", "t1", "h0", "c1"))
        ss, rs = sb("ss", [P, TPS * H]), sb("rs", [P, TPS * H])
        st, mv, rstd = sb("st", [P, TPS, 6]), sb("mv", [P, TPS, 2]), sb("rstd", [P, TPS])
        xT = sb("xT", [D, SEQ])
        tp, pr, rp = pb("tp", [P, SEQ]), pb("pr", [P, SEQ]), pb("rp", [P, TPS * NE])
        consts, loaded, wo_ready, mix_ready, stored = (sem(n) for n in ("consts", "loaded", "wo_ready", "mix_ready", "stored"))
        paths_in = [sem("paths_in0"), sem("paths_in1")]
        paths_used, own, sums_ready, eps_added, r_ready, rows_ready, tp_done, xT_ready, pr_done, rp_done = (
            sem(n) for n in ("paths_used", "own", "sums_ready", "eps_added", "r_ready", "rows_ready", "tp_done", "xT_ready", "pr_done", "rp_done"))
        pool_waits, dve_waits, pe_waits = sem("pool_waits"), sem("dve_waits"), sem("pe_waits")
        block = ctx.enter_context(nc.Block())
        X, PR, ident = res["x"], res["probs"], res["ident"]
        CONST = 16 * 5

        @block.sync
        def _(sp):
            for dst, name in ((wo, "woT"), (mix, "mix_w"), (rw, "router_w"), (cols, "ao_cols")):
                sp.dma_start(dst[:, :], w[name]).then_inc(loaded, 16)
            sp.dma_start(mix_b[:, :], w["mix_b"].partition_broadcast(P)).then_inc(loaded, 16)
            with sp.Fori(0, BATCH // 2) as i:
                for u in range(2):
                    b = 2 * i + u
                    sp.wait_ge(paths_used, b + 1)
                    bb = bass.ds(b, 1)
                    sp.dma_start(of[u][:, :, :], scr["ofir"][bb, :, :].rearrange("a (t p) d -> p (a t) d", p=P)).then_inc(paths_in[u], 16)
                    sp.dma_start(flat(dl[u][:, :, :]), scr["o"][bb, :, :].rearrange("a p n -> (a p) n")).then_inc(paths_in[u], 16)
                    sp.dma_start(vt[u][:, :, :], scr["v"][bb, WIN:WIN + SEQ, :].rearrange("a (t p) d -> p (a t) d", p=P)).then_inc(paths_in[u], 16)

        @block.gpsimd
        def _(pool):
            pool.memset(mhalf[:, :], -0.5).then_inc(consts, 1)
            pool.wait_ge(consts, 1)
            with pool.Fori(0, BATCH) as b:
                for n, (src, m, scale, eps) in enumerate(((ss[:, :], 16, 1.0 / DH, 1e-5),) + ((mv[:, :, 1], TPS, 1.0, 1e-5),) * 4):
                    dst = rs[:, :] if n == 0 else rstd[:, :]
                    wait_apart(pool, sums_ready, 5 * b + n + 1, pool_waits)
                    pool.tensor_scalar(dst, src, scale, eps, ALU.mult, ALU.add).then_inc(eps_added, 1)
                    pool.wait_ge(eps_added, 5 * b + n + 1)
                    pool.tensor_tensor(dst, dst, mhalf[:, 0:m], ALU.pow).then_inc(r_ready, 1)

        @block.vector
        def _(dve):
            dve.wait_ge(loaded, CONST)
            dve.tensor_scalar(wo[:, :], wo[:, :], cols[:, 0:1], None, ALU.mult).then_inc(wo_ready, 1)
            dve.tensor_tensor(mix[:, :], mix[:, :], ident[:, :], ALU.add).then_inc(mix_ready, 1)
            for u in range(2):
                dve.sem_inc(paths_used, 1)
            K = 13
            with dve.Fori(0, BATCH // 2) as i:
                for u in range(2):
                    b = 2 * i + u
                    link = Chain(dve, own, b, K, waits=dve_waits)
                    xs = X[:, bass.ds(b * TPS, TPS), :]

                    def rows(src, dst, n):
                        row_stats(dve, link, src, st, mv).then_inc(sums_ready, 1)
                        dve.wait_ge(r_ready, 5 * b + n + 1)
                        for t in range(TPS):
                            ins = dve.tensor_scalar(dst[:, t, :], src[:, t, :], mv[:, t, 0:1], rstd[:, t:t + 1], ALU.subtract, ALU.mult)
                        return ins

                    gate = PR[:, bass.ds(b * TPS, TPS), :].rearrange("p t (h g) -> p t h g", h=H)
                    dve.wait_ge(paths_in[u], 48 * (i + 1))
                    for t in range(TPS):
                        g4 = lambda k: gate[:, t, :, k].unsqueeze(2).to_broadcast([P, H, DH])
                        hd = lambda a: a[:, t, :].rearrange("p (h d) -> p h d", h=H)
                        dve.tensor_tensor(hd(t1), hd(dl[u]), g4(3), ALU.mult)
                        ins = dve.tensor_tensor(hd(o), hd(vt[u]), g4(4), ALU.mult)
                    link(ins)
                    link(dve.tensor_tensor(t1[:, :, :], t1[:, :, :], of[u][:, :, :], ALU.add))
                    dve.tensor_tensor(o[:, :, :], o[:, :, :], t1[:, :, :], ALU.add).then_inc(paths_used, 1)
                    dve.wait_ge(paths_used, b + 3)
                    link(dve.tensor_tensor(t1[:, :, :], o[:, :, :], o[:, :, :], ALU.mult))
                    dve.reduce_sum(ss[:, :], heads(t1[:, :, :]), axis=AX.X).then_inc(sums_ready, 1)
                    dve.wait_ge(r_ready, 5 * b + 1)
                    dve.tensor_tensor(heads(o[:, :, :]), heads(o[:, :, :]), over(rs[:, :], DH), ALU.mult).then_inc(rows_ready, 1)
                    dve.wait_ge(rows_ready, 3 * b + 1)
                    dve.wait_ge(pr_done, 2 * b + 1)
                    link(rows(pr[:, :].rearrange("p (t d) -> p t d", t=TPS), t1, 1))
                    link.apart(dve.tensor_tensor(xs, xs, t1[:, :, :], ALU.add))
                    xr = [X[:, bass.ds(b * TPS + t, 1), :].rearrange("p a d -> p (a d)") for t in range(TPS)]
                    for t in range(TPS):
                        ins = dve.bn_stats(st[:, t, :], xr[t])
                    link.apart(ins)
                    for t in range(TPS):
                        ins = dve.bn_aggr(mv[:, t, :], st[:, t, :])
                    ins.then_inc(sums_ready, 1)
                    dve.wait_ge(r_ready, 5 * b + 3)
                    for t in range(TPS):
                        ins = dve.tensor_scalar(h0[:, t, :], xr[t], mv[:, t, 0:1], rstd[:, t:t + 1], ALU.subtract, ALU.mult)
                    link(ins)
                    rows(h0, c1, 3).then_inc(rows_ready, 1)
                    dve.wait_ge(rows_ready, 3 * b + 2)
                    link(dve.tensor_tensor(h0[:, :, :], h0[:, :, :], mix_b[:, :].unsqueeze(1).to_broadcast([P, TPS, D]), ALU.add))
                    dve.wait_ge(pr_done, 2 * b + 2)
                    x2 = res["x2"][:, bass.ds(b * TPS, TPS), :]
                    link(dve.tensor_tensor(h0[:, :, :], h0[:, :, :], pr[:, :].rearrange("p (t d) -> p t d", t=TPS), ALU.add))
                    dve.tensor_copy(x2, h0[:, :, :])
                    rows(h0, c1, 4).then_inc(rows_ready, 1)
                    dve.wait_ge(rows_ready, 3 * b + 3)
                    dve.wait_ge(rp_done, b + 1)
                    link(dve.tensor_copy(res["router"][:, bass.ds(b * TPS, TPS), :], rp[:, :].rearrange("p (t e) -> p t e", e=NE)))
                    link.end()

        @block.scalar
        def _(act_e):
            act_e.wait_ge(loaded, CONST)
            with act_e.Fori(0, BATCH) as b:
                act_e.wait_ge(tp_done, 3 * b + 1)
                act_e.activation(xT[:, :], tp[:, :], ACT.Copy).then_inc(xT_ready, 1)
                act_e.wait_ge(tp_done, 3 * b + 2)
                act_e.activation(xT[:, :], tp[:, :], ACT.Identity, bias=cols[:, 2:3], scale=cols[:, 1:2]).then_inc(xT_ready, 1)
                act_e.wait_ge(tp_done, 3 * b + 3)
                act_e.activation(res["n2T"][:, bass.ds(b, 1), :].rearrange("p a n -> p (a n)"), tp[:, :], ACT.Identity, bias=cols[:, 4:5], scale=cols[:, 3:4])
                act_e.activation(xT[:, :], tp[:, :], ACT.Identity, bias=cols[:, 4:5], scale=cols[:, 3:4]).then_inc(xT_ready, 1)

        @block.tensor
        def _(pe):
            pe.wait_ge(loaded, CONST)
            pe.wait_ge(wo_ready, 1)
            pe.wait_ge(mix_ready, 1)
            with pe.Fori(0, BATCH) as b:
                for n, (src, rhs, dst, done) in enumerate(((o, wo, pr, pr_done), (c1, mix, pr, pr_done), (c1, rw, rp, rp_done))):
                    pe.wait_ge(rows_ready, 3 * b + n + 1)
                    for t in range(TPS):
                        ins = pe.transpose(tp[:, t * P:(t + 1) * P], src[:, t, :], ident[:, :])
                    ins.then_inc(tp_done, 1)
                    pe.wait_ge(xT_ready, 3 * b + n + 1)
                    m = NE if n == 2 else D
                    for t in range(TPS):
                        ins = pe.matmul(dst[:, t * m:(t + 1) * m], xT[:, t * P:(t + 1) * P], rhs[:, :], start=True, stop=True)
                    ins.then_inc(done, 1)


def experts(nc, w, scr, res):
    with ExitStack() as ctx:
        sb, pb, sem = tensors(nc, ctx, "ex")
        w1 = sb("w1", [D, NE, FF])
        w2 = sb("w2", [P, NE, FC, D])
        b1 = sb("b1", [P, NE * FC])
        b2 = sb("b2", [NE, D])
        R, E = res["router"], sb("E", [P, NT, NE])
        M1, M2 = sb("M1", [P, NT, NE]), sb("M2", [P, NT, NE])
        m1, m2, sm = sb("m1", [P, NT]), sb("m2", [P, NT]), sb("sm", [P, NT])
        i1 = sb("i1", [P, NT])
        iot, ioti = sb("iot", [P, NE]), sb("ioti", [P, NE], mybir.dt.int32)
        hT = [sb(f"hT{u}", [P, FC, SEQ]) for u in range(2)]
        y = sb("y", [P, TPS, D])
        cT = sb("cT", [NE, SEQ])
        mhalf = sb("mhalf", [P, TPS])
        st, mv, rstd = sb("st", [P, TPS, 6]), sb("mv", [P, TPS, 2]), sb("rstd", [P, TPS])
        h_ps = [pb(f"h{u}", [P, SEQ]) for u in range(4)]
        y_ps = [pb(f"y{u}", [P, TPS, D]) for u in range(2)]
        c_ps, b_ps = pb("c", [P, SEQ]), pb("b", [P, TPS, D])
        loaded, consts, own, own2, sub, exps, comb, ct_done, ct_ready, bias_done, h_done, h_ready, y_done, y_read, stats, eps_added, r_ready, out_ready = (
            sem(n) for n in ("loaded", "consts", "own", "own2", "sub", "exps", "comb", "ct_done", "ct_ready", "bias_done", "h_done", "h_ready", "y_done",
                             "y_read", "stats", "eps_added", "r_ready", "out_ready"))
        ec, ec_ready, bias_read = sb("ec", [P, TPS, NE]), sem("ec_ready"), sem("bias_read")
        pool_waits, dve_waits, pe_waits = sem("pool_waits"), sem("dve_waits"), sem("pe_waits")
        block = ctx.enter_context(nc.Block())
        X, ident = res["x"], res["ident"]

        @block.sync
        def _(sp):
            sp.dma_start(w1[:, :, :], w["w1"].rearrange("e d f -> d e f")).then_inc(loaded, 16)
            sp.dma_start(w2[:, :, :, :], w["w2"].rearrange("e (c f) d -> f e c d", f=P)).then_inc(loaded, 16)
            sp.dma_start(b1[:, :], w["b1"]).then_inc(loaded, 16)
            sp.dma_start(b2[:, :], w["b2"]).then_inc(loaded, 16)

        @block.gpsimd
        def _(pool):
            pool.memset(mhalf[:, :], -0.5).then_inc(consts, 1)
            pool.wait_ge(consts, 1)
            pool.iota(ioti[:, :], pattern=[[1, NE]], base=0, channel_multiplier=0).then_inc(consts, 1)
            pool.wait_ge(consts, 2)
            with pool.Fori(0, BATCH) as b:
                wait_apart(pool, stats, b + 1, pool_waits)
                pool.tensor_scalar(rstd[:, :], mv[:, :, 1], 1e-5, None, ALU.add).then_inc(eps_added, 1)
                pool.wait_ge(eps_added, b + 1)
                pool.tensor_tensor(rstd[:, :], rstd[:, :], mhalf[:, :], ALU.pow).then_inc(r_ready, 1)

        @block.vector
        def _(dve):
            dve.wait_ge(consts, 2)
            link = Chain(dve, own, 0, 17)
            ov = lambda a: over(a[:, :], NE)
            it = iot[:, :].unsqueeze(1).to_broadcast([P, NT, NE])
            link(dve.tensor_copy(iot[:, :], ioti[:, :]))
            link(dve.reduce_max(m1[:, :], R[:, :, :], axis=AX.X))
            dve.tensor_tensor(E[:, :, :], R[:, :, :], ov(m1), ALU.subtract).then_inc(sub, 1)
            dve.wait_ge(exps, 1)
            link(dve.reduce_sum(sm[:, :], E[:, :, :], axis=AX.X))
            link(dve.reciprocal(sm[:, :], sm[:, :]))
            link(dve.tensor_tensor(E[:, :, :], E[:, :, :], ov(sm), ALU.mult))

            def first_of(vals, best, mask):
                link(dve.reduce_max(best[:, :], vals[:, :, :], axis=AX.X))
                link(dve.tensor_tensor(mask[:, :, :], vals[:, :, :], ov(best), ALU.is_lt))
                link(dve.scalar_tensor_tensor(mask[:, :, :], mask[:, :, :], float(NE), it, ALU.mult, ALU.add))
                link(dve.tensor_reduce(i1[:, :], mask[:, :, :], axis=AX.X, op=ALU.min))
                link(dve.tensor_tensor(mask[:, :, :], it, ov(i1), ALU.is_equal))

            first_of(E, m1, M1)
            link(dve.scalar_tensor_tensor(R[:, :, :], M1[:, :, :], -2.0, E[:, :, :], ALU.mult, ALU.add))
            first_of(R, m2, M2)
            link(dve.tensor_tensor(M1[:, :, :], M1[:, :, :], M2[:, :, :], ALU.add))
            dve.tensor_tensor(E[:, :, :], E[:, :, :], M1[:, :, :], ALU.mult).then_inc(comb, 1)
            dve.wait_ge(comb, 1)
            link.end()
            for u in range(2):
                dve.sem_inc(y_read, 1)
            dve.sem_inc(bias_read, 1)
            K = 3
            with dve.Fori(0, BATCH) as b:
                link = Chain(dve, own2, b, K, waits=dve_waits)
                dve.tensor_copy(ec[:, :, :], E[:, bass.ds(b * TPS, TPS), :]).then_inc(ec_ready, 1)
                dve.wait_ge(ec_ready, b + 1)
                x2 = res["x2"][:, bass.ds(b * TPS, TPS), :]
                dve.wait_ge(bias_done, b + 1)
                dve.tensor_tensor(y[:, :, :], x2, b_ps[:, :, :], ALU.add).then_inc(bias_read, 1)
                dve.wait_ge(bias_read, b + 2)
                for e in range(NE):
                    dve.wait_ge(y_done, NE * b + e + 3)
                    for t in range(TPS):
                        ins = dve.scalar_tensor_tensor(y[:, t, :], y_ps[e % 2][:, t, :], ec[:, t, e:e + 1], y[:, t, :], ALU.mult, ALU.add)
                    ins.then_inc(y_read, 1)
                    dve.wait_ge(y_read, NE * b + e + 3)
                row_stats(dve, link, y, st, mv).then_inc(stats, 1)
                dve.wait_ge(r_ready, b + 1)
                for t in range(TPS):
                    ins = dve.tensor_scalar(y[:, t, :], y[:, t, :], mv[:, t, 0:1], rstd[:, t:t + 1], ALU.subtract, ALU.mult)
                link(ins)
                xs = X[:, bass.ds(b * TPS, TPS), :]
                link(dve.tensor_tensor(xs, xs, y[:, :, :], ALU.add))
                link.end()

        @block.scalar
        def _(act_e):
            act_e.wait_ge(sub, 1)
            act_e.activation(E[:, :, :], E[:, :, :], ACT.Exp).then_inc(exps, 1)
            act_e.wait_ge(loaded, 64)
            for f in range(FC):
                act_e.sem_inc(h_ready, 1)
            with act_e.Fori(0, BATCH) as b:
                act_e.wait_ge(ct_done, b + 1)
                act_e.activation(cT[:, :], c_ps[0:NE, :], ACT.Copy).then_inc(ct_ready, 1)
                for e in range(NE):
                    for f in range(FC):
                        act_e.wait_ge(h_done, (b * NE + e) * FC + f + 1)
                        if f == 0:
                            act_e.wait_ge(y_done, b * NE + e + 1)
                        act_e.activation(hT[e % 2][:, f, :], h_ps[f][:, :], ACT.Silu, bias=b1[:, e * FC + f:e * FC + f + 1]).then_inc(h_ready, 1)

        @block.tensor
        def _(pe):
            pe.wait_ge(loaded, 64)
            pe.wait_ge(comb, 1)
            for u in range(2):
                pe.sem_inc(y_done, 1)
            with pe.Fori(0, BATCH) as b:
                nT = res["n2T"][:, bass.ds(b, 1), :].rearrange("p a n -> p (a n)")

                def up(e):
                    for f in range(FC):
                        pe.wait_ge(h_ready, (b * NE + e) * FC + f + 1)
                        pe.matmul(h_ps[f][:, :], w1[:, e, f * P:(f + 1) * P], nT, start=True, stop=True).then_inc(h_done, 1)

                def down(e):
                    pe.wait_ge(h_ready, (b * NE + e) * FC + 2 * FC)
                    pe.wait_ge(y_read, b * NE + e + 1)
                    for t in range(TPS):
                        for f in range(FC):
                            ins = pe.matmul(y_ps[e % 2][:, t, :], hT[e % 2][:, f, t * P:(t + 1) * P], w2[:, e, f, :], start=(f == 0), stop=(f == FC - 1))
                    ins.then_inc(y_done, 1)

                pe.wait_ge(ec_ready, b + 1)
                for t in range(TPS):
                    ins = pe.transpose(c_ps[0:NE, t * P:(t + 1) * P], ec[:, t, :], ident[:, :])
                ins.then_inc(ct_done, 1)
                up(0)
                pe.wait_ge(ct_ready, b + 1)
                pe.wait_ge(bias_read, b + 1)
                for t in range(TPS):
                    ins = pe.matmul(b_ps[:, t, :], cT[:, t * P:(t + 1) * P], b2[:, :], start=True, stop=True)
                ins.then_inc(bias_done, 1)
                for e in range(NE):
                    if e + 1 < NE:
                        up(e + 1)
                    down(e)


def gate_loop(nc, w, res):
    with ExitStack() as ctx:
        sb, pb, sem = tensors(nc, ctx, "gl")
        names = ("wq", "wk", "wv", "wa", "wg", "wo")
        W = {n: sb(n, [D, D]) for n in names}
        gamma = sb("gamma", [D, 1])
        mhalf = sb("mhalf", [P, TPS])
        st, mv, rstd, ss = sb("st", [P, TPS, 6]), sb("mv", [P, TPS, 2]), sb("rstd", [P, TPS]), sb("ss", [P, TPS])
        h, sq = sb("h", [P, TPS, D]), sb("sq", [P, TPS, D])
        xT, k, a, sg, q, y = (sb(n, [D, SEQ]) for n in ("xT", "k", "a", "sg", "q", "y"))
        o = sb("o", [P, TPS, D])
        tp, op = pb("tp", [P, SEQ]), pb("op", [P, TPS, D])
        pq, pk, pv, pa, pg = (pb(n, [D, SEQ]) for n in ("pq", "pk", "pv", "pa", "pg"))
        loaded, consts, own, stats, eps_added, r_ready, h_ready, tp_done, xT_ready, proj_done, k_ready, a_ready, sg_ready, y_ready, o_done, g_ready = (
            sem(n) for n in ("loaded", "consts", "own", "stats", "eps_added", "r_ready", "h_ready", "tp_done", "xT_ready", "proj_done", "k_ready",
                             "a_ready", "sg_ready", "y_ready", "o_done", "g_ready"))
        pool_waits, dve_waits, pe_waits = sem("pool_waits"), sem("dve_waits"), sem("pe_waits")
        block = ctx.enter_context(nc.Block())
        X, ident = res["x"], res["ident"]

        @block.sync
        def _(sp):
            for n in names:
                sp.dma_start(W[n][:, :], w[f"gl_{n}"]).then_inc(loaded, 16)
            sp.dma_start(gamma[:, :], w["gamma"]).then_inc(loaded, 16)

        @block.gpsimd
        def _(pool):
            pool.memset(mhalf[:, :], -0.5).then_inc(consts, 1)
            pool.wait_ge(consts, 1)
            with pool.Fori(0, BATCH) as b:
                for n, src in enumerate((mv[:, :, 1], ss[:, :], mv[:, :, 1])):
                    wait_apart(pool, stats, 3 * b + n + 1, pool_waits)
                    pool.tensor_scalar(rstd[:, :], src, 1e-5, None, ALU.add).then_inc(eps_added, 1)
                    pool.wait_ge(eps_added, 3 * b + n + 1)
                    pool.tensor_tensor(rstd[:, :], rstd[:, :], mhalf[:, :], ALU.pow).then_inc(r_ready, 1)

        @block.vector
        def _(dve):
            dve.wait_ge(loaded, 16 * 7)
            dve.tensor_scalar(gamma[:, :], gamma[:, :], float(D) ** 0.5, None, ALU.mult).then_inc(g_ready, 1)
            K = 10
            with dve.Fori(0, BATCH) as b:
                link = Chain(dve, own, b, K, waits=dve_waits)
                xr = [X[:, bass.ds(b * TPS + t, 1), :].rearrange("p a d -> p (a d)") for t in range(TPS)]
                for t in range(TPS):
                    ins = dve.bn_stats(st[:, t, :], xr[t])
                link.apart(ins)
                for t in range(TPS):
                    ins = dve.bn_aggr(mv[:, t, :], st[:, t, :])
                ins.then_inc(stats, 1)
                dve.wait_ge(r_ready, 3 * b + 1)
                for t in range(TPS):
                    ins = dve.tensor_scalar(h[:, t, :], xr[t], mv[:, t, 0:1], rstd[:, t:t + 1], ALU.subtract, ALU.mult)
                link(ins)
                link(dve.tensor_tensor(sq[:, :, :], h[:, :, :], h[:, :, :], ALU.mult))
                dve.reduce_sum(ss[:, :], sq[:, :, :], axis=AX.X).then_inc(stats, 1)
                dve.wait_ge(r_ready, 3 * b + 2)
                for t in range(TPS):
                    ins = dve.tensor_scalar(h[:, t, :], h[:, t, :], rstd[:, t:t + 1], None, ALU.mult)
                ins.then_inc(h_ready, 1)
                dve.wait_ge(k_ready, b + 1)
                dve.wait_ge(proj_done, 5 * b + 3)
                link(dve.tensor_tensor(k[:, :], k[:, :], pv[:, :], ALU.mult))
                dve.wait_ge(a_ready, b + 1)
                link(dve.tensor_tensor_scan(y[:, :], a[:, :], k[:, :], 0.0, ALU.mult, ALU.add))
                dve.wait_ge(proj_done, 5 * b + 4)
                link(dve.tensor_tensor(y[:, :], y[:, :], pq[:, :], ALU.mult))
                dve.wait_ge(sg_ready, b + 1)
                link(dve.tensor_tensor(sg[:, :], sg[:, :], pg[:, :], ALU.mult))
                dve.tensor_tensor(y[:, :], y[:, :], sg[:, :], ALU.mult).then_inc(y_ready, 1)
                dve.wait_ge(o_done, b + 1)
                row_stats(dve, link, op, st, mv).then_inc(stats, 1)
                dve.wait_ge(r_ready, 3 * b + 3)
                for t in range(TPS):
                    ins = dve.tensor_scalar(o[:, t, :], op[:, t, :], mv[:, t, 0:1], rstd[:, t:t + 1], ALU.subtract, ALU.mult)
                link(ins)
                xs = X[:, bass.ds(b * TPS, TPS), :]
                link(dve.tensor_tensor(xs, xs, o[:, :, :], ALU.add))
                link.end()

        @block.scalar
        def _(act_e):
            act_e.wait_ge(g_ready, 1)
            with act_e.Fori(0, BATCH) as b:
                act_e.wait_ge(tp_done, b + 1)
                act_e.activation(xT[:, :], tp[:, :], ACT.Copy, scale=gamma[:, 0:1]).then_inc(xT_ready, 1)
                act_e.wait_ge(proj_done, 5 * b + 1)
                act_e.activation(k[:, :], pk[:, :], ACT.Copy).then_inc(k_ready, 1)
                act_e.wait_ge(proj_done, 5 * b + 2)
                act_e.activation(a[:, :], pa[:, :], ACT.Sigmoid).then_inc(a_ready, 1)
                act_e.wait_ge(proj_done, 5 * b + 5)
                act_e.activation(sg[:, :], pg[:, :], ACT.Sigmoid).then_inc(sg_ready, 1)

        @block.tensor
        def _(pe):
            pe.wait_ge(loaded, 16 * 7)
            with pe.Fori(0, BATCH) as b:
                pe.wait_ge(h_ready, b + 1)
                for t in range(TPS):
                    ins = pe.transpose(tp[:, t * P:(t + 1) * P], h[:, t, :], ident[:, :])
                ins.then_inc(tp_done, 1)
                pe.wait_ge(xT_ready, b + 1)
                for n, dst in (("wk", pk), ("wa", pa), ("wv", pv), ("wq", pq), ("wg", pg)):
                    pe.matmul(dst[:, :], W[n][:, :], xT[:, :], start=True, stop=True).then_inc(proj_done, 1)
                pe.wait_ge(y_ready, b + 1)
                for t in range(TPS):
                    ins = pe.matmul(op[:, t, :], y[:, t * P:(t + 1) * P], W["wo"][:, :], start=True, stop=True)
                ins.then_inc(o_done, 1)


def phase_ffn(nc, w, res, out):
    TWO_PI = 6.283185307179586
    ROUND = 1.5 * 2.0 ** 23
    HI = 6.28125
    MID = 0.0019350051879882812
    LO = TWO_PI - HI - MID
    with ExitStack() as ctx:
        sb, pb, sem = tensors(nc, ctx, "pf")
        w1, w2 = sb("w1", [D, FF]), sb("w2", [P, FC, D])
        cf = sb("cf", [P, 4, FC])
        b2 = sb("b2", [P, D])
        th, nn, sn, cs, c = (sb(n, [P, FC]) for n in ("th", "nn", "sn", "cs", "c"))
        mhalf = sb("mhalf", [P, TPS])
        st, mv, rstd = sb("st", [P, TPS, 6]), sb("mv", [P, TPS, 2]), sb("rstd", [P, TPS])
        h, o = sb("h", [P, TPS, D]), [sb(f"o{u}", [P, TPS, D]) for u in range(2)]
        xT = sb("xT", [D, SEQ])
        hid, turn, near, sine = ([sb(f"{n}{f}", [P, SEQ]) for f in range(FC)] for n in ("hid", "turn", "near", "sine"))
        tp = pb("tp", [P, SEQ])
        hp = [pb(f"hp{f}", [P, SEQ]) for f in range(FC)]
        op = pb("op", [P, TPS, D])
        loaded, consts, own, pown, coef, trig, stats, eps_added, r_ready, h_ready, tp_done, xT_ready, hp_done, hid_ready, frac, sine_ready, act_ready, relu_ready, o_done, o_ready, out_done, halfpi = (
            sem(n) for n in ("loaded", "consts", "own", "pown", "coef", "trig", "stats", "eps_added", "r_ready", "h_ready", "tp_done", "xT_ready", "hp_done",
                             "hid_ready", "frac", "sine_ready", "act_ready", "relu_ready", "o_done", "o_ready", "out_done", "halfpi"))
        pool_waits, dve_waits, pe_waits = sem("pool_waits"), sem("dve_waits"), sem("pe_waits")
        block = ctx.enter_context(nc.Block())
        X, ident = res["x"], res["ident"]

        @block.sync
        def _(sp):
            sp.dma_start(w1[:, :], w["pf_w1"]).then_inc(loaded, 16)
            sp.dma_start(w2[:, :, :], w["pf_w2"].rearrange("(c f) d -> f c d", f=P)).then_inc(loaded, 16)
            sp.dma_start(cf[:, :, :], w["pf_cols"]).then_inc(loaded, 16)
            sp.dma_start(b2[:, :], w["pf_b2"].partition_broadcast(P)).then_inc(loaded, 16)
            with sp.Fori(0, BATCH) as b:
                sp.wait_ge(o_ready, b + 1)
                sp.dma_start(out[bass.ds(b, 1), :, :].rearrange("a (t p) d -> p (a t) d", p=P), X[:, bass.ds(b * TPS, TPS), :]).then_inc(out_done, 16)
            sp.wait_ge(out_done, 16 * BATCH)

        @block.gpsimd
        def _(pool):
            pool.memset(mhalf[:, :], -0.5).then_inc(consts, 1)
            pool.wait_ge(consts, 1)
            with pool.Fori(0, BATCH) as b:
                for n in range(2):
                    wait_apart(pool, stats, 2 * b + n + 1, pool_waits)
                    pool.tensor_scalar(rstd[:, :], mv[:, :, 1], 1e-5, None, ALU.add).then_inc(eps_added, 1)
                    pool.wait_ge(eps_added, 2 * b + n + 1)
                    pool.tensor_tensor(rstd[:, :], rstd[:, :], mhalf[:, :], ALU.pow).then_inc(r_ready, 1)

        @block.vector
        def _(dve):
            dve.wait_ge(loaded, 64)
            start = Chain(dve, coef, 0, 16)
            b1, phase, real, imag = (cf[:, n, :] for n in range(4))

            def wrap(dst, src):
                start(dve.tensor_scalar(nn[:, :], src, 1.0 / TWO_PI, ROUND, ALU.mult, ALU.add))
                start(dve.tensor_scalar(nn[:, :], nn[:, :], -ROUND, None, ALU.add))
                start(dve.scalar_tensor_tensor(dst, nn[:, :], -HI, src, ALU.mult, ALU.add))
                start(dve.scalar_tensor_tensor(dst, nn[:, :], -MID, dst, ALU.mult, ALU.add))
                start(dve.scalar_tensor_tensor(dst, nn[:, :], -LO, dst, ALU.mult, ALU.add))
                start(dve.tensor_scalar(dst, dst, -3.141592, 3.141592, ALU.max, ALU.min))

            wrap(th[:, :], phase)
            start(dve.tensor_scalar(cs[:, :], th[:, :], TWO_PI / 4, None, ALU.add))
            wrap(cs[:, :], cs[:, :])
            dve.tensor_scalar(nn[:, :], nn[:, :], 0.0, None, ALU.mult).then_inc(halfpi, 1)
            dve.wait_ge(trig, 2)
            start(dve.tensor_tensor(cs[:, :], cs[:, :], real, ALU.mult))
            start(dve.tensor_tensor(sn[:, :], sn[:, :], imag, ALU.mult))
            start(dve.tensor_tensor(c[:, :], cs[:, :], sn[:, :], ALU.add))
            dve.scalar_tensor_tensor(c[:, :], c[:, :], 0.1, imag, ALU.mult, ALU.mult).then_inc(pown, 1)
            dve.tensor_scalar(th[:, :], th[:, :], 1.0 / TWO_PI, None, ALU.mult).then_inc(pown, 1)
            dve.wait_ge(pown, 2)
            start.end()
            K = 16
            with dve.Fori(0, BATCH) as b:
                link = Chain(dve, own, b, K, waits=dve_waits)
                xr = [X[:, bass.ds(b * TPS + t, 1), :].rearrange("p a d -> p (a d)") for t in range(TPS)]
                for t in range(TPS):
                    ins = dve.bn_stats(st[:, t, :], xr[t])
                link.apart(ins)
                for t in range(TPS):
                    ins = dve.bn_aggr(mv[:, t, :], st[:, t, :])
                ins.then_inc(stats, 1)
                dve.wait_ge(r_ready, 2 * b + 1)
                for t in range(TPS):
                    ins = dve.tensor_scalar(h[:, t, :], xr[t], mv[:, t, 0:1], rstd[:, t:t + 1], ALU.subtract, ALU.mult)
                ins.then_inc(h_ready, 1)
                for f in range(FC):
                    dve.wait_ge(hid_ready, FC * b + f + 1)
                    link(dve.tensor_scalar(turn[f][:, :], hid[f][:, :], 0.1 / TWO_PI, th[:, f:f + 1], ALU.mult, ALU.add))
                    link(dve.tensor_scalar(near[f][:, :], turn[f][:, :], ROUND, -ROUND, ALU.add, ALU.add))
                    dve.tensor_tensor(turn[f][:, :], turn[f][:, :], near[f][:, :], ALU.subtract).then_inc(frac, 1)
                for f in range(FC):
                    dve.wait_ge(sine_ready, FC * b + f + 1)
                    link(dve.scalar_tensor_tensor(hid[f][:, :], sine[f][:, :], c[:, f:f + 1], hid[f][:, :], ALU.mult, ALU.add))
                    dve.tensor_scalar(hid[f][:, :], hid[f][:, :], 0.0, None, ALU.max).then_inc(act_ready, 1)
                dve.wait_ge(o_done, b + 1)
                link(dve.tensor_tensor(h[:, :, :], op[:, :, :], b2[:, :].unsqueeze(1).to_broadcast([P, TPS, D]), ALU.add))
                row_stats(dve, link, h, st, mv).then_inc(stats, 1)
                dve.wait_ge(r_ready, 2 * b + 2)
                for t in range(TPS):
                    ins = dve.tensor_scalar(h[:, t, :], h[:, t, :], mv[:, t, 0:1], rstd[:, t:t + 1], ALU.subtract, ALU.mult)
                link(ins)
                xs = X[:, bass.ds(b * TPS, TPS), :]
                dve.tensor_tensor(xs, xs, h[:, :, :], ALU.add).then_inc(o_ready, 1)
                dve.wait_ge(o_ready, b + 1)
                link.end()

        @block.scalar
        def _(act_e):
            act_e.wait_ge(halfpi, 1)
            act_e.activation(sn[:, :], th[:, :], ACT.Sin).then_inc(trig, 1)
            act_e.activation(cs[:, :], cs[:, :], ACT.Sin).then_inc(trig, 1)
            with act_e.Fori(0, BATCH) as b:
                act_e.wait_ge(tp_done, b + 1)
                act_e.activation(xT[:, :], tp[:, :], ACT.Copy).then_inc(xT_ready, 1)
                for f in range(FC):
                    act_e.wait_ge(hp_done, FC * b + f + 1)
                    act_e.activation(hid[f][:, :], hp[f][:, :], ACT.Identity, bias=cf[:, 0, f:f + 1]).then_inc(hid_ready, 1)
                for f in range(FC):
                    act_e.wait_ge(frac, FC * b + f + 1)
                    act_e.activation(sine[f][:, :], turn[f][:, :], ACT.Sin, scale=6.283185).then_inc(sine_ready, 1)

        @block.tensor
        def _(pe):
            pe.wait_ge(loaded, 64)
            with pe.Fori(0, BATCH) as b:
                pe.wait_ge(h_ready, b + 1)
                for t in range(TPS):
                    ins = pe.transpose(tp[:, t * P:(t + 1) * P], h[:, t, :], ident[:, :])
                ins.then_inc(tp_done, 1)
                pe.wait_ge(xT_ready, b + 1)
                for f in range(FC):
                    pe.matmul(hp[f][:, :], w1[:, f * P:(f + 1) * P], xT[:, :], start=True, stop=True).then_inc(hp_done, 1)
                pe.wait_ge(act_ready, FC * (b + 1))
                for t in range(TPS):
                    for f in range(FC):
                        ins = pe.matmul(op[:, t, :], hid[f][:, t * P:(t + 1) * P], w2[:, f, :], start=(f == 0), stop=(f == FC - 1))
                ins.then_inc(o_done, 1)


def build(nc, w, out):
    scr = {name: nc.dram_tensor(f"scratch_{name}", shape, FP32, kind="Internal").ap() for name, shape in (
        ("v", (BATCH, WIN + SEQ, D)), ("k", (BATCH, P, SEQ)), ("kb", (BATCH, P, SEQ)), ("vb", (BATCH, P, SEQ)), ("qT", (BATCH, D, SEQ)),
        ("A", (BATCH, P, SEQ)), ("attnT", (BATCH, P, SEQ)), ("T", (BATCH // 2, P, CH * CH)), ("probs", (BATCH * SEQ, H * NGATE)),
        ("ofir", (BATCH, SEQ, D)), ("o", (BATCH, P, SEQ)))}
    with ExitStack() as ctx:
        def sb(name, shape):
            return ctx.enter_context(nc.sbuf_tensor(name, shape, FP32))

        res = {"x": sb("x_rows", [P, NT, D]), "ident": sb("ident", [P, P])}
        with ExitStack() as mid:
            for name, shape in (("probs", [P, NT, H * NGATE]), ("eps", [P, H]), ("inv_temp", [P, H]), ("logits", [P, NT, H * NGATE])):
                res[name] = mid.enter_context(nc.sbuf_tensor(name, shape, FP32))
            delta_inputs(nc, w["x"], w, scr, res)
            fir_and_inverses(nc, w, scr, res)
            delta_rule(nc, scr, res)
            with ExitStack() as ffn:
                for name, shape in (("n2T", [D, BATCH, SEQ]), ("x2", [P, NT, D]), ("router", [P, NT, NE])):
                    res[name] = ffn.enter_context(nc.sbuf_tensor(name, shape, FP32))
                attention_output(nc, w, scr, res)
                experts(nc, w, scr, res)
        gate_loop(nc, w, res)
        phase_ffn(nc, w, res, out)


def kernel(**inputs):
    import numpy as np
    import concourse.bacc as bacc
    from concourse.bass_utils import run_bass_kernel_spmd

    nc = bacc.Bacc("TRN2", target_bir_lowering=False, num_devices=1)
    a = {k: np.asarray(v) for k, v in inputs.items()}
    L0, F0, L1, F1 = "L0_attn_", "L0_ffn_", "L1_attn_", "L1_ffn_"
    firs = np.zeros((D, len(FIRS), PADW), np.float32)
    for n, (name, k) in enumerate(zip(("fir_s", "fir_m", "fir_l"), FIRS)):
        firs[:, n, 2 * WIN - k:2 * WIN] = a[L0 + name].reshape(D, k)
    laid = {
        "x": a[L0 + "hidden_states"], "wqT": a[L0 + "Wq"].T, "wkT": a[L0 + "Wk"].T, "wvT": a[L0 + "Wv"].T, "woT": a[L0 + "Wo"].T,
        "gatesT": np.concatenate([a[L0 + "gate_w"].reshape(H * NGATE, D), a[L0 + "Wb"]]).T,
        "taps": np.stack([a[L0 + "conv_q"], a[L0 + "conv_k"], a[L0 + "conv_v"]], 1),
        "gate_b": a[L0 + "gate_b"].reshape(-1), "log_temp": a[L0 + "log_temp"].reshape(-1), "eps": a[L0 + "eps_param"].reshape(-1),
        "fir_pad": firs.reshape(D * len(FIRS), PADW),
        "ao_cols": np.stack([np.tile(a[L0 + "norm_w"], H), a[F0 + "g1"], a[F0 + "be1"], a[F0 + "g2"], a[F0 + "be2"]], 1),
        "mix_w": a[F0 + "mix_w"], "mix_b": a[F0 + "mix_b"], "router_w": a[F0 + "router_w"], "w1": a[F0 + "w1"], "w2": a[F0 + "w2"],
        "b1": a[F0 + "b1"].reshape(NE * FC, P).T, "b2": a[F0 + "b2"],
        "gamma": a[L1 + "gamma"].reshape(D, 1), **{f"gl_{n}": a[L1 + n] for n in ("wq", "wk", "wv", "wa", "wg", "wo")},
        "pf_w1": a[F1 + "W1"], "pf_w2": a[F1 + "W2"], "pf_b2": a[F1 + "b2"],
        "pf_cols": np.stack([a[F1 + n].reshape(FC, P).T for n in ("b1", "quantum_phases", "quantum_weights_real", "quantum_weights_imag")], 1),
    }
    arrays = {f"in_{k}": np.ascontiguousarray(v) for k, v in laid.items()}
    w = {k: nc.dram_tensor(f"in_{k}", arrays[f"in_{k}"].shape, FP32, kind="ExternalInput").ap() for k in laid}
    out = nc.dram_tensor("out", (BATCH, SEQ, D), FP32, kind="ExternalOutput").ap()
    build(nc, w, out)
    return run_bass_kernel_spmd(nc, [arrays], core_ids=[0]).results[0]["out"]
```

```python
import concourse.bass as bass
from concourse import mybir
from contextlib import ExitStack

FP32 = mybir.dt.float32
ALU = mybir.AluOpType
ACT = mybir.ActivationFunctionType
AX = mybir.AxisListType

BATCH, SEQ, D = 16, 512, 128
P = 128
TPS = SEQ // P
NT = BATCH * TPS
H, DH = 4, 32
CH = 32
CPT = P // CH
CPS = SEQ // CH
TAPS = 4
FIRS = (3, 15, 63)
WIN = 64
NWIN = SEQ // WIN
NGATE = 5
NE, FF = 8, 512
FC = FF // P
PADW = 2 * WIN + WIN - 1


class Chain:

    def __init__(self, eng, sem, turn=0, per_turn=0, start=0, waits=None):
        self.sem_of_waits = waits
        self.eng, self.sem, self.base, self.per_turn, self.n = eng, sem, turn * per_turn, per_turn, start

    def __call__(self, ins):
        self.n += 1
        ins.then_inc(self.sem, 1)
        self.eng.wait_ge(self.sem, self.base + self.n)

    def apart(self, ins):
        self(ins)
        self.eng.sem_inc(self.sem_of_waits, 1)

    def end(self):
        assert self.n == self.per_turn, (self.n, self.per_turn)


def wait_apart(eng, sem, value, waits):
    eng.wait_ge(sem, value)
    eng.sem_inc(waits, 1)


def tensors(nc, ctx, tag):
    ctx.callback(nc.all_engine_barrier)

    def sb(name, shape, dt=FP32):
        return ctx.enter_context(nc.sbuf_tensor(f"{tag}_{name}", shape, dt))

    def pb(name, shape, dt=FP32):
        return ctx.enter_context(nc.psum_tensor(f"{tag}_{name}", shape, dt))

    def sem(name):
        held = ctx.enter_context(nc.semaphore(f"{tag}_{name}"))
        ctx.callback(nc.gpsimd.sem_clear, held)
        return held

    return sb, pb, sem


def heads(ap):
    return ap.rearrange("p t (h d) -> p (t h) d", h=H)


def flat(ap):
    return ap.rearrange("p t d -> p (t d)")


def nth(i, u, n, of, side=2):
    return i * (side * of) + (side * n + u + 1)


def one(ap):
    return ap.rearrange("p a n -> p (a n)")


def over(ap, n):
    return ap.unsqueeze(2).to_broadcast([ap.shape[0], ap.shape[1], n])


def row_norm(dve, src, dst, mv, rstd):
    for t in range(TPS):
        ins = dve.tensor_scalar(dst[t], src[t], mv[:, t, 0:1], rstd[:, t:t + 1], ALU.subtract, ALU.mult)
    return ins


def tiles_of(ap):
    return [ap[:, t, :] for t in range(TPS)]


def pair_stats(dve, link, srcs, st, mv, ready):
    for u in range(len(srcs)):
        for t, x in enumerate(srcs[u]()):
            ins = dve.bn_stats(st[u][:, t, :], x)
        link.apart(ins)
        for t in range(TPS):
            ins = dve.bn_aggr(mv[u][:, t, :], st[u][:, t, :])
        ins.then_inc(ready, 1)


def row_stats(dve, link, x, st, mv):
    for t in range(TPS):
        ins = dve.bn_stats(st[:, t, :], x[:, t, :])
        if t == TPS - 1:
            link.apart(ins)
    for t in range(TPS):
        last = dve.bn_aggr(mv[:, t, :], st[:, t, :])
    return last


def delta_inputs(nc, x, w, scr, res):
    with ExitStack() as ctx:
        sb, pb, sem = tensors(nc, ctx, "di")
        two = lambda name, shape: [sb(f"{name}{u}", shape) for u in range(2)]
        wq, wk, wv = (sb(n, [D, D]) for n in ("wq", "wk", "wv"))
        wg = sb("wg", [D, H * NGATE + H])
        taps = sb("taps", [D, 3, TAPS])
        gate_b = sb("gate_b", [P, H * NGATE])
        log_temp = sb("log_temp", [P, H])
        mhalf = sb("mhalf", [P, H * TPS])
        lower = sb("lower", [P, CH])
        upper = sb("upper", [P, CH])
        zrow = sb("zrow", [P, D])
        st, mv, rstd = two("st", [P, TPS, 6]), two("mv", [P, TPS, 2]), two("rstd", [P, TPS])
        xn, xnT = two("xn", [P, TPS, D]), two("xnT", [D, SEQ])
        conv = [two(f"conv{n}", [D, SEQ]) for n in range(3)]
        kact, vact = two("kact", [D, SEQ]), two("vact", [D, SEQ])
        sq = [two(f"sq{n}", [D, SEQ]) for n in range(2)]
        head_of = sb("head_of", [D, H])
        ss = two("ss", [P, 2, TPS * H])
        rn = two("rn", [P, TPS * H])
        kt, kb, vt, vb = (two(n, [P, TPS, D]) for n in ("kt", "kb", "vt", "vb"))
        kq = two("kq", [D, 2, SEQ])
        beta = two("beta", [P, TPS * H])
        am, at = two("am", [P, H, TPS, CH]), two("at", [P, H, TPS, CH])
        A = [pb(f"A{u}", [P, 4, 512]) for u in range(2)]

        loaded, consts, x_first, x_rest, x_in, stored, zst, lt, own = (
            sem(n) for n in ("loaded", "consts", "x_first", "x_rest", "x_in", "stored", "zst", "lt", "own"))
        ln_own, rq_ready = sem("ln_own"), sem("rq_ready")
        sums_ready, eps_added, rstd_ready, xn_ready, xT_done, xnT_ready, proj_done, gates_done = (
            sem(n) for n in ("sums_ready", "eps_added", "rstd_ready", "xn_ready", "xT_done", "xnT_ready", "proj_done", "gates_done"))
        tap_done, conv_ready, act_ready, tok_done, sq_ready, ss_ready, ss_eps, rn_ready = (
            sem(n) for n in ("tap_done", "conv_ready", "act_ready", "tok_done", "sq_ready", "ss_ready", "ss_eps", "rn_ready"))
        v_ready, vb_ready, kb_ready, tok_ready, back_done, back_ready, beta_ready, gram_done, masked, at_ready, am_ready, sums_done = (
            sem(n) for n in ("v_ready", "vb_ready", "kb_ready", "tok_ready", "back_done", "back_ready", "beta_ready", "gram_done", "masked", "at_ready", "am_ready", "sums_done"))
        pool_waits, dve_waits, pe_waits = sem("pool_waits"), sem("dve_waits"), sem("pe_waits")
        block = ctx.enter_context(nc.Block())
        X, ident = res["x"], res["ident"]
        PAIRS = BATCH // 2
        STORES = 7 * 2
        CONSTS = 6 + 2 * CPT + 1 + H
        per_head = lambda ap: ap.rearrange("p (g d) -> p g d", d=DH)

        @block.sync
        def _(sp):
            sp.dma_start(X[:, 0:2 * TPS, :], x[0:2, :, :].rearrange("b (t p) d -> p (b t) d", p=P)).then_inc(x_first, 16)
            sp.dma_start(X[:, 2 * TPS:, :], x[2:, :, :].rearrange("b (t p) d -> p (b t) d", p=P)).then_inc(x_rest, 16)
            sp.wait_ge(consts, 1)
            sp.dma_start(scr["xs"].rearrange("(p a) d -> p a d", p=P), zrow[:, :].unsqueeze(1).to_broadcast([P, NTL + DEEP, D])).then_inc(zst, 16)
            for b in range(BATCH):
                sp.dma_start(scr["v"][b, 0:WIN, :], zrow[0:WIN, :]).then_inc(zst, 16)
            sp.wait_ge(x_first, 16)
            sp.sem_inc(x_in, 1)
            sp.wait_ge(x_rest, 16)
            sp.sem_inc(x_in, PAIRS - 1)
            with sp.Fori(0, PAIRS) as i:
                rows = lambda name, u: scr[name][bass.ds(2 * i + u, 1), :, :].rearrange("a p n -> (a p) n")
                for u in range(2):
                    sp.wait_ge(v_ready, nth(i, u, 0, 1))
                    sp.dma_start(scr["v"][bass.ds(2 * i + u, 1), WIN:WIN + SEQ, :].rearrange("a (t p) d -> p (a t) d", p=P), vt[u][:, :, :]).then_inc(stored, 16)
                for name, src, ready, n, of in (("vb", vb, vb_ready, 0, 1), ("k", kt, tok_ready, 0, 1), ("kb", kb, kb_ready, 0, 1)):
                    for u in range(2):
                        sp.wait_ge(ready, nth(i, u, n, of))
                        sp.dma_start(rows(name, u), flat(src[u][:, :, :])).then_inc(stored, 16)
                for u in range(2):
                    sp.wait_ge(act_ready, nth(i, u, 0, 3))
                    sp.dma_start(rows("qT", u), kq[u][:, 1, :]).then_inc(stored, 16)
                for u in range(2):
                    for name, src, ready in (("attnT", at, at_ready), ("A", am, am_ready)):
                        sp.wait_ge(ready, nth(i, u, 0, 1) + (2 if ready is at_ready else 0))
                        sp.dma_start(rows(name, u), src[u][:, :, :, :].rearrange("p h t c -> p (h t c)")).then_inc(stored, 16)
            sp.wait_ge(stored, 16 * STORES * (PAIRS + 1))
            sp.wait_ge(zst, 16 * (BATCH + 1))

        @block.gpsimd
        def _(pool):
            const = Chain(pool, consts)
            for dst, value in ((zrow, 0.0), (ident, 0.0), (lower, -1.0), (upper, 1.0), (mhalf, -0.5)):
                const(pool.memset(dst[:, :], value))
            const(pool.affine_select(out=ident[:, :], in_=ident[:, :], compare_op=ALU.not_equal, fill=1.0,
                                     base=0, pattern=[[-1, P]], channel_multiplier=1))
            for c in range(CPT):
                rows = slice(CH * c, CH * c + CH)
                const(pool.affine_select(out=lower[rows, :], in_=lower[rows, :], compare_op=ALU.is_gt, fill=0.0,
                                         base=0, pattern=[[-1, CH]], channel_multiplier=1))
                const(pool.affine_select(out=upper[rows, :], in_=upper[rows, :], compare_op=ALU.is_ge, fill=0.0,
                                         base=0, pattern=[[1, CH]], channel_multiplier=-1))
            const(pool.memset(head_of[:, :], 0.0))
            for h in range(H):
                const(pool.memset(head_of[h * DH:(h + 1) * DH, h:h + 1], 1.0))

            def norm_powers(i):
                for u in range(2):
                    wait_apart(pool, sums_ready, nth(i, u, 0, 1), pool_waits)
                    pool.tensor_scalar(rstd[u][:, :], mv[u][:, :, 1], 1e-5, None, ALU.add).then_inc(eps_added, 1)
                    pool.wait_ge(eps_added, nth(i, u, 0, 1))
                    pool.tensor_tensor(rstd[u][:, :], rstd[u][:, :], mhalf[:, 0:TPS], ALU.pow).then_inc(rstd_ready, 1)

            def pair(i, more):
                for u in range(2):
                    pool.wait_ge(ss_ready, nth(i, u, 0, 1))
                    pool.tensor_tensor(rn[u][:, :], ss[u][:, 1, :], mhalf[:, :], ALU.pow).then_inc(rn_ready, 1)
                if more:
                    norm_powers(i + 1)
                pool.wait_ge(stored, (i + 1) * (16 * STORES))
                for u in range(2):
                    pool.wait_ge(v_ready, nth(i, u, 0, 1))
                    pool.tensor_tensor(heads(vb[u][:, :, :]), heads(vt[u][:, :, :]), over(beta[u][:, :], DH), ALU.mult).then_inc(vb_ready, 1)
                for u in range(2):
                    pool.wait_ge(tok_ready, nth(i, u, 0, 1))
                    pool.tensor_tensor(heads(kb[u][:, :, :]), heads(kt[u][:, :, :]), over(beta[u][:, :], DH), ALU.mult).then_inc(kb_ready, 1)
                for u in range(2):
                    pool.tensor_tensor(res["rq"][:, bass.ds((2 * i + u) * TPS, TPS), :], ss[u][:, 0, :].rearrange("p (t h) -> p t h", h=H),
                                       mhalf[:, :].rearrange("p (t h) -> p t h", h=H), ALU.pow).then_inc(rq_ready, 1)
                for u in range(2):
                    pool.wait_ge(masked, nth(i, u, 0, 1))
                    bt = beta[u][:, :].rearrange("p (t h) -> p h t", t=TPS).unsqueeze(3).to_broadcast([P, H, TPS, CH])
                    pool.tensor_tensor(am[u][:, :, :, :], am[u][:, :, :, :], bt, ALU.mult).then_inc(am_ready, 1)

            norm_powers(0)
            with pool.Fori(0, PAIRS - 1) as i:
                pair(i, True)
            pair(PAIRS - 1, False)

        @block.vector
        def _(dve):
            K = 3 * (TAPS - 2)
            rows = lambda i, u: [one(X[:, bass.ds((2 * i + u) * TPS + t, 1), :]) for t in range(TPS)]

            def sums(i):
                link = Chain(dve, ln_own, i, 2, waits=dve_waits)
                pair_stats(dve, link, [lambda: rows(i, 0), lambda: rows(i, 1)], st, mv, sums_ready)
                link.end()

            def norm(i):
                for u in range(2):
                    dve.wait_ge(rstd_ready, nth(i, u, 0, 1))
                    row_norm(dve, rows(i, u), tiles_of(xn[u]), mv[u], rstd[u]).then_inc(xn_ready, 1)

            def pair(i, more):
                link = Chain(dve, own, i, K, waits=dve_waits)
                for n in range(3):
                    for j in range(TAPS - 1):
                        s = TAPS - 1 - j
                        for u in range(2):
                            if j == 0:
                                dve.wait_ge(tap_done, nth(i, u, n, 3))
                            ins = dve.scalar_tensor_tensor(conv[n][u][:, s:], A[u][:, 1 + n, 0:SEQ - s], taps[:, n, j:j + 1],
                                                           conv[n][u][:, s:], ALU.mult, ALU.add)
                            if j == TAPS - 2:
                                ins.then_inc(conv_ready, 1)
                        if j < TAPS - 2:
                            link(ins)
                    if n == 1:
                        for u in range(2):
                            dve.wait_ge(beta_ready, nth(i, u, 0, 1))
                            dve.tensor_tensor(res["logits"][:, bass.ds((2 * i + u) * TPS, TPS), :],
                                              A[u][:, 0, 0:96].rearrange("p (t g) -> p t g", t=TPS)[:, :, 0:20],
                                              gate_b[:, :].unsqueeze(1).to_broadcast([P, TPS, 20]), ALU.add)
                for u in range(2):
                    dve.wait_ge(sums_done, nth(i, u, 0, 1))
                    dve.tensor_scalar(ss[u][:, :, :], A[u][:, 1, 0:2 * TPS * H].rearrange("p (n g) -> p n g", n=2), 1e-6, None, ALU.add).then_inc(ss_ready, 1)
                if more:
                    wait_apart(dve, x_in, i + 2, dve_waits)
                    sums(i + 1)
                dve.wait_ge(stored, (i + 1) * (16 * STORES))
                for u in range(2):
                    dve.wait_ge(rn_ready, nth(i, u, 0, 1))
                    dve.tensor_tensor(heads(kt[u][:, :, :]), per_head(A[u][:, 2, :]), over(rn[u][:, :], DH), ALU.mult).then_inc(tok_ready, 1)
                if more:
                    norm(i + 1)
                for u in range(2):
                    dve.wait_ge(gram_done, nth(i, u, 0, 1))
                    for dst, n, mask, ready in ((am, 0, lower, masked), (at, 1, upper, at_ready)):
                        m = mask[:, :].unsqueeze(1).unsqueeze(1).to_broadcast([P, H, TPS, CH])
                        src = A[u][:, :, 0:2 * TPS * CH].rearrange("p h (t n c) -> p h t n c", t=TPS, n=2)[:, :, :, n, :]
                        dve.tensor_tensor(dst[u][:, :, :, :], src, m, ALU.mult).then_inc(ready, 1)
                link.end()

            dve.wait_ge(loaded, 16 * 8)
            dve.wait_ge(consts, CONSTS)
            dve.wait_ge(x_in, 1)
            dve.sem_inc(at_ready, 2)
            sums(0)
            norm(0)
            with dve.Fori(0, PAIRS - 1) as i:
                pair(i, True)
            pair(PAIRS - 1, False)

        @block.scalar
        def _(act_e):
            for dst, src in ((wq, "wqT"), (wk, "wkT"), (wv, "wvT"), (wg, "gatesT")):
                act_e.dma_start(dst[:, :], w[src]).then_inc(loaded, 16)
            act_e.dma_start(taps[:, :, :], w["taps"]).then_inc(loaded, 16)
            act_e.dma_start(gate_b[:, :], w["gate_b"].partition_broadcast(P)).then_inc(loaded, 16)
            act_e.dma_start(log_temp[:, :], w["log_temp"].partition_broadcast(P)).then_inc(loaded, 16)
            act_e.dma_start(res["eps"][:, :], w["eps"].partition_broadcast(P)).then_inc(loaded, 16)
            act_e.sem_inc(stored, 16 * STORES)
            act_e.wait_ge(loaded, 16 * 8)
            act_e.activation(res["inv_temp"][:, :], log_temp[:, :], ACT.Exp, scale=-1.0).then_inc(lt, 1)

            def rows_by_channel(i):
                for u in range(2):
                    act_e.wait_ge(xT_done, nth(i, u, 0, 1))
                    act_e.activation(xnT[u][:, :], A[u][:, 0, :], ACT.Copy).then_inc(xnT_ready, 1)

            def pair(i, more):
                for n in range(3):
                    for u in range(2):
                        act_e.wait_ge(proj_done, nth(i, u, n, 3))
                        act_e.activation(conv[n][u][:, :], A[u][:, 1 + n, :], ACT.Copy, scale=taps[:, n, TAPS - 1:TAPS]).then_inc(tap_done, 1)
                act_e.wait_ge(stored, (i + 1) * (16 * STORES))
                for u in range(2):
                    act_e.wait_ge(gates_done, nth(i, u, 0, 1))
                    act_e.activation(beta[u][:, :].rearrange("p (t h) -> p t h", t=TPS), A[u][:, 0, 0:96].rearrange("p (t g) -> p t g", t=TPS)[:, :, 20:24],
                                     ACT.Sigmoid).then_inc(beta_ready, 1)
                for n, dst in enumerate(([kq[u][:, 1, :] for u in range(2)], [kact[u][:, :] for u in range(2)], [vact[u][:, :] for u in range(2)])):
                    for u in range(2):
                        act_e.wait_ge(conv_ready, nth(i, u, n, 3))
                        act_e.activation(dst[u], conv[n][u][:, :], ACT.Silu).then_inc(act_ready, 1)
                    if n < 2:
                        for u in range(2):
                            act_e.wait_ge(act_ready, nth(i, u, n, 3))
                            act_e.activation(sq[n][u][:, :], dst[u], ACT.Square).then_inc(sq_ready, 1)
                for u in range(2):
                    act_e.wait_ge(tok_done, nth(i, u, 1, 2))
                    act_e.activation(flat(vt[u][:, :, :]), A[u][:, 3, :], ACT.Copy).then_inc(v_ready, 1)
                for u in range(2):
                    act_e.wait_ge(back_done, nth(i, u, 0, 1))
                    act_e.activation(kq[u][:, 0, :], A[u][:, 2, :], ACT.Copy).then_inc(back_ready, 1)
                if more:
                    rows_by_channel(i + 1)

            rows_by_channel(0)
            with act_e.Fori(0, PAIRS - 1) as i:
                pair(i, True)
            pair(PAIRS - 1, False)

        @block.tensor
        def _(pe):
            pe.wait_ge(loaded, 16 * 8)
            pe.wait_ge(consts, CONSTS)

            def rows_by_channel(i):
                for u in range(2):
                    pe.wait_ge(xn_ready, nth(i, u, 0, 1))
                    for t in range(TPS):
                        ins = pe.transpose(A[u][:, 0, t * P:(t + 1) * P], xn[u][:, t, :], ident[:, :])
                    ins.then_inc(xT_done, 1)

            def pair(i, more):
                for n, wt in enumerate((wq, wk, wv)):
                    for u in range(2):
                        if n == 0:
                            pe.wait_ge(xnT_ready, nth(i, u, 0, 1))
                            pe.wait_ge(at_ready, nth(i, u, 0, 1))
                        pe.matmul(A[u][:, 1 + n, :], wt[:, :], xnT[u][:, :], start=True, stop=True).then_inc(proj_done, 1)
                for u in range(2):
                    for t in range(TPS):
                        ins = pe.matmul(A[u][:, 0, t * 24:(t + 1) * 24], xnT[u][:, t * P:(t + 1) * P], wg[:, :], start=True, stop=True)
                    ins.then_inc(gates_done, 1)
                for n, src in enumerate((kact, vact)):
                    for u in range(2):
                        pe.wait_ge(act_ready, nth(i, u, 1 + n, 3))
                        for t in range(TPS):
                            ins = pe.transpose(A[u][:, 2 + n, t * P:(t + 1) * P], src[u][:, t * P:(t + 1) * P], ident[:, :])
                        ins.then_inc(tok_done, 1)
                    if n == 0:
                        for u in range(2):
                            pe.wait_ge(sq_ready, nth(i, u, 1, 2))
                            for m in range(2):
                                for t in range(TPS):
                                    at_ = (m * TPS + t) * H
                                    ins = pe.matmul(A[u][:, 1, at_:at_ + H], sq[m][u][:, t * P:(t + 1) * P], head_of[:, :], start=True, stop=True)
                            ins.then_inc(sums_done, 1)
                for u in range(2):
                    pe.wait_ge(tok_ready, nth(i, u, 0, 1))
                    for t in range(TPS):
                        ins = pe.transpose(A[u][:, 2, t * P:(t + 1) * P], kt[u][:, t, :], ident[:, :])
                    ins.then_inc(back_done, 1)
                if more:
                    rows_by_channel(i + 1)
                for u in range(2):
                    wait_apart(pe, v_ready, nth(i, u, 0, 1), pe_waits)
                    if more:
                        wait_apart(pe, xnT_ready, nth(i + 1, u, 0, 1), pe_waits)
                    wait_apart(pe, back_ready, nth(i, u, 0, 1), pe_waits)
                    for t in range(TPS):
                        for c in range(CPT):
                            cols = slice(t * P + c * CH, t * P + (c + 1) * CH)
                            for h in range(H):
                                rows = slice(DH * h, DH * h + DH)
                                ins = pe.matmul(A[u][CH * c:CH * c + CH, h, t * 2 * CH:(t + 1) * 2 * CH],
                                                kq[u][rows, 0, cols], kq[u][rows, :, cols], start=True, stop=True)
                    ins.then_inc(gram_done, 1)

            rows_by_channel(0)
            with pe.Fori(0, PAIRS - 1) as i:
                pair(i, True)
            pair(PAIRS - 1, False)


def fir_and_inverses(nc, w, scr, res):
    with ExitStack() as ctx:
        sb, pb, sem = tensors(nc, ctx, "fi")
        NG = H * NGATE
        GC = 4
        F3 = len(FIRS)
        vwin = sb("vwin", [P, BATCH, NWIN, D])
        vst = [sb(f"vst{n}", [P, GC, P]) for n in range(2)]
        toep = [sb(f"toep{n}", [P, GC * F3, WIN]) for n in range(2)]
        tmp = [sb(f"tmp{n}", [P, 2, F3, WIN]) for n in range(2)]
        pw = sb("pw", [P, WIN, NG])
        pf = sb("pf", [P, H, F3, WIN])
        oc = sb("oc", [P, WIN, D])
        mx, sm = sb("mx", [P, NT * H]), sb("sm", [P, NT * H])
        gain = sb("gain", [P, H])
        GP = 2
        POOL_GROUPS = 3
        groups = BATCH // GP
        am = {e: sb(f"am_{e}", [P, CH, CH]) for e in ("pool", "dve")}
        um = {e: sb(f"um_{e}", [P, CH, CH]) for e in ("pool", "dve")}
        pr = {e: sb(f"pr_{e}", [P, CH * CH // 4 + CH]) for e in ("pool", "dve")}
        F = [pb(f"F{n}", [P, 2, 512]) for n in range(2)]
        win_in, own, pown, toep_in = sem("win_in"), sem("own"), sem("pown"), [sem("toep_in0"), sem("toep_in1")]
        down, fir_summed = sem("down"), sem("fir_summed")
        vst_ready, fir_done, fir_read, exps, prb, pw_out, pw_in, oc_out = (
            sem(n) for n in ("vst_ready", "fir_done", "fir_read", "exps", "prb", "pw_out", "pw_in", "oc_out"))
        mats_in = {e: sem(f"mats_in_{e}") for e in ("pool", "dve")}
        mats_out = {e: sem(f"mats_out_{e}") for e in ("pool", "dve")}
        solved = {e: sem(f"solved_{e}") for e in ("pool", "dve")}
        sub, pf_ready = sem("sub"), sem("pf_ready")
        pool_waits, dve_waits, pe_waits = sem("pool_waits"), sem("dve_waits"), sem("pe_waits")
        block = ctx.enter_context(nc.Block())
        L, PR, eps = res["logits"], res["probs"], res["eps"]
        L4 = L[:, :, :].rearrange("p t (h g) -> p (t h) g", h=H)
        P4 = PR[:, :, :].rearrange("p t (h g) -> p (t h) g", h=H)

        @block.sync
        def _(sp):
            for b in range(BATCH):
                sp.dma_start(vwin[:, b, :, :], bass.AP(tensor=scr["v"].tensor, offset=b * (SEQ + WIN) * D,
                                                       ap=[[D, P], [WIN * D, NWIN], [1, D]])).then_inc(win_in, 16)
            with sp.Fori(0, D // GC // 2) as i:
                for u in range(2):
                    sp.wait_ge(fir_done, 2 * i + u + 1)
                    rows = w["fir_pad"][bass.ds((2 * i + u) * (GC * F3), GC * F3), :]
                    src = bass.AP(tensor=rows.tensor, offset=rows.offset, ap=[[1, P], [PADW, GC * F3], [1, WIN]])
                    sp.dma_start(toep[u][:, :, :], src).then_inc(toep_in[u], 16)
            sp.wait_ge(fir_summed, D // GC)
            sp.dma_start(scr["ofir"].rearrange("b (j t) d -> (b j) t d", t=WIN), oc[:, :, :]).then_inc(oc_out, 16)
            sp.wait_ge(oc_out, 16)

        def matrices(eng, e, g):
            for b in range(GP):
                for c in range(CPT):
                    src = scr["A"][bass.ds(g * GP + b, 1), c * CH:(c + 1) * CH, :].rearrange("a i (x j) -> (a x) i j", j=CH)
                    p0 = b * 64 + c * 16
                    eng.dma_start(am[e][p0:p0 + 16, :, :], src).then_inc(mats_in[e], 16)

        def solve(eng, e, chain, turn, g):
            A_, U, R = am[e], um[e], pr[e]
            eng.sem_inc(pool_waits if e == "pool" else dve_waits, 1)
            chain.apart(eng.memset(U[:, :, :], 0.0))
            chain(eng.memset(U[:, :, :].rearrange("p a b -> p (a b)")[:, 0:CH * CH:CH + 1], 1.0))
            eng.wait_ge(mats_in[e], (turn + 1) * (16 * GP * CPT))
            for j in range(CH - 1):
                n, m = j + 1, CH - 1 - j
                prod = R[:, 0:n * m].rearrange("p (a b) -> p a b", a=n)
                chain(eng.tensor_tensor(prod, U[:, 0:n, j:j + 1].to_broadcast([P, n, m]),
                                        A_[:, j + 1:, j].unsqueeze(1).to_broadcast([P, n, m]), ALU.mult))
                ins = eng.tensor_tensor(U[:, 0:n, j + 1:], U[:, 0:n, j + 1:], prod, ALU.add)
                if j < CH - 2:
                    chain(ins)
            ins.then_inc(solved[e], 1)

        SOLVE = 2 + 2 * (CH - 1) - 1

        @block.gpsimd
        def _(pool):
            with pool.Fori(0, POOL_GROUPS) as g:
                matrices(pool, "pool", g)
                chain = Chain(pool, pown, g, SOLVE, waits=pool_waits)
                solve(pool, "pool", chain, g, g)
                chain.end()
                pool.wait_ge(solved["pool"], g + 1)
                pool.dma_start(scr["T"][bass.ds(g, 1), :, :].rearrange("a p n -> (a p) n"),
                               um["pool"][:, :, :].rearrange("p a b -> p (a b)")).then_inc(mats_out["pool"], 16)
                pool.wait_ge(mats_out["pool"], (g + 1) * 16)

        @block.vector
        def _(dve):
            SOFT = 9
            link = Chain(dve, own, 0, SOFT)
            temp = res["inv_temp"][:, :].unsqueeze(1).to_broadcast([P, NT, H])
            L_h = lambda g: L[:, :, :].rearrange("p t (h g) -> p t h g", h=H)[:, :, :, g]
            for g in range(NGATE):
                ins = dve.tensor_tensor(L_h(g), L_h(g), temp, ALU.mult)
            link(ins)
            link(dve.reduce_max(mx[:, :], L4, axis=AX.X))
            dve.tensor_tensor(L4, L4, over(mx[:, :], NGATE), ALU.subtract).then_inc(sub, 1)
            link(dve.tensor_scalar(eps[:, :], eps[:, :], 0.0, 0.2, ALU.max, ALU.min))
            link(dve.tensor_scalar(gain[:, :], eps[:, :], -5.0, 1.0, ALU.mult, ALU.add))
            dve.wait_ge(exps, 1)
            link(dve.reduce_sum(sm[:, :], P4, axis=AX.X))
            link(dve.reciprocal(sm[:, :], sm[:, :]))
            smh = sm[:, :].rearrange("p (t h) -> p t h", h=H)
            link(dve.tensor_tensor(smh, smh, gain[:, :].unsqueeze(1).to_broadcast([P, NT, H]), ALU.mult))
            link(dve.tensor_tensor(P4, P4, over(sm[:, :], NGATE), ALU.mult))
            ev = eps[:, :].unsqueeze(1).to_broadcast([P, NT, H])
            for g in range(NGATE):
                pg = PR[:, :, :].rearrange("p t (h g) -> p t h g", h=H)[:, :, :, g]
                ins = dve.tensor_tensor(pg, pg, ev, ALU.add)
            link(ins)
            p3 = P4[:, :, 3]
            dve.tensor_tensor(p3, p3, res["rq"][:, :, :].rearrange("p t h -> p (t h)"), ALU.mult).then_inc(prb, 1)
            dve.wait_ge(pw_in, 16)
            for h in range(H):
                for f in range(F3):
                    ins = dve.tensor_copy(pf[:, h, f, :], pw[:, ::-1, h * NGATE + f])
            ins.then_inc(pf_ready, 1)
            dve.wait_ge(pf_ready, 1)
            for u in range(2):
                dve.sem_inc(fir_read, 1)
            with dve.Fori(0, H) as h:
                with dve.Fori(0, DH // GC // 2) as k:
                    for u in range(2):
                        grp = h * (DH // GC) + k * 2 + u
                        dve.wait_ge(fir_done, grp + 3)
                        wgt = pf[:, bass.ds(h, 1), :, :].rearrange("p a f t -> p (a f) t").unsqueeze(1).to_broadcast([P, 2, F3, WIN])
                        for c2 in range(2):
                            ins = dve.tensor_tensor(tmp[c2][:, :, :, :], F[u][:, c2, 0:2 * F3 * WIN].rearrange("p (c f t) -> p c f t", c=2, f=F3),
                                                    wgt, ALU.mult)
                        ins.then_inc(fir_read, 1)
                        dve.wait_ge(fir_read, grp + 3)
                        for c2 in range(2):
                            out = oc[:, :, bass.ds(grp * GC + 2 * c2, 2)].rearrange("p t c -> p c t")
                            ins = dve.reduce_sum(out, tmp[c2][:, :, :, ::-1].rearrange("p c f t -> p c t f"), axis=AX.X)
                        ins.then_inc(fir_summed, 1)
                        dve.wait_ge(fir_summed, grp + 1)
            with dve.Fori(0, groups - POOL_GROUPS) as g:
                chain = Chain(dve, down, g, SOLVE, waits=dve_waits)
                solve(dve, "dve", chain, g, g)
                chain.end()
                dve.wait_ge(mats_out["dve"], (g + 1) * 16)
            link.end()

        @block.scalar
        def _(act_e):
            act_e.wait_ge(sub, 1)
            act_e.activation(PR[:, :, :], L[:, :, :], ACT.Exp).then_inc(exps, 1)
            act_e.wait_ge(prb, 1)
            act_e.dma_start(scr["probs"].rearrange("(t p) g -> p t g", p=P), PR[:, :, :]).then_inc(pw_out, 16)
            act_e.wait_ge(pw_out, 16)
            act_e.dma_start(pw[:, :, :], scr["probs"].rearrange("(w t) g -> w t g", t=WIN)).then_inc(pw_in, 16)
            act_e.wait_ge(win_in, 16 * BATCH)
            vw = vwin[:, :, :, :].rearrange("p b j d -> p (b j) d")
            with act_e.Fori(0, D // GC // 2) as i:
                for u in range(2):
                    act_e.wait_ge(fir_done, 2 * i + u + 1)
                    act_e.activation(vst[u][:, :, :], vw[:, :, bass.ds((2 * i + u) * GC, GC)].rearrange("p w c -> p c w"), ACT.Copy)\
                         .then_inc(vst_ready, 1)
            with act_e.Fori(0, groups - POOL_GROUPS) as g:
                matrices(act_e, "dve", g + POOL_GROUPS)
                act_e.wait_ge(solved["dve"], g + 1)
                act_e.dma_start(scr["T"][bass.ds(g + POOL_GROUPS, 1), :, :].rearrange("a p n -> (a p) n"),
                                um["dve"][:, :, :].rearrange("p a b -> p (a b)")).then_inc(mats_out["dve"], 16)
                act_e.wait_ge(mats_out["dve"], (g + 1) * 16)

        @block.tensor
        def _(pe):
            for u in range(2):
                pe.sem_inc(fir_done, 1)
            with pe.Fori(0, D // GC // 2) as i:
                for u in range(2):
                    pe.wait_ge(vst_ready, 2 * i + u + 1)
                    pe.wait_ge(toep_in[u], 16 * (i + 1))
                    pe.wait_ge(fir_read, 2 * i + u + 1)
                    for c in range(GC):
                        ins = pe.matmul(F[u][:, c // 2, (c % 2) * F3 * WIN:(c % 2 + 1) * F3 * WIN], vst[u][:, c, :],
                                        toep[u][:, c * F3:(c + 1) * F3, :], start=True, stop=True)
                    ins.then_inc(fir_done, 1)


def delta_rule(nc, scr, res):
    with ExitStack() as ctx:
        sb, pb, sem = tensors(nc, ctx, "dr")
        GB = 4
        TURNS = BATCH // GB
        X2 = TPS * H
        tT = [sb(f"tT{b}", [P, X2, P]) for b in range(GB)]
        aT = [sb(f"aT{b}", [P, X2, P]) for b in range(GB)]
        kb, vb = ([sb(f"{n}{b}", [P, TPS, D]) for b in range(GB)] for n in ("kb", "vb"))
        kk = [[sb(f"kk{m}{b}", [P, TPS, D]) for b in range(GB)] for m in range(2)]
        qT, wT = ([[sb(f"{n}{m}{b}", [D, SEQ]) for b in range(GB)] for m in range(2)] for n in ("qT", "wT"))
        us = [sb(f"us{m}", [P, GB, TPS, D]) for m in range(2)]
        oo = [sb(f"oo{m}", [P, GB, D]) for m in range(2)]
        S = sb("S", [D, GB, D])
        diag = sb("diag", [D, D])
        PAIRS, PB = 2, GB // 2
        W, SP_ = ([pb(f"{n}{k}", [P, 512]) for k in range(PAIRS)] for n in ("W", "SP"))
        O = [pb(f"O{m}", [P, GB, D]) for m in range(2)]
        UW = [pb(f"UW{m}", [P, TPS, D]) for m in range(2)]
        consts, loads_t, loads_a, zeroed, u_done, u_ready, state_zero = (
            sem(n) for n in ("consts", "loads_t", "loads_a", "zeroed", "u_done", "u_ready", "state_zero"))
        loads_kq = [sem("loads_kq0"), sem("loads_kq1")]
        ws_done, ua_ready, s_done, s_ready, o_done, o_ready = (
            sem(n) for n in ("ws_done", "ua_ready", "s_done", "s_ready", "o_done", "o_ready"))
        stored = [sem("stored0"), sem("stored1")]
        block = ctx.enter_context(nc.Block())
        NS = CPS * PAIRS
        UWS = 2 * GB
        FIRST = 6

        @block.sync
        def _(sp):
            sp.wait_ge(zeroed, 2 * GB)
            with sp.Fori(0, TURNS // 2) as j:
                for m in range(2):
                    g = 2 * j + m
                    one = lambda name, b: scr[name][bass.ds(g * GB + b, 1), :, :].rearrange("a p n -> (a p) n")
                    sp.wait_ge(u_done, UWS * g + UWS)
                    for b in range(GB):
                        for c in range(CPT):
                            r = slice(c * CH, (c + 1) * CH)
                            tsrc = scr["T"][bass.ds(g * (GB // 2) + b // 2, 1), (b % 2) * 64 + c * 16:(b % 2) * 64 + c * 16 + 16, :]
                            sp.dma_start(tT[b][r, :, r], tsrc.rearrange("a x (j i) -> j (a x) i", i=CH)).then_inc(loads_t, 16)
                        for name, dst in (("kb", kb), ("vb", vb)):
                            sp.dma_start(flat(dst[b][:, :, :]), one(name, b)).then_inc(loads_t, 16)
                    for b in range(GB):
                        sp.dma_start(flat(kk[m][b][:, :, :]), one("k", b)).then_inc(loads_kq[m], 16)
                        sp.dma_start(qT[m][b][:, :], one("qT", b)).then_inc(loads_kq[m], 16)
                    sp.wait_ge(o_done, TPS * g + TPS)
                    for b in range(GB):
                        for c in range(CPT):
                            r = slice(c * CH, (c + 1) * CH)
                            sp.dma_start(aT[b][r, :, r], scr["attnT"][bass.ds(g * GB + b, 1), r, :].rearrange("a j (x i) -> (a j) x i", i=CH)).then_inc(loads_a, 16)

        @block.gpsimd
        def _(pool):
            const, clear = Chain(pool, consts), Chain(pool, zeroed)
            for b in range(GB):
                clear(pool.memset(tT[b][:, :, :], 0.0))
                clear(pool.memset(aT[b][:, :, :], 0.0))
            const(pool.memset(diag[:, :], 0.0))
            for h in range(H):
                r = slice(h * DH, (h + 1) * DH)
                const(pool.memset(diag[r, r], 1.0))

        @block.tensor
        def _(pe):
            pe.sem_inc(u_done, UWS)
            pe.sem_inc(o_done, TPS)

            def part(g, n):
                b, w_ = n // 2, n % 2
                pe.wait_ge(u_ready, UWS * g + n + 1)
                for h in range(H):
                    hd = slice(h * DH, (h + 1) * DH)
                    for t in range(TPS):
                        if w_:
                            ins = pe.matmul(UW[1][hd, t, :], kb[b][:, t, hd], tT[b][:, h * TPS + t, :], start=True, stop=True)
                        else:
                            ins = pe.matmul(UW[0][:, t, hd], tT[b][:, h * TPS + t, :], vb[b][:, t, hd], start=True, stop=True)
                ins.then_inc(u_done, 1)

            def chunk(g, m, n):
                t, c = n // CPT, n % CPT
                r = slice(c * CH, (c + 1) * CH)
                cols = slice(n * CH, (n + 1) * CH)
                o = O[t % 2]
                for k in range(PAIRS):
                    if n:
                        pe.wait_ge(s_ready, g * NS + (n - 1) * PAIRS + k + 1)
                    for b in range(PB * k, PB * (k + 1)):
                        ins = pe.matmul(W[k][r, (b % PB) * D:(b % PB + 1) * D], wT[m][b][:, cols], S[:, b, :], start=True, stop=True)
                    ins.then_inc(ws_done, 1)
                if c == 0:
                    pe.wait_ge(o_ready, TPS * g + t + 1)
                for b in range(GB):
                    pe.matmul(o[r, b, :], qT[m][b][:, cols], S[:, b, :], start=(b == 0), stop=False, skip_group_check=True)
                for k in range(PAIRS):
                    pe.wait_ge(ua_ready, g * NS + n * PAIRS + k + 1)
                    for b in range(PB * k, PB * (k + 1)):
                        ins = pe.matmul(SP_[k][:, (b % PB) * D:(b % PB + 1) * D], kk[m][b][r, t, :], us[m][r, b, t, :], start=(n == 0 and b % PB == 0),
                                        stop=False, skip_group_check=True)
                    ins.then_inc(s_done, 1)
                if c == CPT - 1:
                    if t == 0:
                        pe.wait_ge(loads_a, (g + 1) * (16 * GB * CPT))
                    for b in range(GB):
                        for h in range(H):
                            ins = pe.matmul(o[:, b, h * DH:(h + 1) * DH], aT[b][:, h * TPS + t, :], us[m][:, b, t, h * DH:(h + 1) * DH],
                                            start=False, stop=True, skip_group_check=True)
                    ins.then_inc(o_done, 1)

            with pe.Fori(0, TURNS // 2) as j:
                pe.wait_ge(loads_t, (2 * j + 1) * (16 * GB * (CPT + 2)))
                for n in range(UWS):
                    part(2 * j, n)
                for m in range(2):
                    g = 2 * j + m
                    pe.wait_ge(u_ready, UWS * (g + 1) + 2)
                    pe.wait_ge(loads_kq[m], (j + 1) * (16 * GB * 2))
                    pe.wait_ge(state_zero, g + 1)
                    for n in range(CPS):
                        chunk(g, m, n)
                        if m == 0 and FIRST <= n < FIRST + UWS:
                            if n == FIRST:
                                pe.wait_ge(loads_t, (2 * j + 2) * (16 * GB * (CPT + 2)))
                            part(g + 1, n - FIRST)

        @block.vector
        def _(dve):
            dve.wait_ge(consts, 1 + H)
            with dve.Fori(0, TURNS // 2) as j:
                for m in range(2):
                    g = 2 * j + m
                    dve.memset(S[:, :, :], 0.0).then_inc(state_zero, 1)
                    for n in range(CPS):
                        t, c = n // CPT, n % CPT
                        r = slice(c * CH, (c + 1) * CH)
                        two = lambda ap: ap.rearrange("p (b d) -> p b d", b=PB)
                        for k in range(PAIRS):
                            u = us[m][r, PB * k:PB * (k + 1), t, :]
                            dve.wait_ge(ws_done, g * NS + n * PAIRS + k + 1)
                            dve.tensor_tensor(u, u, two(W[k][r, 0:PB * D]), ALU.subtract).then_inc(ua_ready, 1)
                        for k in range(PAIRS):
                            dve.wait_ge(s_done, g * NS + n * PAIRS + k + 1)
                            dve.tensor_tensor(S[:, PB * k:PB * (k + 1), :], two(SP_[k][:, 0:PB * D]), diag[:, :].unsqueeze(1).to_broadcast([D, PB, D]),
                                              ALU.mult).then_inc(s_ready, 1)
                    dve.wait_ge(s_ready, (g + 1) * NS)

        @block.scalar
        def _(act_e):
            act_e.sem_inc(u_ready, 2)
            act_e.sem_inc(o_ready, 2)
            for m in range(2):
                act_e.sem_inc(stored[m], 16 * GB)

            def part(g, m, n):
                b, w_ = n // 2, n % 2
                act_e.wait_ge(u_done, UWS * (g + 1) + n + 1)
                act_e.activation(wT[m][b][:, :] if w_ else flat(us[m][:, b, :, :]), flat(UW[w_][:, :, :]), ACT.Copy).then_inc(u_ready, 1)

            with act_e.Fori(0, TURNS // 2) as j:
                for n in range(UWS):
                    part(2 * j, 0, n)
                for m in range(2):
                    g = 2 * j + m
                    for n in range(CPS):
                        t = n // CPT
                        if n % CPT == CPT - 1:
                            act_e.wait_ge(stored[t % 2], (TPS // 2 * g + t // 2 + 1) * (16 * GB))
                            act_e.wait_ge(o_done, TPS * (g + 1) + t + 1)
                            act_e.activation(flat(oo[t % 2][:, :, :]), flat(O[t % 2][:, :, :]), ACT.Copy).then_inc(o_ready, 1)
                            act_e.wait_ge(o_ready, TPS * g + t + 3)
                            for b in range(GB):
                                act_e.dma_start(scr["o"][bass.ds(g * GB + b, 1), :, t * D:(t + 1) * D].rearrange("a p n -> (a p) n"), oo[t % 2][:, b, :]).then_inc(stored[t % 2], 16)
                        if m == 0 and FIRST <= n < FIRST + UWS:
                            part(g + 1, 1, n - FIRST)
            for m in range(2):
                act_e.wait_ge(stored[m], 16 * GB * (TPS // 2 * TURNS + 1))


def attention_output(nc, w, scr, res):
    U = 4
    with ExitStack() as ctx:
        sb, pb, sem = tensors(nc, ctx, "ao")
        each = lambda name, shape: [sb(f"{name}{u}", shape) for u in range(U)]
        wo, mix, rw = sb("wo", [D, D]), sb("mix", [D, D]), sb("rw", [D, NE])
        cols = sb("cols", [D, 5])
        mix_b = sb("mix_b", [P, D])
        mhalf = sb("mhalf", [P, TPS * H])
        of, dl, vt = ([each(f"{n}{m}", [P, TPS, D]) for m in range(2)] for n in ("of", "dl", "vt"))
        o, t1, sq, h0, h1, c1 = (each(n, [P, TPS, D]) for n in ("o", "t1", "sq", "h0", "h1", "c1"))
        ss, rs = each("ss", [P, TPS * H]), each("rs", [P, TPS * H])
        st, mv, rstd, rstd2 = each("st", [P, TPS, 6]), each("mv", [P, TPS, 2]), each("rstd", [P, TPS]), each("rstd2", [P, TPS])
        xT = each("xT", [D, SEQ])
        tp, pr = ([pb(f"{n}{u}", [P, 512]) for u in range(U)] for n in ("tp", "pr"))
        rp = pr
        consts, loaded, wo_ready, mix_ready, stored, own, pown = (sem(n) for n in ("consts", "loaded", "wo_ready", "mix_ready", "stored", "own", "pown"))
        paths_in = [sem("paths_in0"), sem("paths_in1")]
        paths_used, gated, sum_ready, sq_ready, sums_ready, eps_added, r_ready, rows_ready, tp_done, xT_ready, pr_done, rp_done, x2_ready, x_added, bias_added = (
            sem(n) for n in ("paths_used", "gated", "sum_ready", "sq_ready", "sums_ready", "eps_added", "r_ready", "rows_ready", "tp_done", "xT_ready",
                             "pr_done", "rp_done", "x2_ready", "x_added", "bias_added"))
        pool_waits, dve_waits = sem("pool_waits"), sem("dve_waits")
        block = ctx.enter_context(nc.Block())
        X, PR, ident = res["x"], res["probs"], res["ident"]
        CONST = 16 * 5
        GROUPS = BATCH // U
        PATHS = 16 * 3 * U
        NORMS = 5

        def gate(b, k):
            g = PR[:, bass.ds(b * TPS, TPS), :].rearrange("p t (h g) -> p (t h) g", h=H)[:, :, k:k + 1]
            return g.to_broadcast([P, TPS * H, DH])

        @block.sync
        def _(sp):
            for dst, name in ((wo, "woT"), (mix, "mix_w"), (rw, "router_w"), (cols, "ao_cols")):
                sp.dma_start(dst[:, :], w[name]).then_inc(loaded, 16)
            sp.dma_start(mix_b[:, :], w["mix_b"].partition_broadcast(P)).then_inc(loaded, 16)
            with sp.Fori(0, GROUPS // 2) as j:
                for m in range(2):
                    sp.wait_ge(paths_used, U * (2 * j + m) + U)
                    for u in range(U):
                        bb = bass.ds(U * (2 * j + m) + u, 1)
                        sp.dma_start(of[m][u][:, :, :], scr["ofir"][bb, :, :].rearrange("a (t p) d -> p (a t) d", p=P)).then_inc(paths_in[m], 16)
                        sp.dma_start(flat(dl[m][u][:, :, :]), scr["o"][bb, :, :].rearrange("a p n -> (a p) n")).then_inc(paths_in[m], 16)
                        sp.dma_start(vt[m][u][:, :, :], scr["v"][bb, WIN:WIN + SEQ, :].rearrange("a (t p) d -> p (a t) d", p=P)).then_inc(paths_in[m], 16)

        @block.gpsimd
        def _(pool):
            pool.memset(mhalf[:, :], -0.5).then_inc(consts, 1)
            pool.wait_ge(consts, 1)
            with pool.Fori(0, GROUPS // 2) as j:
                for m in range(2):
                    i = 2 * j + m
                    pool.wait_ge(paths_in[m], PATHS * (j + 1))
                    for u in range(U):
                        pool.wait_ge(sum_ready, nth(i, u, 0, 1, U))
                        pool.tensor_tensor(heads(t1[u][:, :, :]), heads(dl[m][u][:, :, :]), gate(U * i + u, 3), ALU.mult).then_inc(pown, 1)
                        pool.wait_ge(pown, nth(i, u, 0, 1, U))
                        pool.tensor_tensor(t1[u][:, :, :], t1[u][:, :, :], of[m][u][:, :, :], ALU.add).then_inc(gated, 1)
                    for n in range(NORMS):
                        for u in range(U):
                            src, dst, k, scale, eps = (ss[u][:, :], rs[u][:, :], TPS * H, 1.0 / DH, 1e-5) if n == 0 else (mv[u][:, :, 1], rstd[u][:, :], TPS, 1.0, 1e-5)
                            if n == 2:
                                dst, scale, eps = rstd2[u][:, :], 1.0 + 1e-5, 1e-10
                            if n != 3:
                                wait_apart(pool, sums_ready, nth(i, u, n - (n > 3), NORMS - 1, U), pool_waits)
                            pool.tensor_scalar(dst, src, scale, eps, ALU.mult, ALU.add).then_inc(eps_added, 1)
                            pool.wait_ge(eps_added, nth(i, u, n, NORMS, U))
                            pool.tensor_tensor(dst, dst, mhalf[:, 0:k], ALU.pow).then_inc(r_ready, 1)

        @block.vector
        def _(dve):
            dve.wait_ge(loaded, CONST)
            dve.tensor_scalar(wo[:, :], wo[:, :], cols[:, 0:1], None, ALU.mult).then_inc(wo_ready, 1)
            dve.tensor_tensor(mix[:, :], mix[:, :], ident[:, :], ALU.add).then_inc(mix_ready, 1)
            dve.sem_inc(paths_used, 2 * U)
            dve.sem_inc(sum_ready, U)
            dve.sem_inc(stored, 16 * U)
            K = 5 + 3 * U + 2
            with dve.Fori(0, GROUPS // 2) as j:
                for m in range(2):
                    i = 2 * j + m
                    link = Chain(dve, own, i, K, waits=dve_waits)
                    rows_x = lambda u: [one(X[:, bass.ds((U * i + u) * TPS + t, 1), :]) for t in range(TPS)]
                    tiles_ps = lambda p: [p[:, t * D:(t + 1) * D] for t in range(TPS)]

                    def ready(sem_, n, of_, u, give):
                        def f():
                            dve.wait_ge(sem_, nth(i, u, n, of_, U))
                            return give(u)
                        return f

                    dve.wait_ge(paths_in[m], PATHS * (j + 1))
                    for u in range(U):
                        ins = dve.tensor_tensor(heads(o[u][:, :, :]), heads(vt[m][u][:, :, :]), gate(U * i + u, 4), ALU.mult)
                    link(ins)
                    for u in range(U):
                        dve.wait_ge(gated, nth(i, u, 0, 1, U))
                        dve.tensor_tensor(o[u][:, :, :], o[u][:, :, :], t1[u][:, :, :], ALU.add).then_inc(sum_ready, 1)
                    for u in range(U):
                        dve.wait_ge(sq_ready, nth(i, u, 0, 1, U))
                        dve.reduce_sum(ss[u][:, :], heads(sq[u][:, :, :]), axis=AX.X).then_inc(sums_ready, 1)
                    for u in range(U):
                        dve.wait_ge(r_ready, nth(i, u, 0, NORMS, U))
                        dve.tensor_tensor(heads(o[u][:, :, :]), heads(o[u][:, :, :]), over(rs[u][:, :], DH), ALU.mult).then_inc(rows_ready, 1)
                    dve.sem_inc(paths_used, U)
                    pair_stats(dve, link, [ready(pr_done, 0, 2, u, lambda u: tiles_ps(pr[u])) for u in range(U)], st, mv, sums_ready)
                    for u in range(U):
                        dve.wait_ge(r_ready, nth(i, u, 1, NORMS, U))
                        ins = row_norm(dve, tiles_ps(pr[u]), tiles_of(h1[u]), mv[u], rstd[u])
                    link(ins)
                    for u in range(U):
                        xs = X[:, bass.ds((U * i + u) * TPS, TPS), :]
                        ins = dve.tensor_tensor(xs, xs, h1[u][:, :, :], ALU.add)
                    link.apart(ins)
                    pair_stats(dve, link, [lambda u=u: rows_x(u) for u in range(U)], st, mv, sums_ready)
                    dve.wait_ge(stored, 16 * U * (i + 1))
                    for u in range(U):
                        dve.wait_ge(r_ready, nth(i, u, 2, NORMS, U))
                        row_norm(dve, rows_x(u), tiles_of(c1[u]), mv[u], rstd2[u]).then_inc(rows_ready, 1)
                    for u in range(U):
                        dve.wait_ge(r_ready, nth(i, u, 3, NORMS, U))
                        ins = row_norm(dve, rows_x(u), tiles_of(h0[u]), mv[u], rstd[u])
                    link(ins)
                    for u in range(U):
                        ins = dve.tensor_tensor(h1[u][:, :, :], h0[u][:, :, :], mix_b[:, :].unsqueeze(1).to_broadcast([P, TPS, D]), ALU.add)
                    link(ins)
                    for u in range(U):
                        dve.wait_ge(pr_done, nth(i, u, 1, 2, U))
                        x2 = res["x2"][:, bass.ds((U * i + u) * TPS, TPS), :]
                        ins = dve.tensor_tensor(x2, h1[u][:, :, :], pr[u][:, :].rearrange("p (t d) -> p t d", t=TPS), ALU.add)
                    link.apart(ins)
                    rows_2 = lambda u: [one(res["x2"][:, bass.ds((U * i + u) * TPS + t, 1), :]) for t in range(TPS)]
                    pair_stats(dve, link, [lambda u=u: rows_2(u) for u in range(U)], st, mv, sums_ready)
                    for u in range(U):
                        dve.wait_ge(r_ready, nth(i, u, 4, NORMS, U))
                        row_norm(dve, rows_2(u), tiles_of(c1[u]), mv[u], rstd[u]).then_inc(rows_ready, 1)
                    for u in range(U):
                        dve.wait_ge(rp_done, nth(i, u, 0, 1, U))
                        ins = dve.tensor_copy(res["router"][:, bass.ds((U * i + u) * TPS, TPS), :], rp[u][:, 0:TPS * NE].rearrange("p (t e) -> p t e", e=NE))
                    link(ins)
                    link.end()

        @block.scalar
        def _(act_e):
            act_e.wait_ge(loaded, CONST)
            with act_e.Fori(0, GROUPS) as i:
                for u in range(U):
                    act_e.wait_ge(sum_ready, nth(i, u, 0, 1, U) + U)
                    act_e.activation(flat(sq[u][:, :, :]), flat(o[u][:, :, :]), ACT.Square).then_inc(sq_ready, 1)
                for n in range(3):
                    for u in range(U):
                        act_e.wait_ge(tp_done, nth(i, u, n, 3, U))
                        if n == 0:
                            act_e.activation(xT[u][:, :], tp[u][:, :], ACT.Copy).then_inc(xT_ready, 1)
                        else:
                            g = 2 * n - 1
                            act_e.activation(xT[u][:, :], tp[u][:, :], ACT.Identity, bias=cols[:, g + 1:g + 2], scale=cols[:, g:g + 1]).then_inc(xT_ready, 1)
                for u in range(U):
                    act_e.dma_start(scr["c1"][bass.ds(U * i + u, 1), :, :].rearrange("a p n -> (a p) n"), flat(c1[u][:, :, :])).then_inc(stored, 16)
            act_e.wait_ge(stored, 16 * U * (GROUPS + 1))

        @block.tensor
        def _(pe):
            pe.wait_ge(loaded, CONST)
            pe.wait_ge(wo_ready, 1)
            pe.wait_ge(mix_ready, 1)
            with pe.Fori(0, GROUPS) as i:
                for n, (src, rhs, dst) in enumerate(((o, wo, pr), (c1, mix, pr), (c1, rw, rp))):
                    for u in range(U):
                        pe.wait_ge(rows_ready, nth(i, u, n, 3, U))
                        for t in range(TPS):
                            ins = pe.transpose(tp[u][:, t * P:(t + 1) * P], src[u][:, t, :], ident[:, :])
                        ins.then_inc(tp_done, 1)
                    m = NE if n == 2 else D
                    for u in range(U):
                        pe.wait_ge(xT_ready, nth(i, u, n, 3, U))
                        for t in range(TPS):
                            ins = pe.matmul(dst[u][:, t * m:(t + 1) * m], xT[u][:, t * P:(t + 1) * P], rhs[:, :], start=True, stop=True)
                        ins.then_inc(rp_done if n == 2 else pr_done, 1)


ROUND = 1.5 * 2.0 ** 23
TOPK = 2
STEP = 8
NTL = -(-(NT * TOPK + NE - 2) // STEP) * STEP + 1
AHEAD = 2
DEEP = 4
I32 = mybir.dt.int32


def route(nc, w, scr, res):
    with ExitStack() as ctx:
        sb, pb, sem = tensors(nc, ctx, "rt")
        R, E = res["router"], sb("E", [P, NT, NE])
        M = [sb(f"M{k}", [P, NT, NE]) for k in range(TOPK)]
        C, tot, cum, pos = (sb(n, [P, NT, NE]) for n in ("C", "tot", "cum", "pos"))
        m1, sm, i1 = (sb(n, [P, NT]) for n in ("m1", "sm", "i1"))
        ioti = sb("ioti", [P, NTL], I32)
        iot = sb("iot", [P, NTL])
        ones, before = sb("ones", [P, P]), sb("before", [P, P])
        tiles, ends, starts = (sb(n, [P, NE]) for n in ("tiles", "ends", "starts"))
        tile_e = sb("tile_e", [P, NTL])
        slots = sb("slots", [P, TOPK, NT])
        rows = [sb(f"rows{u}", [P, TPS, D]) for u in range(2)]
        sl = [sb(f"sl{u}", [P, TOPK, TPS], I32) for u in range(2)]
        rank_ps, tot_ps = pb("rank_ps", [P, NT, NE]), pb("tot_ps", [P, NT, NE])
        consts, own, sub, exps, counted, ranked, slots_ready = (sem(n) for n in ("consts", "own", "sub", "exps", "counted", "ranked", "slots_ready"))
        rows_in, sent, staged = [sem("rows_in0"), sem("rows_in1")], [sem("sent0"), sem("sent1")], sem("staged")
        freed, pool_waits = sem("freed"), sem("pool_waits")
        block = ctx.enter_context(nc.Block())

        @block.sync
        def _(sp):
            for u in range(2):
                sp.sem_inc(freed, 1)
            with sp.Fori(0, BATCH // 2) as i:
                for u in range(2):
                    sp.wait_ge(freed, 2 * i + u + 1)
                    sp.dma_start(flat(rows[u][:, :, :]), scr["c1"][bass.ds(2 * i + u, 1), :, :].rearrange("a p n -> (a p) n")).then_inc(rows_in[u], 16)

        @block.gpsimd
        def _(pool):
            const = Chain(pool, consts)
            const(pool.memset(ones[:, :], 1.0))
            const(pool.memset(before[:, :], 1.0))
            const(pool.affine_select(out=before[:, :], in_=before[:, :], compare_op=ALU.is_gt, fill=0.0, base=0, pattern=[[1, P]], channel_multiplier=-1))
            const(pool.iota(ioti[:, :], pattern=[[1, NTL]], base=0, channel_multiplier=0))
            pool.wait_ge(slots_ready, 1)
            def send(b, u, m):
                pool.tensor_copy(sl[u][:, :, :], res["slots"][:, :, bass.ds(b * TPS, TPS)]).then_inc(staged, 1)
                pool.wait_ge(staged, b + 1)
                wait_apart(pool, rows_in[u], 16 * (m + 1), pool_waits)
                for k in range(TOPK):
                    for t in range(TPS):
                        pool.indirect_dma_start(out=scr["xs"], out_offset=bass.IndirectOffsetOnAxis(ap=sl[u][:, k, t:t + 1], axis=0),
                                                in_=rows[u][:, t, :], in_offset=None).then_inc(sent[u], 16)

            send(0, 0, 0)
            with pool.Fori(0, BATCH // 2 - 1) as i:
                for s in range(2):
                    send(2 * i + 1 + s, 1 - s, i + s)
                    pool.wait_ge(sent[s], (i + 1) * (16 * TOPK * TPS))
                    pool.sem_inc(freed, 1)
            send(BATCH - 1, 1, BATCH // 2 - 1)
            for u in range(2):
                pool.wait_ge(sent[u], (BATCH // 2) * (16 * TOPK * TPS))

        @block.vector
        def _(dve):
            dve.wait_ge(consts, 4)
            link = Chain(dve, own)
            ov = lambda a: over(a[:, :], NE)
            it = iot[:, 0:NE].unsqueeze(1).to_broadcast([P, NT, NE])
            link(dve.tensor_copy(iot[:, :], ioti[:, :]))
            link(dve.reduce_max(m1[:, :], R[:, :, :], axis=AX.X))
            dve.tensor_tensor(E[:, :, :], R[:, :, :], ov(m1), ALU.subtract).then_inc(sub, 1)
            dve.wait_ge(exps, 1)
            link(dve.reduce_sum(sm[:, :], E[:, :, :], axis=AX.X))
            link(dve.reciprocal(sm[:, :], sm[:, :]))
            link(dve.tensor_tensor(E[:, :, :], E[:, :, :], ov(sm), ALU.mult))

            def first_of(vals, best, mask):
                link(dve.reduce_max(best, vals[:, :, :], axis=AX.X))
                link(dve.tensor_tensor(mask[:, :, :], vals[:, :, :], over(best, NE), ALU.is_lt))
                link(dve.scalar_tensor_tensor(mask[:, :, :], mask[:, :, :], float(NE), it, ALU.mult, ALU.add))
                link(dve.tensor_reduce(i1[:, :], mask[:, :, :], axis=AX.X, op=ALU.min))
                link(dve.tensor_tensor(mask[:, :, :], it, ov(i1), ALU.is_equal))

            first_of(E, res["gate"][:, 0, :], M[0])
            link(dve.scalar_tensor_tensor(R[:, :, :], M[0][:, :, :], -2.0, E[:, :, :], ALU.mult, ALU.add))
            first_of(R, res["gate"][:, 1, :], M[1])
            dve.tensor_tensor(C[:, :, :], M[0][:, :, :], M[1][:, :, :], ALU.add).then_inc(counted, 1)
            dve.wait_ge(ranked, 1)
            link(dve.tensor_copy(tot[:, :, :], tot_ps[:, :, :]))
            for e in range(NE):
                ins = dve.tensor_tensor_scan(cum[:, :, e], ones[:, 0:NT], tot[:, :, e], 0.0, ALU.mult, ALU.add)
            link(ins)
            link(dve.tensor_scalar(tiles[:, :], cum[:, NT - 1, :], 1.0 / P, (P - 1.0) / (2 * P), ALU.mult, ALU.add))
            link(dve.tensor_scalar(tiles[:, :], tiles[:, :], ROUND, -ROUND, ALU.add, ALU.add))
            link(dve.tensor_tensor_scan(ends[:, :], ones[:, 0:NE], tiles[:, :], 0.0, ALU.mult, ALU.add))
            link(dve.tensor_tensor(starts[:, :], ends[:, :], tiles[:, :], ALU.subtract))
            link(dve.tensor_scalar(starts[:, :], starts[:, :], float(P), None, ALU.mult))
            link(dve.tensor_tensor(pos[:, :, :], cum[:, :, :], tot[:, :, :], ALU.subtract))
            link(dve.tensor_tensor(pos[:, :, :], pos[:, :, :], rank_ps[:, :, :], ALU.add))
            link(dve.tensor_tensor(pos[:, :, :], pos[:, :, :], starts[:, :].unsqueeze(1).to_broadcast([P, NT, NE]), ALU.add))
            for k in range(TOPK):
                link(dve.tensor_tensor(M[k][:, :, :], M[k][:, :, :], pos[:, :, :], ALU.mult))
                link(dve.reduce_sum(slots[:, k, :], M[k][:, :, :], axis=AX.X))
            dve.tensor_copy(res["slots"][:, :, :], slots[:, :, :]).then_inc(slots_ready, 1)
            link(dve.memset(tile_e[:, :], 0.0))
            for e in range(NE):
                link(dve.scalar_tensor_tensor(tile_e[:, :], iot[:, :], ends[:, e:e + 1], tile_e[:, :], ALU.is_ge, ALU.add))
            link(dve.tensor_scalar(tile_e[:, :], tile_e[:, :], NE - 1.0, None, ALU.min))
            link(dve.tensor_copy(res["tile_e"][:, :], tile_e[:, :]))

        @block.scalar
        def _(act_e):
            act_e.wait_ge(sub, 1)
            act_e.activation(E[:, :, :], E[:, :, :], ACT.Exp).then_inc(exps, 1)

        @block.tensor
        def _(pe):
            pe.wait_ge(counted, 1)
            pe.matmul(rank_ps[:, :, :], before[:, :], C[:, :, :], start=True, stop=True)
            pe.matmul(tot_ps[:, :, :], ones[:, :], C[:, :, :], start=True, stop=True).then_inc(ranked, 1)


def experts(nc, w, scr, res):
    with ExitStack() as ctx:
        sb, pb, sem = tensors(nc, ctx, "ex")
        w1 = sb("w1", [D, NE, FF])
        w2 = sb("w2", [P, NE, FC * D])
        b1, b2 = sb("b1", [P, NE, FF]), sb("b2", [P, NE, D])
        cols = sb("cols", [D, 5])
        xin = [sb(f"xin{u}", [P, D]) for u in range(DEEP)]
        xT = [sb(f"xT{u}", [D, P]) for u in range(2)]
        hid = [sb(f"hid{u}", [P, FF]) for u in range(2)]
        hT = [sb(f"hT{u}", [P, FF]) for u in range(2)]
        ys = [sb(f"ys{u}", [P, D]) for u in range(2)]
        x_ps, h_ps, t_ps, y_ps = ([pb(f"{n}{u}", [P, 512]) for u in range(2)] for n in ("xp", "hp", "tp", "yp"))
        loaded, xt_done, xT_ready, h_done, hid_ready, ht_done, hT_ready, y_done, ys_ready = (
            sem(n) for n in ("loaded", "xt_done", "xT_ready", "h_done", "hid_ready", "ht_done", "hT_ready", "y_done", "ys_ready"))
        rows_in, out_done = [sem(f"rows_in{u}") for u in range(DEEP)], [sem("out_done0"), sem("out_done1")]
        block = ctx.enter_context(nc.Block())
        ident, tile_e = res["ident"], res["tile_e"]
        xs, yr = (scr[n].rearrange("(i p) d -> i p d", p=P) for n in ("xs", "ys"))
        last = NTL - 1

        @block.sync
        def _(sp):
            def load(j, u):
                if not isinstance(j, int) or j >= DEEP:
                    sp.wait_ge(xt_done, j - DEEP + 3)
                sp.dma_start(xin[u][:, :], xs[bass.ds(j, 1), :, :].rearrange("a p d -> (a p) d")).then_inc(rows_in[u], 16)

            for dst, name in ((b1, "b1"), (b2, "b2")):
                sp.dma_start(dst[:, :, :], w[name].partition_broadcast(P)).then_inc(loaded, 16)
            sp.dma_start(w1[:, :, :], w["w1"].rearrange("e d f -> d e f")).then_inc(loaded, 16)
            sp.dma_start(cols[:, :], w["ao_cols"]).then_inc(loaded, 16)
            sp.dma_start(w2[:, :, :].rearrange("p e (c d) -> p e c d", c=FC), w["w2"].rearrange("e (c f) d -> f e c d", f=P)).then_inc(loaded, 16)
            for j in range(1 + DEEP):
                load(j, j % DEEP)
            with sp.Fori(0, last // STEP) as n:
                for s in range(STEP):
                    i = STEP * n + 1 + s
                    load(i + DEEP, (1 + s) % DEEP)
                    sp.wait_ge(ys_ready, i)
                    sp.dma_start(yr[bass.ds(i - 1, 1), :, :].rearrange("a p d -> (a p) d"), ys[s % 2][:, :]).then_inc(out_done[s % 2], 16)
            sp.wait_ge(ys_ready, NTL)
            sp.dma_start(yr[last], ys[last % 2][:, :]).then_inc(out_done[last % 2], 16)
            sp.wait_ge(out_done[0], 16 * (last // 2 + 2))
            sp.wait_ge(out_done[1], 16 * (last // 2 + 1))

        def expert_of(eng, i):
            return eng.value_load(tile_e[0:1, bass.ds(i, 1)], min_val=0, max_val=NE - 1)

        @block.vector
        def _(dve):
            dve.wait_ge(loaded, 80)
            def bias_up(i, u, e):
                dve.wait_ge(h_done, i + 1)
                dve.tensor_tensor(hid[u][:, :], h_ps[u][:, :], b1[:, bass.ds(e, 1), :].rearrange("p a f -> p (a f)"), ALU.add).then_inc(hid_ready, 1)

            def bias_down(i, u, e, m):
                dve.wait_ge(y_done, i + 3)
                dve.wait_ge(out_done[u], 16 * (m + 1))
                dve.tensor_tensor(ys[u][:, :], y_ps[u][:, 0:D], b2[:, bass.ds(e, 1), :].rearrange("p a d -> p (a d)"), ALU.add).then_inc(ys_ready, 1)

            for u in range(2):
                dve.sem_inc(out_done[u], 16)
            bias_up(0, 0, expert_of(dve, 0))
            with dve.Fori(0, last // STEP) as n:
                before = expert_of(dve, STEP * n)
                for s in range(STEP):
                    i = STEP * n + 1 + s
                    e = expert_of(dve, i)
                    bias_up(i, (1 + s) % 2, e)
                    bias_down(i - 1, s % 2, before, STEP // 2 * n + s // 2)
                    before = e
            bias_down(last, last % 2, expert_of(dve, last), last // 2)

        @block.scalar
        def _(act_e):
            act_e.wait_ge(loaded, 80)

            def affine(j, u):
                act_e.wait_ge(xt_done, j + 3)
                act_e.activation(xT[u][:, :], x_ps[u][:, 0:P], ACT.Identity, bias=cols[:, 4:5], scale=cols[:, 3:4]).then_inc(xT_ready, 1)

            def silu(i, u):
                act_e.wait_ge(ht_done, i + 1)
                act_e.wait_ge(y_done, i + 1)
                act_e.activation(hT[u][:, :], t_ps[u][:, :], ACT.Silu).then_inc(hT_ready, 1)

            for j in range(AHEAD):
                affine(j, j % 2)
            silu(0, 0)
            affine(AHEAD, AHEAD % 2)
            with act_e.Fori(0, last // STEP) as n:
                for s in range(STEP):
                    i = STEP * n + 1 + s
                    silu(i, (1 + s) % 2)
                    affine(i + AHEAD, (1 + s) % 2)

        @block.tensor
        def _(pe):
            pe.wait_ge(loaded, 80)
            for u in range(2):
                pe.sem_inc(xt_done, 1)
                pe.sem_inc(y_done, 1)

            def turn_rows(j, u, v, m):
                pe.wait_ge(rows_in[v], 16 * (m + 1))
                pe.transpose(x_ps[u][:, 0:P], xin[v][:, :], ident[:, :]).then_inc(xt_done, 1)

            def up(i, u, e):
                pe.wait_ge(xT_ready, i + 1)
                pe.matmul(h_ps[u][:, :], xT[u][:, :], w1[:, bass.ds(e, 1), :].rearrange("p a f -> p (a f)"), start=True, stop=True).then_inc(h_done, 1)

            def turn_hidden(i, u):
                pe.wait_ge(hid_ready, i + 1)
                for f in range(FC):
                    ins = pe.transpose(t_ps[u][:, f * P:(f + 1) * P], hid[u][:, f * P:(f + 1) * P], ident[:, :])
                ins.then_inc(ht_done, 1)

            def down(i, u, e):
                pe.wait_ge(hT_ready, i + 1)
                for f in range(FC):
                    w2f = w2[:, bass.ds(e, 1), f * D:(f + 1) * D].rearrange("p a d -> p (a d)")
                    ins = pe.matmul(y_ps[u][:, 0:D], hT[u][:, f * P:(f + 1) * P], w2f, start=(f == 0), stop=(f == FC - 1))
                ins.then_inc(y_done, 1)

            for j in range(AHEAD):
                turn_rows(j, j % 2, j % DEEP, j // DEEP)
            up(0, 0, expert_of(pe, 0))
            turn_hidden(0, 0)
            turn_rows(AHEAD, AHEAD % 2, AHEAD % DEEP, AHEAD // DEEP)
            with pe.Fori(0, last // STEP) as n:
                before, e = expert_of(pe, STEP * n), expert_of(pe, STEP * n + 1)
                for s in range(STEP):
                    i = STEP * n + 1 + s
                    u = (1 + s) % 2
                    up(i, u, e)
                    after = expert_of(pe, i + 1) if s < STEP - 1 else None
                    down(i - 1, s % 2, before)
                    turn_rows(i + AHEAD, u, (1 + s + AHEAD) % DEEP, STEP // DEEP * n + (1 + s + AHEAD) // DEEP)
                    turn_hidden(i, u)
                    before, e = e, after
            down(last, last % 2, expert_of(pe, last))


def gate_loop(nc, w, scr, res):
    with ExitStack() as ctx:
        sb, pb, sem = tensors(nc, ctx, "gl")
        two = lambda name, shape, dt=FP32: [sb(f"{name}{u}", shape, dt) for u in range(2)]
        names = ("wq", "wk", "wv", "wa", "wg", "wo")
        W = {n: sb(n, [D, D]) for n in names}
        gamma = sb("gamma", [D, 1])
        mhalf = sb("mhalf", [P, TPS])
        st, mv, rstd = two("st", [P, TPS, 6]), two("mv", [P, TPS, 2]), two("rstd", [P, TPS])
        f, h, o = (two(n, [P, TPS, D]) for n in ("f", "h", "o"))
        xT, k, a, sg, y = (two(n, [D, SEQ]) for n in ("xT", "k", "a", "sg", "y"))
        yk = [two(f"yk{m}", [P, TOPK, TPS, D]) for m in range(2)]
        sl = [two(f"sl{m}", [P, TOPK, TPS], I32) for m in range(2)]
        xq, kg, ao, vv = ([pb(f"{n}{u}", [P, SEQ]) for u in range(2)] for n in ("xq", "kg", "ao", "vv"))
        loaded, consts, own, sums_ready, eps_added, r_ready, h_ready, tp_done, xT_ready, proj_done, k_ready, a_ready, sg_ready, y_ready, o_done, g_ready = (
            sem(n) for n in ("loaded", "consts", "own", "sums_ready", "eps_added", "r_ready", "h_ready", "tp_done", "xT_ready", "proj_done", "k_ready",
                             "a_ready", "sg_ready", "y_ready", "o_done", "g_ready"))
        pool_waits, dve_waits = sem("pool_waits"), sem("dve_waits")
        rows_in = [[sem(f"rows_in{m}{u}") for u in range(2)] for m in range(2)]
        rows_used, staged = sem("rows_used"), sem("staged")
        block = ctx.enter_context(nc.Block())
        X, ident = res["x"], res["ident"]
        PAIRS = BATCH // 2
        NORMS, PROJ = 3, 5
        SCALES = ((1.0, 1e-5), (D + 1e-5, 1e-10), (1.0, 1e-5))

        @block.sync
        def _(sp):
            for n in names:
                sp.dma_start(W[n][:, :], w[f"gl_{n}"]).then_inc(loaded, 16)
            sp.dma_start(gamma[:, :], w["gamma"]).then_inc(loaded, 16)

        @block.gpsimd
        def _(pool):
            pool.memset(mhalf[:, :], -0.5).then_inc(consts, 1)
            pool.wait_ge(consts, 1)

            def stage(i, m):
                pool.wait_ge(rows_used, 2 * i + 2)
                for u in range(2):
                    pool.tensor_copy(sl[m][u][:, :, :], res["slots"][:, :, bass.ds((2 * i + u) * TPS, TPS)]).then_inc(staged, 1)
                wait_apart(pool, staged, 2 * i + 2, pool_waits)

            def gather(m, part, parts):
                every = [(u, n, t) for u in range(2) for n in range(TOPK) for t in range(TPS)]
                for u, n, t in every[len(every) * part // parts:len(every) * (part + 1) // parts]:
                    pool.indirect_dma_start(out=yk[m][u][:, n, t, :], out_offset=None, in_=scr["ys"],
                                            in_offset=bass.IndirectOffsetOnAxis(ap=sl[m][u][:, n, t:t + 1], axis=0)).then_inc(rows_in[m][u], 16)

            def powers(i, n):
                for u in range(2):
                    wait_apart(pool, sums_ready, nth(i, u, n, NORMS), pool_waits)
                    pool.tensor_scalar(rstd[u][:, :], mv[u][:, :, 1], *SCALES[n], ALU.mult, ALU.add).then_inc(eps_added, 1)
                    pool.wait_ge(eps_added, nth(i, u, n, NORMS))
                    pool.tensor_tensor(rstd[u][:, :], rstd[u][:, :], mhalf[:, :], ALU.pow).then_inc(r_ready, 1)

            def pair(i, m, more):
                powers(i, 0)
                if more:
                    stage(i + 1, 1 - m)
                    gather(1 - m, 0, 4)
                powers(i, 1)
                if more:
                    for part in range(1, 4):
                        gather(1 - m, part, 4)
                powers(i, 2)

            stage(0, 0)
            gather(0, 0, 1)
            with pool.Fori(0, PAIRS // 2 - 1) as j:
                for m in range(2):
                    pair(2 * j + m, m, True)
            pair(PAIRS - 2, 0, True)
            pair(PAIRS - 1, 1, False)

        @block.vector
        def _(dve):
            dve.wait_ge(loaded, 16 * 7)
            dve.tensor_scalar(gamma[:, :], gamma[:, :], float(D) ** 0.5, None, ALU.mult).then_inc(g_ready, 1)
            dve.sem_inc(rows_used, 4)
            K = 15
            with dve.Fori(0, PAIRS // 2) as j:
                for m in range(2):
                    i = 2 * j + m
                    link = Chain(dve, own, i, K, waits=dve_waits)
                    rows = lambda r, u: [one(r[:, bass.ds((2 * i + u) * TPS + t, 1), :]) for t in range(TPS)]
                    for n in range(TOPK):
                        for u in range(2):
                            if n == 0:
                                dve.wait_ge(rows_in[m][u], (j + 1) * (16 * TOPK * TPS))
                            left = rows(res["x2"], u) if n == 0 else tiles_of(f[u])
                            for t in range(TPS):
                                ins = dve.scalar_tensor_tensor(f[u][:, t, :], yk[m][u][:, n, t, :],
                                                               res["gate"][:, n, bass.ds((2 * i + u) * TPS + t, 1)], left[t], ALU.mult, ALU.add)
                        link(ins)
                    dve.sem_inc(rows_used, 2)
                    pair_stats(dve, link, [lambda: tiles_of(f[0]), lambda: tiles_of(f[1])], st, mv, sums_ready)
                    for u in range(2):
                        dve.wait_ge(r_ready, nth(i, u, 0, NORMS))
                        ins = row_norm(dve, tiles_of(f[u]), tiles_of(f[u]), mv[u], rstd[u])
                    link(ins)
                    for u in range(2):
                        xs = X[:, bass.ds((2 * i + u) * TPS, TPS), :]
                        ins = dve.tensor_tensor(xs, xs, f[u][:, :, :], ALU.add)
                    link.apart(ins)
                    pair_stats(dve, link, [lambda: rows(X, 0), lambda: rows(X, 1)], st, mv, sums_ready)
                    for u in range(2):
                        dve.wait_ge(r_ready, nth(i, u, 1, NORMS))
                        row_norm(dve, rows(X, u), tiles_of(h[u]), mv[u], rstd[u]).then_inc(h_ready, 1)
                    for u in range(2):
                        dve.wait_ge(k_ready, nth(i, u, 0, 1))
                        dve.wait_ge(proj_done, nth(i, u, 2, PROJ))
                        ins = dve.tensor_tensor(k[u][:, :], k[u][:, :], vv[u][:, :], ALU.mult)
                    link(ins)
                    for u in range(2):
                        dve.wait_ge(a_ready, nth(i, u, 0, 1))
                        ins = dve.tensor_tensor_scan(y[u][:, :], a[u][:, :], k[u][:, :], 0.0, ALU.mult, ALU.add)
                    link(ins)
                    for u in range(2):
                        dve.wait_ge(proj_done, nth(i, u, 3, PROJ))
                        ins = dve.tensor_tensor(y[u][:, :], y[u][:, :], xq[u][:, :], ALU.mult)
                    link(ins)
                    for u in range(2):
                        dve.wait_ge(sg_ready, nth(i, u, 0, 1))
                        dve.tensor_tensor(y[u][:, :], y[u][:, :], sg[u][:, :], ALU.mult).then_inc(y_ready, 1)

                    def projected(u):
                        def rows_of_output():
                            dve.wait_ge(o_done, nth(i, u, 0, 1))
                            return [ao[u][:, t * D:(t + 1) * D] for t in range(TPS)]
                        return rows_of_output

                    pair_stats(dve, link, [projected(0), projected(1)], st, mv, sums_ready)
                    for u in range(2):
                        dve.wait_ge(r_ready, nth(i, u, 2, NORMS))
                        ins = row_norm(dve, [ao[u][:, t * D:(t + 1) * D] for t in range(TPS)], tiles_of(o[u]), mv[u], rstd[u])
                    link(ins)
                    for u in range(2):
                        xs = X[:, bass.ds((2 * i + u) * TPS, TPS), :]
                        ins = dve.tensor_tensor(xs, xs, o[u][:, :, :], ALU.add)
                    ins.then_inc(own, 1)
                    link.n += 1
                    link.end()
            dve.wait_ge(own, K * PAIRS)

        @block.scalar
        def _(act_e):
            act_e.wait_ge(g_ready, 1)
            with act_e.Fori(0, PAIRS) as i:
                for u in range(2):
                    act_e.wait_ge(tp_done, nth(i, u, 0, 1))
                    act_e.activation(xT[u][:, :], xq[u][:, :], ACT.Copy, scale=gamma[:, 0:1]).then_inc(xT_ready, 1)
                for n, dst, src, func, ready in ((0, k, kg, ACT.Copy, k_ready), (1, a, ao, ACT.Sigmoid, a_ready), (4, sg, kg, ACT.Silu, sg_ready)):
                    for u in range(2):
                        act_e.wait_ge(proj_done, nth(i, u, n, PROJ))
                        act_e.activation(dst[u][:, :], src[u][:, :], func).then_inc(ready, 1)

        @block.tensor
        def _(pe):
            pe.wait_ge(loaded, 16 * 7)
            with pe.Fori(0, PAIRS) as i:
                for u in range(2):
                    pe.wait_ge(h_ready, nth(i, u, 0, 1))
                    for t in range(TPS):
                        ins = pe.transpose(xq[u][:, t * P:(t + 1) * P], h[u][:, t, :], ident[:, :])
                    ins.then_inc(tp_done, 1)
                for n, (name, dst) in enumerate((("wk", kg), ("wa", ao), ("wv", vv), ("wq", xq), ("wg", kg))):
                    for u in range(2):
                        if n == 0:
                            pe.wait_ge(xT_ready, nth(i, u, 0, 1))
                        if n == PROJ - 1:
                            pe.wait_ge(k_ready, nth(i, u, 0, 1))
                        pe.matmul(dst[u][:, :], W[name][:, :], xT[u][:, :], start=True, stop=True).then_inc(proj_done, 1)
                for u in range(2):
                    pe.wait_ge(y_ready, nth(i, u, 0, 1))
                    for t in range(TPS):
                        ins = pe.matmul(ao[u][:, t * D:(t + 1) * D], y[u][:, t * P:(t + 1) * P], W["wo"][:, :], start=True, stop=True)
                    ins.then_inc(o_done, 1)


def phase_ffn(nc, w, res, out):
    TWO_PI = 6.283185307179586
    ROUND = 1.5 * 2.0 ** 23
    HI = 6.28125
    MID = 0.0019350051879882812
    LO = TWO_PI - HI - MID
    U = 4
    with ExitStack() as ctx:
        sb, pb, sem = tensors(nc, ctx, "pf")
        w1, w2 = sb("w1", [D, FF]), sb("w2", [P, FC, D])
        cf = sb("cf", [P, 4, FC])
        b2 = sb("b2", [P, D])
        th, nn, sn, cs, c = (sb(n, [P, FC]) for n in ("th", "nn", "sn", "cs", "c"))
        mhalf = sb("mhalf", [P, TPS])
        each = lambda name, shape: [sb(f"{name}{u}", shape) for u in range(U)]
        st, mv, rstd = each("st", [P, TPS, 6]), each("mv", [P, TPS, 2]), each("rstd", [P, TPS])
        h, o = each("h", [P, TPS, D]), each("o", [P, TPS, D])
        xT = each("xT", [D, SEQ])
        hid, turn, near = ([each(f"{n}{f}", [P, SEQ]) for f in range(FC)] for n in ("hid", "turn", "near"))
        bank = [[pb(f"bank{m}{u}", [P, SEQ]) for u in range(U)] for m in range(2)]
        tp = op = bank[0]
        loaded, consts, coef, trig, done, halfpi, own, sums_ready, eps_added, r_ready, h_ready, tp_done, xT_ready = (
            sem(n) for n in ("loaded", "consts", "coef", "trig", "done", "halfpi", "own", "sums_ready", "eps_added", "r_ready", "h_ready", "tp_done", "xT_ready"))
        hp_done, hid_ready, near_ready, frac, sine_ready, sum_ready, relu_ready, o_done, o_ready, x_ready, out_done = (
            sem(n) for n in ("hp_done", "hid_ready", "near_ready", "frac", "sine_ready", "sum_ready", "relu_ready", "o_done", "o_ready", "x_ready", "out_done"))
        pool_waits, dve_waits = sem("pool_waits"), sem("dve_waits")
        block = ctx.enter_context(nc.Block())
        X, ident = res["x"], res["ident"]
        GROUPS = BATCH // U

        @block.sync
        def _(sp):
            sp.dma_start(w1[:, :], w["pf_w1"]).then_inc(loaded, 16)
            sp.dma_start(w2[:, :, :], w["pf_w2"].rearrange("(c f) d -> f c d", f=P)).then_inc(loaded, 16)
            sp.dma_start(cf[:, :, :], w["pf_cols"]).then_inc(loaded, 16)
            sp.dma_start(b2[:, :], w["pf_b2"].partition_broadcast(P)).then_inc(loaded, 16)
            with sp.Fori(0, BATCH) as b:
                sp.wait_ge(x_ready, b + (U + 1))
                sp.dma_start(out[bass.ds(b, 1), :, :].rearrange("a (t p) d -> p (a t) d", p=P), X[:, bass.ds(b * TPS, TPS), :]).then_inc(out_done, 16)
            sp.wait_ge(out_done, 16 * BATCH)

        @block.gpsimd
        def _(pool):
            pool.memset(mhalf[:, :], -0.5).then_inc(consts, 1)
            pool.wait_ge(consts, 1)
            pool.sem_inc(x_ready, U)

            def powers(i, n):
                for u in range(U):
                    wait_apart(pool, sums_ready, nth(i, u, n, 2, U), pool_waits)
                    pool.tensor_scalar(rstd[u][:, :], mv[u][:, :, 1], 1e-5, None, ALU.add).then_inc(eps_added, 1)
                    pool.wait_ge(eps_added, nth(i, u, n, 2, U))
                    pool.tensor_tensor(rstd[u][:, :], rstd[u][:, :], mhalf[:, :], ALU.pow).then_inc(r_ready, 1)

            with pool.Fori(0, GROUPS) as i:
                powers(i, 0)
                for f in range(FC):
                    for u in range(U):
                        pool.wait_ge(near_ready, nth(i, u, f, FC, U))
                        pool.tensor_tensor(turn[f][u][:, :], turn[f][u][:, :], near[f][u][:, :], ALU.subtract).then_inc(frac, 1)
                powers(i, 1)
                for u in range(U):
                    xs = X[:, bass.ds((U * i + u) * TPS, TPS), :]
                    pool.wait_ge(o_ready, nth(i, u, 0, 1, U))
                    pool.tensor_tensor(xs, xs, o[u][:, :, :], ALU.add).then_inc(x_ready, 1)

        @block.vector
        def _(dve):
            dve.wait_ge(loaded, 64)
            start = Chain(dve, coef, 0, 16)
            b1, phase, real, imag = (cf[:, n, :] for n in range(4))

            def wrap(dst, src):
                start(dve.tensor_scalar(nn[:, :], src, 1.0 / TWO_PI, ROUND, ALU.mult, ALU.add))
                start(dve.tensor_scalar(nn[:, :], nn[:, :], -ROUND, None, ALU.add))
                start(dve.scalar_tensor_tensor(dst, nn[:, :], -HI, src, ALU.mult, ALU.add))
                start(dve.scalar_tensor_tensor(dst, nn[:, :], -MID, dst, ALU.mult, ALU.add))
                start(dve.scalar_tensor_tensor(dst, nn[:, :], -LO, dst, ALU.mult, ALU.add))
                start(dve.tensor_scalar(dst, dst, -3.141592, 3.141592, ALU.max, ALU.min))

            wrap(th[:, :], phase)
            start(dve.tensor_scalar(cs[:, :], th[:, :], TWO_PI / 4, None, ALU.add))
            wrap(cs[:, :], cs[:, :])
            dve.tensor_scalar(nn[:, :], nn[:, :], 0.0, None, ALU.mult).then_inc(halfpi, 1)
            dve.wait_ge(trig, 2)
            start(dve.tensor_tensor(cs[:, :], cs[:, :], real, ALU.mult))
            start(dve.tensor_tensor(sn[:, :], sn[:, :], imag, ALU.mult))
            start(dve.tensor_tensor(c[:, :], cs[:, :], sn[:, :], ALU.add))
            dve.scalar_tensor_tensor(c[:, :], c[:, :], 0.1, imag, ALU.mult, ALU.mult).then_inc(done, 1)
            dve.tensor_scalar(th[:, :], th[:, :], 1.0 / TWO_PI, None, ALU.mult).then_inc(done, 1)
            dve.wait_ge(done, 2)
            start.end()
            K = 3 * U + FC
            with dve.Fori(0, GROUPS) as i:
                link = Chain(dve, own, i, K, waits=dve_waits)
                rows = lambda u: [one(X[:, bass.ds((U * i + u) * TPS + t, 1), :]) for t in range(TPS)]
                pair_stats(dve, link, [lambda u=u: rows(u) for u in range(U)], st, mv, sums_ready)
                for u in range(U):
                    dve.wait_ge(r_ready, nth(i, u, 0, 2, U))
                    row_norm(dve, rows(u), tiles_of(h[u]), mv[u], rstd[u]).then_inc(h_ready, 1)
                for f in range(FC):
                    for u in range(U):
                        dve.wait_ge(hid_ready, nth(i, u, f, FC, U))
                        ins = dve.tensor_scalar(turn[f][u][:, :], hid[f][u][:, :], 0.1 / TWO_PI, th[:, f:f + 1], ALU.mult, ALU.add)
                    link(ins)
                    for u in range(U):
                        dve.tensor_scalar(near[f][u][:, :], turn[f][u][:, :], ROUND, -ROUND, ALU.add, ALU.add).then_inc(near_ready, 1)
                for f in range(FC):
                    for u in range(U):
                        dve.wait_ge(sine_ready, nth(i, u, f, FC, U))
                        dve.scalar_tensor_tensor(hid[f][u][:, :], turn[f][u][:, :], c[:, f:f + 1], hid[f][u][:, :], ALU.mult, ALU.add).then_inc(sum_ready, 1)
                dve.wait_ge(x_ready, U * i + U)
                for u in range(U):
                    dve.wait_ge(o_done, nth(i, u, 0, 1, U))
                    link(dve.tensor_tensor(o[u][:, :, :], op[u][:, :].rearrange("p (t d) -> p t d", d=D), b2[:, :].unsqueeze(1).to_broadcast([P, TPS, D]), ALU.add))
                pair_stats(dve, link, [lambda u=u: tiles_of(o[u]) for u in range(U)], st, mv, sums_ready)
                for u in range(U):
                    dve.wait_ge(r_ready, nth(i, u, 1, 2, U))
                    row_norm(dve, tiles_of(o[u]), tiles_of(o[u]), mv[u], rstd[u]).then_inc(o_ready, 1)
                link.end()

        @block.scalar
        def _(act_e):
            act_e.wait_ge(halfpi, 1)
            act_e.activation(sn[:, :], th[:, :], ACT.Sin).then_inc(trig, 1)
            act_e.activation(cs[:, :], cs[:, :], ACT.Sin).then_inc(trig, 1)
            with act_e.Fori(0, GROUPS) as i:
                for u in range(U):
                    act_e.wait_ge(tp_done, nth(i, u, 0, 1, U))
                    act_e.activation(xT[u][:, :], tp[u][:, :], ACT.Copy).then_inc(xT_ready, 1)
                for f in range(FC):
                    for u in range(U):
                        act_e.wait_ge(hp_done, nth(i, u, f, FC, U))
                        act_e.activation(hid[f][u][:, :], bank[(f + 1) % 2][u][:, :], ACT.Identity, bias=cf[:, 0, f:f + 1]).then_inc(hid_ready, 1)
                steps = [(f, u) for f in range(FC) for u in range(U)]
                LAG = 3
                for n in range(len(steps) + LAG):
                    if n < len(steps):
                        f, u = steps[n]
                        act_e.wait_ge(frac, nth(i, u, f, FC, U))
                        act_e.activation(turn[f][u][:, :], turn[f][u][:, :], ACT.Sin, scale=6.283185).then_inc(sine_ready, 1)
                    if n >= LAG:
                        f, u = steps[n - LAG]
                        act_e.wait_ge(sum_ready, nth(i, u, f, FC, U))
                        act_e.activation(hid[f][u][:, :], hid[f][u][:, :], ACT.Relu).then_inc(relu_ready, 1)

        @block.tensor
        def _(pe):
            pe.wait_ge(loaded, 64)
            with pe.Fori(0, GROUPS) as i:
                for u in range(U):
                    pe.wait_ge(h_ready, nth(i, u, 0, 1, U))
                    for t in range(TPS):
                        ins = pe.transpose(tp[u][:, t * P:(t + 1) * P], h[u][:, t, :], ident[:, :])
                    ins.then_inc(tp_done, 1)
                for f in range(FC):
                    for u in range(U):
                        if f == 0:
                            pe.wait_ge(xT_ready, nth(i, u, 0, 1, U))
                        if f >= 2:
                            pe.wait_ge(hid_ready, nth(i, u, f - 2, FC, U))
                        pe.matmul(bank[(f + 1) % 2][u][:, :], w1[:, f * P:(f + 1) * P], xT[u][:, :], start=True, stop=True).then_inc(hp_done, 1)
                for u in range(U):
                    pe.wait_ge(relu_ready, nth(i, u, FC - 1, FC, U))
                    for t in range(TPS):
                        for f in range(FC):
                            ins = pe.matmul(op[u][:, t * D:(t + 1) * D], hid[f][u][:, t * P:(t + 1) * P], w2[:, f, :], start=(f == 0), stop=(f == FC - 1))
                    ins.then_inc(o_done, 1)


def build(nc, w, out):
    scr = {name: nc.dram_tensor(f"scratch_{name}", shape, FP32, kind="Internal").ap() for name, shape in (
        ("v", (BATCH, WIN + SEQ, D)), ("k", (BATCH, P, SEQ)), ("kb", (BATCH, P, SEQ)), ("vb", (BATCH, P, SEQ)), ("qT", (BATCH, D, SEQ)),
        ("A", (BATCH, P, SEQ)), ("attnT", (BATCH, P, SEQ)), ("T", (BATCH // 2, P, CH * CH)), ("probs", (BATCH * SEQ, H * NGATE)),
        ("ofir", (BATCH, SEQ, D)), ("o", (BATCH, P, SEQ)), ("c1", (BATCH, P, SEQ)),
        ("xs", ((NTL + DEEP) * P, D)), ("ys", (NTL * P, D)))}
    with ExitStack() as ctx:
        def sb(name, shape):
            return ctx.enter_context(nc.sbuf_tensor(name, shape, FP32))

        res = {"x": sb("x_rows", [P, NT, D]), "ident": sb("ident", [P, P])}
        with ExitStack() as mid:
            for name, shape in (("probs", [P, NT, H * NGATE]), ("eps", [P, H]), ("inv_temp", [P, H]), ("rq", [P, NT, H])):
                res[name] = mid.enter_context(nc.sbuf_tensor(name, shape, FP32))
            with nc.sbuf_tensor("logits", [P, NT, H * NGATE], FP32) as res["logits"]:
                delta_inputs(nc, w["x"], w, scr, res)
                fir_and_inverses(nc, w, scr, res)
            delta_rule(nc, scr, res)
            with ExitStack() as ffn:
                for name, shape, dt in (("x2", [P, NT, D], FP32), ("router", [P, NT, NE], FP32), ("gate", [P, TOPK, NT], FP32),
                                        ("slots", [P, TOPK, NT], I32), ("tile_e", [P, NTL], I32)):
                    res[name] = ffn.enter_context(nc.sbuf_tensor(name, shape, dt))
                attention_output(nc, w, scr, res)
                route(nc, w, scr, res)
                experts(nc, w, scr, res)
                gate_loop(nc, w, scr, res)
        phase_ffn(nc, w, res, out)


def kernel(**inputs):
    import numpy as np
    import concourse.bacc as bacc
    from concourse.bass_utils import run_bass_kernel_spmd

    nc = bacc.Bacc("TRN2", target_bir_lowering=False, num_devices=1)
    a = {k: np.asarray(v) for k, v in inputs.items()}
    L0, F0, L1, F1 = "L0_attn_", "L0_ffn_", "L1_attn_", "L1_ffn_"
    firs = np.zeros((D, len(FIRS), PADW), np.float32)
    for n, (name, k) in enumerate(zip(("fir_s", "fir_m", "fir_l"), FIRS)):
        firs[:, n, 2 * WIN - k:2 * WIN] = a[L0 + name].reshape(D, k)
    laid = {
        "x": a[L0 + "hidden_states"], "wqT": a[L0 + "Wq"].T, "wkT": a[L0 + "Wk"].T, "wvT": a[L0 + "Wv"].T, "woT": a[L0 + "Wo"].T,
        "gatesT": np.concatenate([a[L0 + "gate_w"].reshape(H * NGATE, D), a[L0 + "Wb"]]).T,
        "taps": np.stack([a[L0 + "conv_q"], a[L0 + "conv_k"], a[L0 + "conv_v"]], 1),
        "gate_b": a[L0 + "gate_b"].reshape(-1), "log_temp": a[L0 + "log_temp"].reshape(-1), "eps": a[L0 + "eps_param"].reshape(-1),
        "fir_pad": firs.reshape(D * len(FIRS), PADW),
        "ao_cols": np.stack([np.tile(a[L0 + "norm_w"], H), a[F0 + "g1"], a[F0 + "be1"], a[F0 + "g2"], a[F0 + "be2"]], 1),
        "mix_w": a[F0 + "mix_w"], "mix_b": a[F0 + "mix_b"], "router_w": a[F0 + "router_w"], "w1": a[F0 + "w1"], "w2": a[F0 + "w2"],
        "b1": a[F0 + "b1"], "b2": a[F0 + "b2"],
        "gamma": a[L1 + "gamma"].reshape(D, 1), **{f"gl_{n}": a[L1 + n] for n in ("wq", "wk", "wv", "wa", "wg", "wo")},
        "pf_w1": a[F1 + "W1"], "pf_w2": a[F1 + "W2"], "pf_b2": a[F1 + "b2"],
        "pf_cols": np.stack([a[F1 + n].reshape(FC, P).T for n in ("b1", "quantum_phases", "quantum_weights_real", "quantum_weights_imag")], 1),
    }
    arrays = {f"in_{k}": np.ascontiguousarray(v) for k, v in laid.items()}
    w = {k: nc.dram_tensor(f"in_{k}", arrays[f"in_{k}"].shape, FP32, kind="ExternalInput").ap() for k in laid}
    out = nc.dram_tensor("out", (BATCH, SEQ, D), FP32, kind="ExternalOutput").ap()
    build(nc, w, out)
    return run_bass_kernel_spmd(nc, [arrays], core_ids=[0]).results[0]["out"]
```

```python
import concourse.bass as bass
from concourse import mybir
from contextlib import ExitStack

FP32 = mybir.dt.float32
ALU = mybir.AluOpType
ACT = mybir.ActivationFunctionType
AX = mybir.AxisListType

BATCH, SEQ, D = 16, 512, 128
P = 128
TPS = SEQ // P
NT = BATCH * TPS
H, DH = 4, 32
CH = 32
CPT = P // CH
CPS = SEQ // CH
TAPS = 4
FIRS = (3, 15, 63)
WIN = 64
NWIN = SEQ // WIN
NGATE = 5
NE, FF = 8, 512
FC = FF // P
PADW = 2 * WIN + WIN - 1


class Chain:

    def __init__(self, eng, sem, turn=0, per_turn=0, start=0, waits=None):
        self.sem_of_waits = waits
        self.eng, self.sem, self.base, self.per_turn, self.n = eng, sem, turn * per_turn, per_turn, start

    def __call__(self, ins):
        self.n += 1
        ins.then_inc(self.sem, 1)
        self.eng.wait_ge(self.sem, self.base + self.n)

    def apart(self, ins):
        self(ins)
        self.eng.sem_inc(self.sem_of_waits, 1)

    def end(self):
        assert self.n == self.per_turn, (self.n, self.per_turn)


def wait_apart(eng, sem, value, waits):
    eng.wait_ge(sem, value)
    eng.sem_inc(waits, 1)


def tensors(nc, ctx, tag):
    ctx.callback(nc.all_engine_barrier)

    def sb(name, shape, dt=FP32):
        return ctx.enter_context(nc.sbuf_tensor(f"{tag}_{name}", shape, dt))

    def pb(name, shape, dt=FP32):
        return ctx.enter_context(nc.psum_tensor(f"{tag}_{name}", shape, dt))

    def sem(name):
        held = ctx.enter_context(nc.semaphore(f"{tag}_{name}"))
        ctx.callback(nc.gpsimd.sem_clear, held)
        return held

    return sb, pb, sem


def heads(ap):
    return ap.rearrange("p t (h d) -> p (t h) d", h=H)


def flat(ap):
    return ap.rearrange("p t d -> p (t d)")


def nth(i, u, n, of, side=2):
    return i * (side * of) + (side * n + u + 1)


def one(ap):
    return ap.rearrange("p a n -> p (a n)")


def over(ap, n):
    return ap.unsqueeze(2).to_broadcast([ap.shape[0], ap.shape[1], n])


def row_norm(dve, src, dst, mv, rstd):
    for t in range(TPS):
        ins = dve.tensor_scalar(dst[t], src[t], mv[:, t, 0:1], rstd[:, t:t + 1], ALU.subtract, ALU.mult)
    return ins


def tiles_of(ap):
    return [ap[:, t, :] for t in range(TPS)]


def pair_stats(dve, link, srcs, st, mv, ready):
    for u in range(len(srcs)):
        for t, x in enumerate(srcs[u]()):
            ins = dve.bn_stats(st[u][:, t, :], x)
        link.apart(ins)
        for t in range(TPS):
            ins = dve.bn_aggr(mv[u][:, t, :], st[u][:, t, :])
        ins.then_inc(ready, 1)


def delta_inputs(nc, x, w, scr, res):
    with ExitStack() as ctx:
        sb, pb, sem = tensors(nc, ctx, "di")
        two = lambda name, shape: [sb(f"{name}{u}", shape) for u in range(2)]
        wq, wk, wv = (sb(n, [D, D]) for n in ("wq", "wk", "wv"))
        wg = sb("wg", [D, H * NGATE + H])
        taps = sb("taps", [D, 3, TAPS])
        gate_b = sb("gate_b", [P, H * NGATE])
        log_temp = sb("log_temp", [P, H])
        mhalf = sb("mhalf", [P, H * TPS])
        lower = sb("lower", [P, CH])
        upper = sb("upper", [P, CH])
        zrow = sb("zrow", [P, D])
        st, mv, rstd = two("st", [P, TPS, 6]), two("mv", [P, TPS, 2]), two("rstd", [P, TPS])
        xn, xnT = two("xn", [P, TPS, D]), two("xnT", [D, SEQ])
        conv = [two(f"conv{n}", [D, SEQ]) for n in range(3)]
        kact, vact = two("kact", [D, SEQ]), two("vact", [D, SEQ])
        sq = [two(f"sq{n}", [D, SEQ]) for n in range(2)]
        head_of = sb("head_of", [D, H])
        ss = two("ss", [P, 2, TPS * H])
        rn = two("rn", [P, TPS * H])
        kt, kb, vt, vb = (two(n, [P, TPS, D]) for n in ("kt", "kb", "vt", "vb"))
        kq = two("kq", [D, 2, SEQ])
        beta = two("beta", [P, TPS * H])
        am, at = two("am", [P, H, TPS, CH]), two("at", [P, H, TPS, CH])
        TAP = (1, 0, 2)
        A = [pb(f"A{u}", [P, 4, 512]) for u in range(2)]

        loaded, consts, x_first, x_rest, x_in, stored, zst, lt, own = (
            sem(n) for n in ("loaded", "consts", "x_first", "x_rest", "x_in", "stored", "zst", "lt", "own"))
        ln_own, rq_ready = sem("ln_own"), sem("rq_ready")
        sums_ready, eps_added, rstd_ready, xn_ready, xT_done, xnT_ready, proj_done, gates_done = (
            sem(n) for n in ("sums_ready", "eps_added", "rstd_ready", "xn_ready", "xT_done", "xnT_ready", "proj_done", "gates_done"))
        tap_done, conv_ready, act_ready, tok_done, sq_ready, ss_ready, rn_ready = (
            sem(n) for n in ("tap_done", "conv_ready", "act_ready", "tok_done", "sq_ready", "ss_ready", "rn_ready"))
        v_ready, vb_ready, kb_ready, tok_ready, back_done, back_ready, beta_ready, gram_done, masked, at_ready, am_ready, sums_done, logits_ready = (
            sem(n) for n in ("v_ready", "vb_ready", "kb_ready", "tok_ready", "back_done", "back_ready", "beta_ready", "gram_done", "masked", "at_ready", "am_ready", "sums_done", "logits_ready"))
        pool_waits, dve_waits, pe_waits = sem("pool_waits"), sem("dve_waits"), sem("pe_waits")
        block = ctx.enter_context(nc.Block())
        X, ident = res["x"], res["ident"]
        PAIRS = BATCH // 2
        STORES = 7 * 2
        CONSTS = 6 + 2 * CPT + 1 + H
        SS = 128
        per_head = lambda ap: ap.rearrange("p (g d) -> p g d", d=DH)

        @block.sync
        def _(sp):
            sp.dma_start(X[:, 0:2 * TPS, :], x[0:2, :, :].rearrange("b (t p) d -> p (b t) d", p=P)).then_inc(x_first, 16)
            sp.wait_ge(loaded, 16 * 8)
            sp.dma_start(X[:, 2 * TPS:, :], x[2:, :, :].rearrange("b (t p) d -> p (b t) d", p=P)).then_inc(x_rest, 16)
            sp.wait_ge(x_first, 16)
            sp.sem_inc(x_in, 1)
            sp.wait_ge(x_rest, 16)
            sp.sem_inc(x_in, PAIRS - 1)
            sp.wait_ge(consts, 1)
            sp.dma_start(scr["xs"].rearrange("(p a) d -> p a d", p=P), zrow[:, :].unsqueeze(1).to_broadcast([P, NTL + DEEP, D])).then_inc(zst, 16)
            for b in range(BATCH):
                sp.dma_start(scr["v"][b, 0:WIN, :], zrow[0:WIN, :]).then_inc(zst, 16)
            with sp.Fori(0, PAIRS) as i:
                rows = lambda name, u: scr[name][bass.ds(2 * i + u, 1), :, :].rearrange("a p n -> (a p) n")
                for u in range(2):
                    sp.wait_ge(v_ready, nth(i, u, 0, 1))
                    sp.dma_start(scr["v"][bass.ds(2 * i + u, 1), WIN:WIN + SEQ, :].rearrange("a (t p) d -> p (a t) d", p=P), vt[u][:, :, :]).then_inc(stored, 16)
                for name, src, ready, n, of in (("vb", vb, vb_ready, 0, 1), ("k", kt, tok_ready, 0, 1), ("kb", kb, kb_ready, 0, 1)):
                    for u in range(2):
                        sp.wait_ge(ready, nth(i, u, n, of))
                        sp.dma_start(rows(name, u), flat(src[u][:, :, :])).then_inc(stored, 16)
                for u in range(2):
                    sp.wait_ge(act_ready, nth(i, u, 1, 3))
                    sp.dma_start(rows("qT", u), kq[u][:, 1, :]).then_inc(stored, 16)
                for u in range(2):
                    for name, src, ready in (("attnT", at, at_ready), ("A", am, am_ready)):
                        sp.wait_ge(ready, nth(i, u, 0, 1) + (2 if ready is at_ready else 0))
                        sp.dma_start(rows(name, u), src[u][:, :, :, :].rearrange("p h t c -> p (h t c)")).then_inc(stored, 16)
            sp.wait_ge(stored, 16 * STORES * (PAIRS + 1))
            sp.wait_ge(zst, 16 * (BATCH + 1))

        @block.gpsimd
        def _(pool):
            const = Chain(pool, consts)
            for dst, value in ((zrow, 0.0), (ident, 0.0), (lower, -1.0), (upper, 1.0), (mhalf, -0.5)):
                const(pool.memset(dst[:, :], value))
            const(pool.affine_select(out=ident[:, :], in_=ident[:, :], compare_op=ALU.not_equal, fill=1.0,
                                     base=0, pattern=[[-1, P]], channel_multiplier=1))
            for c in range(CPT):
                rows = slice(CH * c, CH * c + CH)
                const(pool.affine_select(out=lower[rows, :], in_=lower[rows, :], compare_op=ALU.is_gt, fill=0.0,
                                         base=0, pattern=[[-1, CH]], channel_multiplier=1))
                const(pool.affine_select(out=upper[rows, :], in_=upper[rows, :], compare_op=ALU.is_ge, fill=0.0,
                                         base=0, pattern=[[1, CH]], channel_multiplier=-1))
            const(pool.memset(head_of[:, :], 0.0))
            for h in range(H):
                const(pool.memset(head_of[h * DH:(h + 1) * DH, h:h + 1], 1.0))

            def norm_powers(i):
                for u in range(2):
                    wait_apart(pool, sums_ready, nth(i, u, 0, 1), pool_waits)
                    pool.tensor_scalar(rstd[u][:, :], mv[u][:, :, 1], 1e-5, None, ALU.add).then_inc(eps_added, 1)
                    pool.wait_ge(eps_added, nth(i, u, 0, 1))
                    pool.tensor_tensor(rstd[u][:, :], rstd[u][:, :], mhalf[:, 0:TPS], ALU.pow).then_inc(rstd_ready, 1)

            def pair(i, more):
                for u in range(2):
                    pool.wait_ge(ss_ready, nth(i, u, 0, 2))
                    pool.tensor_tensor(rn[u][:, :], ss[u][:, 0, :], mhalf[:, :], ALU.pow).then_inc(rn_ready, 1)
                if more:
                    norm_powers(i + 1)
                pool.wait_ge(stored, (i + 1) * (16 * STORES))
                for u in range(2):
                    pool.wait_ge(v_ready, nth(i, u, 0, 1))
                    pool.tensor_tensor(heads(vb[u][:, :, :]), heads(vt[u][:, :, :]), over(beta[u][:, :], DH), ALU.mult).then_inc(vb_ready, 1)
                for u in range(2):
                    pool.wait_ge(tok_ready, nth(i, u, 0, 1))
                    pool.tensor_tensor(heads(kb[u][:, :, :]), heads(kt[u][:, :, :]), over(beta[u][:, :], DH), ALU.mult).then_inc(kb_ready, 1)
                for u in range(2):
                    pool.wait_ge(ss_ready, nth(i, u, 1, 2))
                    pool.tensor_tensor(res["rq"][:, bass.ds((2 * i + u) * TPS, TPS), :], ss[u][:, 1, :].rearrange("p (t h) -> p t h", h=H),
                                       mhalf[:, :].rearrange("p (t h) -> p t h", h=H), ALU.pow).then_inc(rq_ready, 1)
                for u in range(2):
                    pool.wait_ge(masked, nth(i, u, 0, 1))
                    bt = beta[u][:, :].rearrange("p (t h) -> p h t", t=TPS).unsqueeze(3).to_broadcast([P, H, TPS, CH])
                    pool.tensor_tensor(am[u][:, :, :, :], am[u][:, :, :, :], bt, ALU.mult).then_inc(am_ready, 1)

            norm_powers(0)
            with pool.Fori(0, PAIRS - 1) as i:
                pair(i, True)
            pair(PAIRS - 1, False)

        @block.vector
        def _(dve):
            K = 3 * (TAPS - 2)
            rows = lambda i, u: [one(X[:, bass.ds((2 * i + u) * TPS + t, 1), :]) for t in range(TPS)]

            def sums(i):
                link = Chain(dve, ln_own, i, 2, waits=dve_waits)
                pair_stats(dve, link, [lambda: rows(i, 0), lambda: rows(i, 1)], st, mv, sums_ready)
                link.end()

            def norm(i):
                for u in range(2):
                    dve.wait_ge(rstd_ready, nth(i, u, 0, 1))
                    row_norm(dve, rows(i, u), tiles_of(xn[u]), mv[u], rstd[u]).then_inc(xn_ready, 1)

            def pair(i, more):
                link = Chain(dve, own, i, K, waits=dve_waits)
                for n in range(3):
                    for j in range(TAPS - 1):
                        s = TAPS - 1 - j
                        for u in range(2):
                            if j == 0:
                                dve.wait_ge(tap_done, nth(i, u, n, 3))
                            ins = dve.scalar_tensor_tensor(conv[n][u][:, s:], A[u][:, 1 + n, 0:SEQ - s], taps[:, TAP[n], j:j + 1],
                                                           conv[n][u][:, s:], ALU.mult, ALU.add)
                            if j == TAPS - 2:
                                ins.then_inc(conv_ready, 1)
                        if j < TAPS - 2:
                            link(ins)
                    for u in range(2):
                        if n == 0:
                            dve.wait_ge(beta_ready, nth(i, u, 0, 1))
                            dve.tensor_tensor(res["logits"][:, bass.ds((2 * i + u) * TPS, TPS), :],
                                              A[u][:, 0, 0:96].rearrange("p (t g) -> p t g", t=TPS)[:, :, 0:20],
                                              gate_b[:, :].unsqueeze(1).to_broadcast([P, TPS, 20]), ALU.add).then_inc(logits_ready, 1)
                        else:
                            dve.wait_ge(sums_done, nth(i, u, n - 1, 2))
                            dve.tensor_scalar(ss[u][:, n - 1, :], A[u][:, 0, SS + (n - 1) * TPS * H:SS + n * TPS * H], 1e-6, None, ALU.add).then_inc(ss_ready, 1)
                if more:
                    wait_apart(dve, x_in, i + 2, dve_waits)
                    sums(i + 1)
                dve.wait_ge(stored, (i + 1) * (16 * STORES))
                for u in range(2):
                    dve.wait_ge(rn_ready, nth(i, u, 0, 1))
                    dve.tensor_tensor(heads(kt[u][:, :, :]), per_head(A[u][:, 1, :]), over(rn[u][:, :], DH), ALU.mult).then_inc(tok_ready, 1)
                if more:
                    norm(i + 1)
                for u in range(2):
                    dve.wait_ge(gram_done, nth(i, u, 0, 1))
                    for dst, n, mask, ready in ((am, 0, lower, masked), (at, 1, upper, at_ready)):
                        m = mask[:, :].unsqueeze(1).unsqueeze(1).to_broadcast([P, H, TPS, CH])
                        src = A[u][:, :, 0:2 * TPS * CH].rearrange("p h (t n c) -> p h t n c", t=TPS, n=2)[:, :, :, n, :]
                        dve.tensor_tensor(dst[u][:, :, :, :], src, m, ALU.mult).then_inc(ready, 1)
                link.end()

            dve.wait_ge(loaded, 16 * 8)
            dve.wait_ge(consts, CONSTS)
            dve.wait_ge(x_in, 1)
            dve.sem_inc(at_ready, 2)
            sums(0)
            norm(0)
            with dve.Fori(0, PAIRS - 1) as i:
                pair(i, True)
            pair(PAIRS - 1, False)

        @block.scalar
        def _(act_e):
            for dst, src in ((wq, "wqT"), (wk, "wkT"), (wv, "wvT"), (wg, "gatesT")):
                act_e.dma_start(dst[:, :], w[src]).then_inc(loaded, 16)
            act_e.dma_start(taps[:, :, :], w["taps"]).then_inc(loaded, 16)
            act_e.dma_start(gate_b[:, :], w["gate_b"].partition_broadcast(P)).then_inc(loaded, 16)
            act_e.dma_start(log_temp[:, :], w["log_temp"].partition_broadcast(P)).then_inc(loaded, 16)
            act_e.dma_start(res["eps"][:, :], w["eps"].partition_broadcast(P)).then_inc(loaded, 16)
            act_e.sem_inc(stored, 16 * STORES)
            act_e.wait_ge(loaded, 16 * 8)
            act_e.activation(res["inv_temp"][:, :], log_temp[:, :], ACT.Exp, scale=-1.0).then_inc(lt, 1)

            def rows_by_channel(i):
                for u in range(2):
                    act_e.wait_ge(xT_done, nth(i, u, 0, 1))
                    act_e.activation(xnT[u][:, :], A[u][:, 0, :], ACT.Copy).then_inc(xnT_ready, 1)

            def pair(i, more):
                def started(n):
                    for u in range(2):
                        act_e.wait_ge(proj_done, nth(i, u, n, 3))
                        act_e.activation(conv[n][u][:, :], A[u][:, 1 + n, :], ACT.Copy, scale=taps[:, TAP[n], TAPS - 1:TAPS]).then_inc(tap_done, 1)

                def activated(n, dst):
                    for u in range(2):
                        act_e.wait_ge(conv_ready, nth(i, u, n, 3))
                        act_e.activation(dst[u], conv[n][u][:, :], ACT.Silu).then_inc(act_ready, 1)
                    if n < 2:
                        for u in range(2):
                            act_e.wait_ge(act_ready, nth(i, u, n, 3))
                            act_e.activation(sq[n][u][:, :], dst[u], ACT.Square).then_inc(sq_ready, 1)

                started(0)
                act_e.wait_ge(stored, (i + 1) * (16 * STORES))
                for u in range(2):
                    act_e.wait_ge(gates_done, nth(i, u, 0, 1))
                    act_e.activation(beta[u][:, :].rearrange("p (t h) -> p t h", t=TPS), A[u][:, 0, 0:96].rearrange("p (t g) -> p t g", t=TPS)[:, :, 20:24],
                                     ACT.Sigmoid).then_inc(beta_ready, 1)
                started(1)
                activated(0, [kact[u][:, :] for u in range(2)])
                started(2)
                activated(1, [kq[u][:, 1, :] for u in range(2)])
                activated(2, [vact[u][:, :] for u in range(2)])
                for u in range(2):
                    act_e.wait_ge(tok_done, nth(i, u, 1, 2))
                    act_e.activation(flat(vt[u][:, :, :]), A[u][:, 3, :], ACT.Copy).then_inc(v_ready, 1)
                for u in range(2):
                    act_e.wait_ge(back_done, nth(i, u, 0, 1))
                    act_e.activation(kq[u][:, 0, :], A[u][:, 1, :], ACT.Copy).then_inc(back_ready, 1)
                if more:
                    rows_by_channel(i + 1)

            rows_by_channel(0)
            with act_e.Fori(0, PAIRS - 1) as i:
                pair(i, True)
            pair(PAIRS - 1, False)

        @block.tensor
        def _(pe):
            pe.wait_ge(loaded, 16 * 8)
            pe.wait_ge(consts, CONSTS)

            def rows_by_channel(i):
                for u in range(2):
                    pe.wait_ge(xn_ready, nth(i, u, 0, 1))
                    for t in range(TPS):
                        ins = pe.transpose(A[u][:, 0, t * P:(t + 1) * P], xn[u][:, t, :], ident[:, :])
                    ins.then_inc(xT_done, 1)

            def pair(i, more):
                for n, wt in enumerate((wk, wq, wv)):
                    for u in range(2):
                        if n == 0:
                            pe.wait_ge(xnT_ready, nth(i, u, 0, 1))
                            pe.wait_ge(at_ready, nth(i, u, 0, 1))
                        pe.matmul(A[u][:, 1 + n, :], wt[:, :], xnT[u][:, :], start=True, stop=True).then_inc(proj_done, 1)
                    if n == 0:
                        for u in range(2):
                            for t in range(TPS):
                                ins = pe.matmul(A[u][:, 0, t * 24:(t + 1) * 24], xnT[u][:, t * P:(t + 1) * P], wg[:, :], start=True, stop=True)
                            ins.then_inc(gates_done, 1)

                def rows_of(n, bank, src):
                    for u in range(2):
                        pe.wait_ge(act_ready, nth(i, u, n, 3))
                        for t in range(TPS):
                            ins = pe.transpose(A[u][:, bank, t * P:(t + 1) * P], src[u][:, t * P:(t + 1) * P], ident[:, :])
                        ins.then_inc(tok_done, 1)

                def squares_of(n):
                    for u in range(2):
                        pe.wait_ge(sq_ready, nth(i, u, n, 2))
                        if n == 0:
                            pe.wait_ge(logits_ready, nth(i, u, 0, 1))
                        else:
                            pe.wait_ge(ss_ready, nth(i, u, 0, 2))
                        for t in range(TPS):
                            at_ = SS + (n * TPS + t) * H
                            ins = pe.matmul(A[u][:, 0, at_:at_ + H], sq[n][u][:, t * P:(t + 1) * P], head_of[:, :], start=True, stop=True)
                        ins.then_inc(sums_done, 1)

                rows_of(0, 1, kact)
                squares_of(0)
                squares_of(1)
                rows_of(2, 3, vact)
                for u in range(2):
                    pe.wait_ge(tok_ready, nth(i, u, 0, 1))
                    for t in range(TPS):
                        ins = pe.transpose(A[u][:, 1, t * P:(t + 1) * P], kt[u][:, t, :], ident[:, :])
                    ins.then_inc(back_done, 1)
                if more:
                    rows_by_channel(i + 1)
                for u in range(2):
                    wait_apart(pe, v_ready, nth(i, u, 0, 1), pe_waits)
                    if more:
                        wait_apart(pe, xnT_ready, nth(i + 1, u, 0, 1), pe_waits)
                    wait_apart(pe, back_ready, nth(i, u, 0, 1), pe_waits)
                    for t in range(TPS):
                        for c in range(CPT):
                            cols = slice(t * P + c * CH, t * P + (c + 1) * CH)
                            for h in range(H):
                                rows = slice(DH * h, DH * h + DH)
                                ins = pe.matmul(A[u][CH * c:CH * c + CH, h, t * 2 * CH:(t + 1) * 2 * CH],
                                                kq[u][rows, 0, cols], kq[u][rows, :, cols], start=True, stop=True)
                    ins.then_inc(gram_done, 1)

            rows_by_channel(0)
            with pe.Fori(0, PAIRS - 1) as i:
                pair(i, True)
            pair(PAIRS - 1, False)


def fir_and_inverses(nc, w, scr, res):
    with ExitStack() as ctx:
        sb, pb, sem = tensors(nc, ctx, "fi")
        NG = H * NGATE
        GC = 4
        F3 = len(FIRS)
        vwin = sb("vwin", [P, BATCH, NWIN, D])
        vst = [sb(f"vst{n}", [P, GC, P]) for n in range(2)]
        TB = 4
        toep = [sb(f"toep{n}", [P, GC * F3, WIN]) for n in range(TB)]
        tmp = [sb(f"tmp{n}", [P, 2, F3, WIN]) for n in range(2)]
        pw = sb("pw", [P, WIN, NG])
        pf = sb("pf", [P, H, F3, WIN])
        oc = sb("oc", [P, WIN, D])
        mx, sm = sb("mx", [P, NT * H]), sb("sm", [P, NT * H])
        gain = sb("gain", [P, H])
        GP = 2
        SHARE = BATCH // GP // 2
        first = {"pool": 0, "dve": SHARE}
        am = {e: [sb(f"am_{e}{m}", [P, CH, CH]) for m in range(2)] for e in ("pool", "dve")}
        um = {e: [sb(f"um_{e}{m}", [P, CH, CH]) for m in range(2)] for e in ("pool", "dve")}
        pr = {e: sb(f"pr_{e}", [P, CH * CH // 4 + CH]) for e in ("pool", "dve")}
        F = [pb(f"F{n}", [P, 2, 512]) for n in range(2)]
        win_in, own, pown, toep_in = sem("win_in"), sem("own"), sem("pown"), [sem(f"toep_in{n}") for n in range(TB)]
        down, fir_summed = sem("down"), sem("fir_summed")
        vst_ready, fir_done, fir_read, exps, prb, pw_out, pw_in, oc_out = (
            sem(n) for n in ("vst_ready", "fir_done", "fir_read", "exps", "prb", "pw_out", "pw_in", "oc_out"))
        mats_in = {e: [sem(f"mats_in_{e}{m}") for m in range(2)] for e in ("pool", "dve")}
        mats_out = {e: [sem(f"mats_out_{e}{m}") for m in range(2)] for e in ("pool", "dve")}
        solved = {e: sem(f"solved_{e}") for e in ("pool", "dve")}
        sub, pf_ready = sem("sub"), sem("pf_ready")
        pool_waits, dve_waits = sem("pool_waits"), sem("dve_waits")
        block = ctx.enter_context(nc.Block())
        L, PR, eps = res["logits"], res["probs"], res["eps"]
        L4 = L[:, :, :].rearrange("p t (h g) -> p (t h) g", h=H)
        P4 = PR[:, :, :].rearrange("p t (h g) -> p (t h) g", h=H)

        def matrices(eng, e, k):
            g = first[e] + k
            if k >= 2:
                eng.wait_ge(solved[e], k - 1)
            for b in range(GP):
                for c in range(CPT):
                    src = scr["A"][g * GP + b, c * CH:(c + 1) * CH, :].rearrange("i (x j) -> x i j", j=CH)
                    p0 = b * 64 + c * 16
                    eng.dma_start(am[e][k % 2][p0:p0 + 16, :, :], src).then_inc(mats_in[e][k % 2], 16)

        @block.sync
        def _(sp):
            matrices(sp, "dve", 0)
            for b in range(BATCH):
                sp.dma_start(vwin[:, b, :, :], bass.AP(tensor=scr["v"].tensor, offset=b * (SEQ + WIN) * D,
                                                       ap=[[D, P], [WIN * D, NWIN], [1, D]])).then_inc(win_in, 16)
            matrices(sp, "dve", 1)
            with sp.Fori(0, D // GC // TB) as i:
                for u in range(TB):
                    sp.wait_ge(fir_done, TB * i + u + 1)
                    rows = w["fir_pad"][bass.ds((TB * i + u) * (GC * F3), GC * F3), :]
                    src = bass.AP(tensor=rows.tensor, offset=rows.offset, ap=[[1, P], [PADW, GC * F3], [1, WIN]])
                    sp.dma_start(toep[u][:, :, :], src).then_inc(toep_in[u], 16)
            matrices(sp, "pool", 2)
            matrices(sp, "dve", 2)
            sp.wait_ge(fir_summed, D // GC)
            sp.dma_start(scr["ofir"].rearrange("b (j t) d -> (b j) t d", t=WIN), oc[:, :, :]).then_inc(oc_out, 16)
            matrices(sp, "pool", 3)
            matrices(sp, "dve", 3)
            sp.wait_ge(oc_out, 16)

        def solve(eng, e, chain, m, turn):
            A_, U, R = am[e][m], um[e][m], pr[e]
            wait_apart(eng, mats_out[e][m], 16 * (turn + 1), pool_waits if e == "pool" else dve_waits)
            chain.apart(eng.memset(U[:, :, :], 0.0))
            chain(eng.memset(U[:, :, :].rearrange("p a b -> p (a b)")[:, 0:CH * CH:CH + 1], 1.0))
            eng.wait_ge(mats_in[e][m], (turn + 1) * (16 * GP * CPT))
            for j in range(CH - 1):
                n, m = j + 1, CH - 1 - j
                prod = R[:, 0:n * m].rearrange("p (a b) -> p a b", a=n)
                chain(eng.tensor_tensor(prod, U[:, 0:n, j:j + 1].to_broadcast([P, n, m]),
                                        A_[:, j + 1:, j].unsqueeze(1).to_broadcast([P, n, m]), ALU.mult))
                ins = eng.tensor_tensor(U[:, 0:n, j + 1:], U[:, 0:n, j + 1:], prod, ALU.add)
                chain(ins)
            chain.eng.sem_inc(solved[e], 1)

        SOLVE = 2 + 2 * (CH - 1)

        @block.gpsimd
        def _(pool):
            for m in range(2):
                pool.sem_inc(mats_out["pool"][m], 16)
            with pool.Fori(0, SHARE // 2) as j:
                for m in range(2):
                    chain = Chain(pool, pown, 2 * j + m, SOLVE, waits=pool_waits)
                    solve(pool, "pool", chain, m, j)
                    chain.end()

        @block.vector
        def _(dve):
            SOFT = 9
            link = Chain(dve, own, 0, SOFT)
            temp = res["inv_temp"][:, :].unsqueeze(1).to_broadcast([P, NT, H])
            L_h = lambda g: L[:, :, :].rearrange("p t (h g) -> p t h g", h=H)[:, :, :, g]
            for g in range(NGATE):
                ins = dve.tensor_tensor(L_h(g), L_h(g), temp, ALU.mult)
            link(ins)
            link(dve.reduce_max(mx[:, :], L4, axis=AX.X))
            dve.tensor_tensor(L4, L4, over(mx[:, :], NGATE), ALU.subtract).then_inc(sub, 1)
            link(dve.tensor_scalar(eps[:, :], eps[:, :], 0.0, 0.2, ALU.max, ALU.min))
            link(dve.tensor_scalar(gain[:, :], eps[:, :], -5.0, 1.0, ALU.mult, ALU.add))
            dve.wait_ge(exps, 1)
            link(dve.reduce_sum(sm[:, :], P4, axis=AX.X))
            link(dve.reciprocal(sm[:, :], sm[:, :]))
            smh = sm[:, :].rearrange("p (t h) -> p t h", h=H)
            link(dve.tensor_tensor(smh, smh, gain[:, :].unsqueeze(1).to_broadcast([P, NT, H]), ALU.mult))
            link(dve.tensor_tensor(P4, P4, over(sm[:, :], NGATE), ALU.mult))
            ev = eps[:, :].unsqueeze(1).to_broadcast([P, NT, H])
            for g in range(NGATE):
                pg = PR[:, :, :].rearrange("p t (h g) -> p t h g", h=H)[:, :, :, g]
                ins = dve.tensor_tensor(pg, pg, ev, ALU.add)
            link(ins)
            p3 = P4[:, :, 3]
            dve.tensor_tensor(p3, p3, res["rq"][:, :, :].rearrange("p t h -> p (t h)"), ALU.mult).then_inc(prb, 1)

            def solve_group(k):
                chain = Chain(dve, down, k, SOLVE, waits=dve_waits)
                solve(dve, "dve", chain, k % 2, k // 2)
                chain.end()

            for m in range(2):
                dve.sem_inc(mats_out["dve"][m], 16)
            solve_group(0)
            dve.wait_ge(pw_in, 16)
            for h in range(H):
                for f in range(F3):
                    ins = dve.tensor_copy(pf[:, h, f, :], pw[:, ::-1, h * NGATE + f])
            ins.then_inc(pf_ready, 1)
            dve.wait_ge(pf_ready, 1)
            dve.sem_inc(fir_read, 2)
            with dve.Fori(0, H) as h:
                with dve.Fori(0, DH // GC // 2) as k:
                    for u in range(2):
                        grp = h * (DH // GC) + k * 2 + u
                        dve.wait_ge(fir_done, grp + 1 + TB)
                        wgt = pf[:, bass.ds(h, 1), :, :].rearrange("p a f t -> p (a f) t").unsqueeze(1).to_broadcast([P, 2, F3, WIN])
                        for c2 in range(2):
                            ins = dve.tensor_tensor(tmp[c2][:, :, :, :], F[u][:, c2, 0:2 * F3 * WIN].rearrange("p (c f t) -> p c f t", c=2, f=F3),
                                                    wgt, ALU.mult)
                        ins.then_inc(fir_read, 1)
                        dve.wait_ge(fir_read, grp + 3)
                        for c2 in range(2):
                            out = oc[:, :, bass.ds(grp * GC + 2 * c2, 2)].rearrange("p t c -> p c t")
                            ins = dve.reduce_sum(out, tmp[c2][:, :, :, ::-1].rearrange("p c f t -> p c t f"), axis=AX.X)
                        ins.then_inc(fir_summed, 1)
                        dve.wait_ge(fir_summed, grp + 1)
            for k in range(1, SHARE):
                solve_group(k)
            link.end()

        @block.scalar
        def _(act_e):
            matrices(act_e, "pool", 0)
            matrices(act_e, "pool", 1)
            act_e.wait_ge(sub, 1)
            act_e.activation(PR[:, :, :], L[:, :, :], ACT.Exp).then_inc(exps, 1)
            act_e.wait_ge(prb, 1)
            act_e.dma_start(scr["probs"].rearrange("(t p) g -> p t g", p=P), PR[:, :, :]).then_inc(pw_out, 16)
            act_e.wait_ge(pw_out, 16)
            act_e.dma_start(pw[:, :, :], scr["probs"].rearrange("(w t) g -> w t g", t=WIN)).then_inc(pw_in, 16)
            act_e.wait_ge(win_in, 16 * BATCH)
            vw = vwin[:, :, :, :].rearrange("p b j d -> p (b j) d")
            with act_e.Fori(0, D // GC // 2) as i:
                for u in range(2):
                    act_e.wait_ge(fir_done, 2 * i + u + TB - 1)
                    act_e.activation(vst[u][:, :, :], vw[:, :, bass.ds((2 * i + u) * GC, GC)].rearrange("p w c -> p c w"), ACT.Copy)\
                         .then_inc(vst_ready, 1)
            for e, k in (("dve", 0), ("pool", 0), ("pool", 1), ("dve", 1), ("pool", 2), ("dve", 2), ("pool", 3), ("dve", 3)):
                act_e.wait_ge(solved[e], k + 1)
                act_e.dma_start(scr["T"][first[e] + k], um[e][k % 2][:, :, :].rearrange("p a b -> p (a b)")).then_inc(mats_out[e][k % 2], 16)
            for e in ("pool", "dve"):
                for m in range(2):
                    act_e.wait_ge(mats_out[e][m], 16 * (SHARE // 2 + 1))

        @block.tensor
        def _(pe):
            pe.sem_inc(fir_done, TB)
            with pe.Fori(0, D // GC // TB) as i:
                for v in range(TB):
                    u = v % 2
                    pe.wait_ge(vst_ready, TB * i + v + 1)
                    pe.wait_ge(toep_in[v], 16 * (i + 1))
                    pe.wait_ge(fir_read, TB * i + v + 1)
                    for c in range(GC):
                        ins = pe.matmul(F[u][:, c // 2, (c % 2) * F3 * WIN:(c % 2 + 1) * F3 * WIN], vst[u][:, c, :],
                                        toep[v][:, c * F3:(c + 1) * F3, :], start=True, stop=True)
                    ins.then_inc(fir_done, 1)


def delta_rule(nc, scr, res):
    with ExitStack() as ctx:
        sb, pb, sem = tensors(nc, ctx, "dr")
        GB = 4
        TURNS = BATCH // GB
        X2 = TPS * H
        sets = lambda name, shape: [[sb(f"{name}{m}{b}", shape) for b in range(GB)] for m in range(2)]
        tT, aT = sets("tT", [P, X2, CH]), sets("aT", [P, X2, CH])
        kk, kb, vb = (sets(n, [P, TPS, D]) for n in ("kk", "kb", "vb"))
        qT, wT = sets("qT", [D, SEQ]), sets("wT", [D, SEQ])
        us = sb("us", [P, GB, TPS, D])
        oo = [sb(f"oo{m}", [P, GB, D]) for m in range(2)]
        S = sb("S", [D, GB, D])
        diag = sb("diag", [D, D])
        PAIRS, PB = 2, GB // 2
        W, SP_ = ([pb(f"{n}{k}", [P, 512]) for k in range(PAIRS)] for n in ("W", "SP"))
        O = [pb(f"O{m}", [P, GB, D]) for m in range(2)]
        UW = [pb(f"UW{m}", [P, TPS, D]) for m in range(2)]
        consts, w_done, w_ready, state_zero, pe_waits = (sem(n) for n in ("consts", "w_done", "w_ready", "state_zero", "pe_waits"))
        w_loads, loads = ([sem(f"{n}{m}") for m in range(2)] for n in ("w_loads", "loads"))
        ws_done, ua_ready, s_done, s_ready, o_done, o_ready = (
            sem(n) for n in ("ws_done", "ua_ready", "s_done", "s_ready", "o_done", "o_ready"))
        stored = [sem("stored0"), sem("stored1")]
        block = ctx.enter_context(nc.Block())
        NS = CPS * PAIRS
        W_LOADS, LOADS = 16 * GB * (CPT + 1), 16 * GB * 4

        @block.sync
        def _(sp):
            with sp.Fori(0, TURNS // 2) as j:
                for m in range(2):
                    g = 2 * j + m
                    one = lambda name, b: scr[name][bass.ds(g * GB + b, 1), :, :].rearrange("a p n -> (a p) n")
                    sp.wait_ge(o_done, TPS * g + 1)
                    for b in range(GB):
                        for c in range(CPT):
                            r = slice(c * CH, (c + 1) * CH)
                            tsrc = scr["T"][bass.ds(g * (GB // 2) + b // 2, 1), (b % 2) * 64 + c * 16:(b % 2) * 64 + c * 16 + 16, :]
                            sp.dma_start(tT[m][b][r, :, :], tsrc.rearrange("a x (j i) -> j (a x) i", i=CH)).then_inc(w_loads[m], 16)
                        sp.dma_start(flat(kb[m][b][:, :, :]), one("kb", b)).then_inc(w_loads[m], 16)
                    for b in range(GB):
                        for name, dst in (("vb", vb), ("k", kk), ("qT", qT), ("attnT", aT)):
                            to = dst[m][b]
                            sp.dma_start(to[:, :] if dst is qT else flat(to[:, :, :]), one(name, b)).then_inc(loads[m], 16)

        @block.gpsimd
        def _(pool):
            const = Chain(pool, consts)
            const(pool.memset(diag[:, :], 0.0))
            for h in range(H):
                r = slice(h * DH, (h + 1) * DH)
                const(pool.memset(diag[r, r], 1.0))

        @block.tensor
        def _(pe):
            pe.sem_inc(o_done, TPS + 1)
            pe.sem_inc(w_done, 1)

            def w_part(g, m, b, c):
                if c == 0:
                    wait_apart(pe, w_ready, GB * g + b + 1, pe_waits)
                wait_apart(pe, w_done, CPT * (GB * g + b) + c + 1, pe_waits)
                r = slice(c * CH, (c + 1) * CH)
                for t in range(TPS):
                    for h in range(H):
                        hd = slice(h * DH, (h + 1) * DH)
                        ins = pe.matmul(UW[b % 2][hd, t, r], kb[m][b][r, t, hd], tT[m][b][r, h * TPS + t, :], start=True, stop=True)
                ins.then_inc(w_done, 1)

            def u_chunk(m, n):
                t, c = n // CPT, n % CPT
                r = slice(c * CH, (c + 1) * CH)
                for b in range(GB):
                    for h in range(H):
                        at_ = (b % PB) * D + h * DH
                        pe.matmul(W[b // PB][r, at_:at_ + DH], tT[m][b][r, h * TPS + t, :], vb[m][b][r, t, h * DH:(h + 1) * DH],
                                  start=(b % PB == 0 and h == 0), stop=False, skip_group_check=True)

            def chunk(g, m, n):
                t, c = n // CPT, n % CPT
                r = slice(c * CH, (c + 1) * CH)
                cols = slice(n * CH, (n + 1) * CH)
                o = O[t % 2]
                for k in range(PAIRS):
                    if n:
                        pe.wait_ge(s_ready, g * NS + (n - 1) * PAIRS + k + 1)
                    for b in range(PB * k, PB * (k + 1)):
                        ins = pe.matmul(W[k][r, (b % PB) * D:(b % PB + 1) * D], wT[m][b][:, cols], S[:, b, :], start=False, stop=True, skip_group_check=True)
                    ins.then_inc(ws_done, 1)
                if c == 0:
                    pe.wait_ge(o_ready, TPS * g + t + 1)
                for b in range(GB):
                    pe.matmul(o[r, b, :], qT[m][b][:, cols], S[:, b, :], start=(b == 0), stop=False, skip_group_check=True)
                for k in range(PAIRS):
                    wait_apart(pe, ua_ready, g * NS + n * PAIRS + k + 1, pe_waits)
                    for b in range(PB * k, PB * (k + 1)):
                        for h in range(H):
                            hd = slice(h * DH, (h + 1) * DH)
                            ins = pe.matmul(SP_[k][hd, (b % PB) * DH:(b % PB + 1) * DH], kk[m][b][r, t, hd], us[r, b, t, hd],
                                            start=(n == 0 and b % PB == 0), stop=False, skip_group_check=True)
                    ins.then_inc(s_done, 1)
                for b in range(GB):
                    for h in range(H):
                        hd = slice(h * DH, (h + 1) * DH)
                        ins = pe.matmul(o[r, b, hd], aT[m][b][r, h * TPS + t, :], us[r, b, t, hd], start=False, stop=True, skip_group_check=True)
                if c == CPT - 1:
                    ins.then_inc(o_done, 1)
                if n < CPS - 1:
                    u_chunk(m, n + 1)

            with pe.Fori(0, TURNS // 2) as j:
                wait_apart(pe, w_loads[0], W_LOADS * (j + 1), pe_waits)
                for b in range(GB):
                    for c in range(CPT):
                        w_part(2 * j, 0, b, c)
                for m in range(2):
                    g = 2 * j + m
                    wait_apart(pe, loads[m], LOADS * (j + 1), pe_waits)
                    u_chunk(m, 0)
                    pe.wait_ge(w_ready, GB * (g + 1) + 2)
                    pe.wait_ge(state_zero, g + 1)
                    for n in range(CPS):
                        chunk(g, m, n)
                        if m == 0:
                            if n == 0:
                                wait_apart(pe, w_loads[1], W_LOADS * (j + 1), pe_waits)
                            w_part(g + 1, 1, n // CPT, n % CPT)

        @block.vector
        def _(dve):
            dve.wait_ge(consts, 1 + H)
            with dve.Fori(0, TURNS // 2) as j:
                for m in range(2):
                    g = 2 * j + m
                    dve.memset(S[:, :, :], 0.0).then_inc(state_zero, 1)
                    for n in range(CPS):
                        t, c = n // CPT, n % CPT
                        r = slice(c * CH, (c + 1) * CH)
                        two = lambda ap: ap.rearrange("p (b d) -> p b d", b=PB)
                        for k in range(PAIRS):
                            dve.wait_ge(ws_done, g * NS + n * PAIRS + k + 1)
                            dve.tensor_copy(us[r, PB * k:PB * (k + 1), t, :], two(W[k][r, 0:PB * D])).then_inc(ua_ready, 1)
                        for k in range(PAIRS):
                            dve.wait_ge(s_done, g * NS + n * PAIRS + k + 1)
                            state = SP_[k][:, 0:PB * DH].rearrange("p (b d) -> p b d", b=PB).unsqueeze(2).to_broadcast([D, PB, H, DH])
                            mask = diag[:, :].rearrange("p (h d) -> p h d", h=H).unsqueeze(1).to_broadcast([D, PB, H, DH])
                            dve.tensor_tensor(S[:, PB * k:PB * (k + 1), :].rearrange("p b (h d) -> p b h d", h=H), state, mask, ALU.mult).then_inc(s_ready, 1)
                    dve.wait_ge(s_ready, (g + 1) * NS)

        @block.scalar
        def _(act_e):
            act_e.sem_inc(w_ready, 2)
            act_e.sem_inc(o_ready, 2)
            for m in range(2):
                act_e.sem_inc(stored[m], 16 * GB)

            def w_out(g, m, b):
                act_e.wait_ge(w_done, CPT * (GB * g + b + 1) + 1)
                act_e.activation(wT[m][b][:, :], flat(UW[b % 2][:, :, :]), ACT.Copy, scale=-1.0).then_inc(w_ready, 1)

            with act_e.Fori(0, TURNS // 2) as j:
                for b in range(GB):
                    w_out(2 * j, 0, b)
                for m in range(2):
                    g = 2 * j + m
                    for t in range(TPS):
                        act_e.wait_ge(stored[t % 2], (TPS // 2 * g + t // 2 + 1) * (16 * GB))
                        act_e.wait_ge(o_done, TPS * (g + 1) + t + 2)
                        act_e.activation(flat(oo[t % 2][:, :, :]), flat(O[t % 2][:, :, :]), ACT.Copy).then_inc(o_ready, 1)
                        act_e.wait_ge(o_ready, TPS * g + t + 3)
                        for b in range(GB):
                            act_e.dma_start(scr["o"][bass.ds(g * GB + b, 1), :, t * D:(t + 1) * D].rearrange("a p n -> (a p) n"), oo[t % 2][:, b, :]).then_inc(stored[t % 2], 16)
                        if m == 0:
                            w_out(g + 1, 1, t)
            for m in range(2):
                act_e.wait_ge(stored[m], 16 * GB * (TPS // 2 * TURNS + 1))


def attention_output(nc, w, scr, res):
    U = 4
    with ExitStack() as ctx:
        sb, pb, sem = tensors(nc, ctx, "ao")
        each = lambda name, shape: [sb(f"{name}{u}", shape) for u in range(U)]
        wo, mix, rw = sb("wo", [D, D]), sb("mix", [D, D]), sb("rw", [D, NE])
        cols = sb("cols", [D, 5])
        mix_b = sb("mix_b", [P, D])
        mhalf = sb("mhalf", [P, TPS * H])
        of, dl, vt = ([each(f"{n}{m}", [P, TPS, D]) for m in range(2)] for n in ("of", "dl", "vt"))
        o, t1, sq, h0, h1, c1 = (each(n, [P, TPS, D]) for n in ("o", "t1", "sq", "h0", "h1", "c1"))
        ss, root, rs = (each(n, [P, TPS * H]) for n in ("ss", "root", "rs"))
        st, mv, rstd, rstd2 = each("st", [P, TPS, 6]), each("mv", [P, TPS, 2]), each("rstd", [P, TPS]), each("rstd2", [P, TPS])
        xT = each("xT", [D, SEQ])
        tp, pr = ([pb(f"{n}{u}", [P, 512]) for u in range(U)] for n in ("tp", "pr"))
        rp = pr
        consts, loaded, wo_ready, mix_ready, stored, own, pown = (sem(n) for n in ("consts", "loaded", "wo_ready", "mix_ready", "stored", "own", "pown"))
        paths_in = [sem("paths_in0"), sem("paths_in1")]
        paths_used, gated, sum_ready, sq_ready, sums_ready, eps_added, r_ready, rows_ready, tp_done, xT_ready, pr_done, rp_done, means_ready, root_ready = (
            sem(n) for n in ("paths_used", "gated", "sum_ready", "sq_ready", "sums_ready", "eps_added", "r_ready", "rows_ready", "tp_done", "xT_ready",
                             "pr_done", "rp_done", "means_ready", "root_ready"))
        pool_waits, dve_waits = sem("pool_waits"), sem("dve_waits")
        block = ctx.enter_context(nc.Block())
        X, PR, ident = res["x"], res["probs"], res["ident"]
        CONST = 16 * 5
        GROUPS = BATCH // U
        PATHS = 16 * 3 * U
        NORMS = 4

        def gate(b, k):
            g = PR[:, bass.ds(b * TPS, TPS), :].rearrange("p t (h g) -> p (t h) g", h=H)[:, :, k:k + 1]
            return g.to_broadcast([P, TPS * H, DH])

        @block.sync
        def _(sp):
            for dst, name in ((wo, "woT"), (mix, "mix_w"), (rw, "router_w"), (cols, "ao_cols")):
                sp.dma_start(dst[:, :], w[name]).then_inc(loaded, 16)
            sp.dma_start(mix_b[:, :], w["mix_b"].partition_broadcast(P)).then_inc(loaded, 16)
            with sp.Fori(0, GROUPS // 2) as j:
                for m in range(2):
                    sp.wait_ge(paths_used, U * (2 * j + m) + U)
                    for u in range(U):
                        bb = bass.ds(U * (2 * j + m) + u, 1)
                        sp.dma_start(of[m][u][:, :, :], scr["ofir"][bb, :, :].rearrange("a (t p) d -> p (a t) d", p=P)).then_inc(paths_in[m], 16)
                        sp.dma_start(flat(dl[m][u][:, :, :]), scr["o"][bb, :, :].rearrange("a p n -> (a p) n")).then_inc(paths_in[m], 16)
                        sp.dma_start(vt[m][u][:, :, :], scr["v"][bb, WIN:WIN + SEQ, :].rearrange("a (t p) d -> p (a t) d", p=P)).then_inc(paths_in[m], 16)

        @block.gpsimd
        def _(pool):
            pool.memset(mhalf[:, :], -0.5).then_inc(consts, 1)
            pool.wait_ge(consts, 1)
            with pool.Fori(0, GROUPS // 2) as j:
                for m in range(2):
                    i = 2 * j + m
                    pool.wait_ge(paths_in[m], PATHS * (j + 1))
                    for u in range(U):
                        pool.wait_ge(sum_ready, nth(i, u, 0, 1, U))
                        pool.tensor_tensor(heads(t1[u][:, :, :]), heads(dl[m][u][:, :, :]), gate(U * i + u, 3), ALU.mult).then_inc(pown, 1)
                        pool.wait_ge(pown, nth(i, u, 0, 1, U))
                        pool.tensor_tensor(t1[u][:, :, :], t1[u][:, :, :], of[m][u][:, :, :], ALU.add).then_inc(gated, 1)
                    for n in range(NORMS):
                        for u in range(U):
                            src, dst, k, scale, eps = mv[u][:, :, 1], rstd[u][:, :], TPS, 1.0, 1e-5
                            if n == 1:
                                dst, scale, eps = rstd2[u][:, :], 1.0 + 1e-5, 1e-10
                            if n != 2:
                                wait_apart(pool, sums_ready, nth(i, u, n - (n > 2), NORMS - 1, U), pool_waits)
                            pool.tensor_scalar(dst, src, scale, eps, ALU.mult, ALU.add).then_inc(eps_added, 1)
                            pool.wait_ge(eps_added, nth(i, u, n, NORMS, U))
                            pool.tensor_tensor(dst, dst, mhalf[:, 0:k], ALU.pow).then_inc(r_ready, 1)

        @block.vector
        def _(dve):
            dve.wait_ge(loaded, CONST)
            dve.tensor_scalar(wo[:, :], wo[:, :], cols[:, 0:1], None, ALU.mult).then_inc(wo_ready, 1)
            dve.tensor_tensor(mix[:, :], mix[:, :], ident[:, :], ALU.add).then_inc(mix_ready, 1)
            dve.sem_inc(paths_used, 2 * U)
            dve.sem_inc(sum_ready, U)
            dve.sem_inc(stored, 16 * U)
            K = 5 + 3 * U + 4
            with dve.Fori(0, GROUPS // 2) as j:
                for m in range(2):
                    i = 2 * j + m
                    link = Chain(dve, own, i, K, waits=dve_waits)
                    rows_x = lambda u: [one(X[:, bass.ds((U * i + u) * TPS + t, 1), :]) for t in range(TPS)]
                    tiles_ps = lambda p: [p[:, t * D:(t + 1) * D] for t in range(TPS)]

                    def ready(sem_, n, of_, u, give):
                        def f():
                            dve.wait_ge(sem_, nth(i, u, n, of_, U))
                            return give(u)
                        return f

                    dve.wait_ge(paths_in[m], PATHS * (j + 1))
                    for u in range(U):
                        ins = dve.tensor_tensor(heads(o[u][:, :, :]), heads(vt[m][u][:, :, :]), gate(U * i + u, 4), ALU.mult)
                    link(ins)
                    for u in range(U):
                        dve.wait_ge(gated, nth(i, u, 0, 1, U))
                        dve.tensor_tensor(o[u][:, :, :], o[u][:, :, :], t1[u][:, :, :], ALU.add).then_inc(sum_ready, 1)
                    for u in range(U):
                        dve.wait_ge(sq_ready, nth(i, u, 0, 1, U))
                        ins = dve.reduce_sum(ss[u][:, :], heads(sq[u][:, :, :]), axis=AX.X)
                    link(ins)
                    for u in range(U):
                        dve.tensor_scalar(ss[u][:, :], ss[u][:, :], 1.0 / DH, 1e-5, ALU.mult, ALU.add).then_inc(means_ready, 1)
                    for u in range(U):
                        dve.wait_ge(root_ready, nth(i, u, 0, 1, U))
                        ins = dve.reciprocal(rs[u][:, :], root[u][:, :])
                    link(ins)
                    for u in range(U):
                        dve.tensor_tensor(heads(o[u][:, :, :]), heads(o[u][:, :, :]), over(rs[u][:, :], DH), ALU.mult).then_inc(rows_ready, 1)
                    dve.sem_inc(paths_used, U)
                    pair_stats(dve, link, [ready(pr_done, 0, 2, u, lambda u: tiles_ps(pr[u])) for u in range(U)], st, mv, sums_ready)
                    for u in range(U):
                        dve.wait_ge(r_ready, nth(i, u, 0, NORMS, U))
                        ins = row_norm(dve, tiles_ps(pr[u]), tiles_of(h1[u]), mv[u], rstd[u])
                    link(ins)
                    for u in range(U):
                        xs = X[:, bass.ds((U * i + u) * TPS, TPS), :]
                        ins = dve.tensor_tensor(xs, xs, h1[u][:, :, :], ALU.add)
                    link.apart(ins)
                    pair_stats(dve, link, [lambda u=u: rows_x(u) for u in range(U)], st, mv, sums_ready)
                    dve.wait_ge(stored, 16 * U * (i + 1))
                    for u in range(U):
                        dve.wait_ge(r_ready, nth(i, u, 1, NORMS, U))
                        row_norm(dve, rows_x(u), tiles_of(c1[u]), mv[u], rstd2[u]).then_inc(rows_ready, 1)
                    for u in range(U):
                        dve.wait_ge(r_ready, nth(i, u, 2, NORMS, U))
                        ins = row_norm(dve, rows_x(u), tiles_of(h0[u]), mv[u], rstd[u])
                    link(ins)
                    for u in range(U):
                        ins = dve.tensor_tensor(h1[u][:, :, :], h0[u][:, :, :], mix_b[:, :].unsqueeze(1).to_broadcast([P, TPS, D]), ALU.add)
                    link(ins)
                    for u in range(U):
                        dve.wait_ge(pr_done, nth(i, u, 1, 2, U))
                        x2 = res["x2"][:, bass.ds((U * i + u) * TPS, TPS), :]
                        ins = dve.tensor_tensor(x2, h1[u][:, :, :], pr[u][:, :].rearrange("p (t d) -> p t d", t=TPS), ALU.add)
                    link.apart(ins)
                    rows_2 = lambda u: [one(res["x2"][:, bass.ds((U * i + u) * TPS + t, 1), :]) for t in range(TPS)]
                    pair_stats(dve, link, [lambda u=u: rows_2(u) for u in range(U)], st, mv, sums_ready)
                    for u in range(U):
                        dve.wait_ge(r_ready, nth(i, u, 3, NORMS, U))
                        row_norm(dve, rows_2(u), tiles_of(c1[u]), mv[u], rstd[u]).then_inc(rows_ready, 1)
                    for u in range(U):
                        dve.wait_ge(rp_done, nth(i, u, 0, 1, U))
                        ins = dve.tensor_copy(res["router"][:, bass.ds((U * i + u) * TPS, TPS), :], rp[u][:, 0:TPS * NE].rearrange("p (t e) -> p t e", e=NE))
                    link(ins)
                    link.end()

        @block.scalar
        def _(act_e):
            act_e.wait_ge(loaded, CONST)
            with act_e.Fori(0, GROUPS) as i:
                for u in range(U):
                    act_e.wait_ge(sum_ready, nth(i, u, 0, 1, U) + U)
                    act_e.activation(flat(sq[u][:, :, :]), flat(o[u][:, :, :]), ACT.Square).then_inc(sq_ready, 1)
                for u in range(U):
                    act_e.wait_ge(means_ready, nth(i, u, 0, 1, U))
                    act_e.activation(root[u][:, :], ss[u][:, :], ACT.Sqrt).then_inc(root_ready, 1)
                for n in range(3):
                    for u in range(U):
                        act_e.wait_ge(tp_done, nth(i, u, n, 3, U))
                        if n == 0:
                            act_e.activation(xT[u][:, :], tp[u][:, :], ACT.Copy).then_inc(xT_ready, 1)
                        else:
                            g = 2 * n - 1
                            act_e.activation(xT[u][:, :], tp[u][:, :], ACT.Identity, bias=cols[:, g + 1:g + 2], scale=cols[:, g:g + 1]).then_inc(xT_ready, 1)
                for u in range(U):
                    act_e.dma_start(scr["c1"][bass.ds(U * i + u, 1), :, :].rearrange("a p n -> (a p) n"), flat(c1[u][:, :, :])).then_inc(stored, 16)
            act_e.wait_ge(stored, 16 * U * (GROUPS + 1))

        @block.tensor
        def _(pe):
            pe.wait_ge(loaded, CONST)
            pe.wait_ge(wo_ready, 1)
            pe.wait_ge(mix_ready, 1)
            with pe.Fori(0, GROUPS) as i:
                for n, (src, rhs, dst) in enumerate(((o, wo, pr), (c1, mix, pr), (c1, rw, rp))):
                    for u in range(U):
                        pe.wait_ge(rows_ready, nth(i, u, n, 3, U))
                        for t in range(TPS):
                            ins = pe.transpose(tp[u][:, t * P:(t + 1) * P], src[u][:, t, :], ident[:, :])
                        ins.then_inc(tp_done, 1)
                    m = NE if n == 2 else D
                    for u in range(U):
                        pe.wait_ge(xT_ready, nth(i, u, n, 3, U))
                        for t in range(TPS):
                            ins = pe.matmul(dst[u][:, t * m:(t + 1) * m], xT[u][:, t * P:(t + 1) * P], rhs[:, :], start=True, stop=True)
                        ins.then_inc(rp_done if n == 2 else pr_done, 1)


ROUND = 1.5 * 2.0 ** 23
TOPK = 2
STEP = 8
NTL = -(-(NT * TOPK + NE - 2) // STEP) * STEP + 1
AHEAD = 2
DEEP = 4
I32 = mybir.dt.int32


def route(nc, w, scr, res):
    with ExitStack() as ctx:
        sb, pb, sem = tensors(nc, ctx, "rt")
        R, E = res["router"], sb("E", [P, NT, NE])
        M = [sb(f"M{k}", [P, NT, NE]) for k in range(TOPK)]
        C, tot, cum, pos = (sb(n, [P, NT, NE]) for n in ("C", "tot", "cum", "pos"))
        m1, sm, i1 = (sb(n, [P, NT]) for n in ("m1", "sm", "i1"))
        ioti = sb("ioti", [P, NTL], I32)
        iot = sb("iot", [P, NTL])
        ones, before = sb("ones", [P, P]), sb("before", [P, P])
        tiles, ends, starts = (sb(n, [P, NE]) for n in ("tiles", "ends", "starts"))
        tile_e = sb("tile_e", [P, NTL])
        slots = sb("slots", [P, TOPK, NT])
        rows = [sb(f"rows{u}", [P, TPS, D]) for u in range(2)]
        sl = [sb(f"sl{u}", [P, TOPK, TPS], I32) for u in range(2)]
        rank_ps, tot_ps = pb("rank_ps", [P, NT, NE]), pb("tot_ps", [P, NT, NE])
        consts, own, sub, exps, counted, ranked, slots_ready = (sem(n) for n in ("consts", "own", "sub", "exps", "counted", "ranked", "slots_ready"))
        rows_in, sent, staged = [sem("rows_in0"), sem("rows_in1")], [sem("sent0"), sem("sent1")], sem("staged")
        freed, pool_waits, weights_in = sem("freed"), sem("pool_waits"), sem("weights_in")
        block = ctx.enter_context(nc.Block())

        @block.sync
        def _(sp):
            for u in range(2):
                sp.sem_inc(freed, 1)
            with sp.Fori(0, BATCH // 2) as i:
                for u in range(2):
                    sp.wait_ge(freed, 2 * i + u + 1)
                    sp.dma_start(flat(rows[u][:, :, :]), scr["c1"][bass.ds(2 * i + u, 1), :, :].rearrange("a p n -> (a p) n")).then_inc(rows_in[u], 16)

        @block.gpsimd
        def _(pool):
            const = Chain(pool, consts)
            const(pool.memset(ones[:, :], 1.0))
            const(pool.memset(before[:, :], 1.0))
            const(pool.affine_select(out=before[:, :], in_=before[:, :], compare_op=ALU.is_gt, fill=0.0, base=0, pattern=[[1, P]], channel_multiplier=-1))
            const(pool.iota(ioti[:, :], pattern=[[1, NTL]], base=0, channel_multiplier=0))
            pool.wait_ge(slots_ready, 1)
            def send(b, u, m):
                pool.tensor_copy(sl[u][:, :, :], res["slots"][:, :, bass.ds(b * TPS, TPS)]).then_inc(staged, 1)
                pool.wait_ge(staged, b + 1)
                wait_apart(pool, rows_in[u], 16 * (m + 1), pool_waits)
                for k in range(TOPK):
                    for t in range(TPS):
                        pool.indirect_dma_start(out=scr["xs"], out_offset=bass.IndirectOffsetOnAxis(ap=sl[u][:, k, t:t + 1], axis=0),
                                                in_=rows[u][:, t, :], in_offset=None).then_inc(sent[u], 16)

            send(0, 0, 0)
            with pool.Fori(0, BATCH // 2 - 1) as i:
                for s in range(2):
                    send(2 * i + 1 + s, 1 - s, i + s)
                    pool.wait_ge(sent[s], (i + 1) * (16 * TOPK * TPS))
                    pool.sem_inc(freed, 1)
            send(BATCH - 1, 1, BATCH // 2 - 1)
            for u in range(2):
                pool.wait_ge(sent[u], (BATCH // 2) * (16 * TOPK * TPS))

        @block.vector
        def _(dve):
            dve.wait_ge(consts, 4)
            link = Chain(dve, own)
            ov = lambda a: over(a[:, :], NE)
            it = iot[:, 0:NE].unsqueeze(1).to_broadcast([P, NT, NE])
            link(dve.tensor_copy(iot[:, :], ioti[:, :]))
            link(dve.reduce_max(m1[:, :], R[:, :, :], axis=AX.X))
            dve.tensor_tensor(E[:, :, :], R[:, :, :], ov(m1), ALU.subtract).then_inc(sub, 1)
            dve.wait_ge(exps, 1)
            link(dve.reduce_sum(sm[:, :], E[:, :, :], axis=AX.X))
            link(dve.reciprocal(sm[:, :], sm[:, :]))
            link(dve.tensor_tensor(E[:, :, :], E[:, :, :], ov(sm), ALU.mult))

            def first_of(vals, best, mask):
                link(dve.reduce_max(best, vals[:, :, :], axis=AX.X))
                link(dve.tensor_tensor(mask[:, :, :], vals[:, :, :], over(best, NE), ALU.is_lt))
                link(dve.scalar_tensor_tensor(mask[:, :, :], mask[:, :, :], float(NE), it, ALU.mult, ALU.add))
                link(dve.tensor_reduce(i1[:, :], mask[:, :, :], axis=AX.X, op=ALU.min))
                link(dve.tensor_tensor(mask[:, :, :], it, ov(i1), ALU.is_equal))

            first_of(E, res["gate"][:, 0, :], M[0])
            link(dve.scalar_tensor_tensor(R[:, :, :], M[0][:, :, :], -2.0, E[:, :, :], ALU.mult, ALU.add))
            first_of(R, res["gate"][:, 1, :], M[1])
            dve.tensor_tensor(C[:, :, :], M[0][:, :, :], M[1][:, :, :], ALU.add).then_inc(counted, 1)
            dve.wait_ge(ranked, 1)
            link(dve.tensor_copy(tot[:, :, :], tot_ps[:, :, :]))
            for e in range(NE):
                ins = dve.tensor_tensor_scan(cum[:, :, e], ones[:, 0:NT], tot[:, :, e], 0.0, ALU.mult, ALU.add)
            link(ins)
            link(dve.tensor_scalar(tiles[:, :], cum[:, NT - 1, :], 1.0 / P, (P - 1.0) / (2 * P), ALU.mult, ALU.add))
            link(dve.tensor_scalar(tiles[:, :], tiles[:, :], ROUND, -ROUND, ALU.add, ALU.add))
            link(dve.tensor_tensor_scan(ends[:, :], ones[:, 0:NE], tiles[:, :], 0.0, ALU.mult, ALU.add))
            link(dve.tensor_tensor(starts[:, :], ends[:, :], tiles[:, :], ALU.subtract))
            link(dve.tensor_scalar(starts[:, :], starts[:, :], float(P), None, ALU.mult))
            link(dve.tensor_tensor(pos[:, :, :], cum[:, :, :], tot[:, :, :], ALU.subtract))
            link(dve.tensor_tensor(pos[:, :, :], pos[:, :, :], rank_ps[:, :, :], ALU.add))
            link(dve.tensor_tensor(pos[:, :, :], pos[:, :, :], starts[:, :].unsqueeze(1).to_broadcast([P, NT, NE]), ALU.add))
            for k in range(TOPK):
                link(dve.tensor_tensor(M[k][:, :, :], M[k][:, :, :], pos[:, :, :], ALU.mult))
                link(dve.reduce_sum(slots[:, k, :], M[k][:, :, :], axis=AX.X))
            dve.tensor_copy(res["slots"][:, :, :], slots[:, :, :]).then_inc(slots_ready, 1)
            link(dve.memset(tile_e[:, :], 0.0))
            for e in range(NE):
                link(dve.scalar_tensor_tensor(tile_e[:, :], iot[:, :], ends[:, e:e + 1], tile_e[:, :], ALU.is_ge, ALU.add))
            link(dve.tensor_scalar(tile_e[:, :], tile_e[:, :], NE - 1.0, None, ALU.min))
            link(dve.tensor_copy(res["tile_e"][:, :], tile_e[:, :]))

        @block.scalar
        def _(act_e):
            for name in ("b1", "b2"):
                act_e.dma_start(res["ex_" + name][:, :, :], w[name].partition_broadcast(P)).then_inc(weights_in, 16)
            act_e.dma_start(res["ex_w1"][:, :, :], w["w1"].rearrange("e d f -> d e f")).then_inc(weights_in, 16)
            act_e.dma_start(res["ex_w2"][:, :, :].rearrange("p e (c d) -> p e c d", c=FC), w["w2"].rearrange("e (c f) d -> f e c d", f=P)).then_inc(weights_in, 16)
            act_e.dma_start(res["ex_cols"][:, :], w["ao_cols"]).then_inc(weights_in, 16)
            act_e.wait_ge(sub, 1)
            act_e.activation(E[:, :, :], E[:, :, :], ACT.Exp).then_inc(exps, 1)
            act_e.wait_ge(weights_in, 16 * 5)

        @block.tensor
        def _(pe):
            pe.wait_ge(counted, 1)
            pe.matmul(rank_ps[:, :, :], before[:, :], C[:, :, :], start=True, stop=True)
            pe.matmul(tot_ps[:, :, :], ones[:, :], C[:, :, :], start=True, stop=True).then_inc(ranked, 1)


def experts(nc, w, scr, res):
    with ExitStack() as ctx:
        sb, pb, sem = tensors(nc, ctx, "ex")
        w1, w2, b1, b2, cols = (res[n] for n in ("ex_w1", "ex_w2", "ex_b1", "ex_b2", "ex_cols"))
        xin = [sb(f"xin{u}", [P, D]) for u in range(DEEP)]
        xT = [sb(f"xT{u}", [D, P]) for u in range(2)]
        hid = [sb(f"hid{u}", [P, FF]) for u in range(2)]
        hT = [sb(f"hT{u}", [P, FF]) for u in range(2)]
        ys = [sb(f"ys{u}", [P, D]) for u in range(2)]
        x_ps, h_ps, t_ps, y_ps = ([pb(f"{n}{u}", [P, 512]) for u in range(2)] for n in ("xp", "hp", "tp", "yp"))
        xt_done, xT_ready, h_done, hid_ready, ht_done, hT_ready, y_done, ys_ready = (
            sem(n) for n in ("xt_done", "xT_ready", "h_done", "hid_ready", "ht_done", "hT_ready", "y_done", "ys_ready"))
        rows_in, out_done = [sem(f"rows_in{u}") for u in range(DEEP)], [sem("out_done0"), sem("out_done1")]
        block = ctx.enter_context(nc.Block())
        ident, tile_e = res["ident"], res["tile_e"]
        xs, yr = (scr[n].rearrange("(i p) d -> i p d", p=P) for n in ("xs", "ys"))
        last = NTL - 1

        @block.sync
        def _(sp):
            def load(j, u):
                if not isinstance(j, int) or j >= DEEP:
                    sp.wait_ge(xt_done, j - DEEP + 3)
                sp.dma_start(xin[u][:, :], xs[bass.ds(j, 1), :, :].rearrange("a p d -> (a p) d")).then_inc(rows_in[u], 16)

            for j in range(1 + DEEP):
                load(j, j % DEEP)
            with sp.Fori(0, last // STEP) as n:
                for s in range(STEP):
                    i = STEP * n + 1 + s
                    load(i + DEEP, (1 + s) % DEEP)
                    sp.wait_ge(ys_ready, i)
                    sp.dma_start(yr[bass.ds(i - 1, 1), :, :].rearrange("a p d -> (a p) d"), ys[s % 2][:, :]).then_inc(out_done[s % 2], 16)
            sp.wait_ge(ys_ready, NTL)
            sp.dma_start(yr[last], ys[last % 2][:, :]).then_inc(out_done[last % 2], 16)
            sp.wait_ge(out_done[0], 16 * (last // 2 + 2))
            sp.wait_ge(out_done[1], 16 * (last // 2 + 1))

        def expert_of(eng, i):
            return eng.value_load(tile_e[0:1, bass.ds(i, 1)], min_val=0, max_val=NE - 1)

        @block.vector
        def _(dve):
            def bias_up(i, u, e):
                dve.wait_ge(h_done, i + 1)
                dve.tensor_tensor(hid[u][:, :], h_ps[u][:, :], b1[:, bass.ds(e, 1), :].rearrange("p a f -> p (a f)"), ALU.add).then_inc(hid_ready, 1)

            def bias_down(i, u, e, m):
                dve.wait_ge(y_done, i + 3)
                dve.wait_ge(out_done[u], 16 * (m + 1))
                dve.tensor_tensor(ys[u][:, :], y_ps[u][:, 0:D], b2[:, bass.ds(e, 1), :].rearrange("p a d -> p (a d)"), ALU.add).then_inc(ys_ready, 1)

            for u in range(2):
                dve.sem_inc(out_done[u], 16)
            bias_up(0, 0, expert_of(dve, 0))
            with dve.Fori(0, last // STEP) as n:
                before = expert_of(dve, STEP * n)
                for s in range(STEP):
                    i = STEP * n + 1 + s
                    e = expert_of(dve, i)
                    bias_up(i, (1 + s) % 2, e)
                    bias_down(i - 1, s % 2, before, STEP // 2 * n + s // 2)
                    before = e
            bias_down(last, last % 2, expert_of(dve, last), last // 2)

        @block.scalar
        def _(act_e):
            def affine(j, u):
                act_e.wait_ge(xt_done, j + 3)
                act_e.activation(xT[u][:, :], x_ps[u][:, 0:P], ACT.Identity, bias=cols[:, 4:5], scale=cols[:, 3:4]).then_inc(xT_ready, 1)

            def silu(i, u):
                act_e.wait_ge(ht_done, i + 1)
                act_e.wait_ge(y_done, i + 1)
                act_e.activation(hT[u][:, :], t_ps[u][:, :], ACT.Silu).then_inc(hT_ready, 1)

            for j in range(AHEAD):
                affine(j, j % 2)
            silu(0, 0)
            affine(AHEAD, AHEAD % 2)
            with act_e.Fori(0, last // STEP) as n:
                for s in range(STEP):
                    i = STEP * n + 1 + s
                    silu(i, (1 + s) % 2)
                    affine(i + AHEAD, (1 + s) % 2)

        @block.tensor
        def _(pe):
            for u in range(2):
                pe.sem_inc(xt_done, 1)
                pe.sem_inc(y_done, 1)

            def turn_rows(j, u, v, m):
                pe.wait_ge(rows_in[v], 16 * (m + 1))
                pe.transpose(x_ps[u][:, 0:P], xin[v][:, :], ident[:, :]).then_inc(xt_done, 1)

            def up(i, u, e):
                pe.wait_ge(xT_ready, i + 1)
                pe.matmul(h_ps[u][:, :], xT[u][:, :], w1[:, bass.ds(e, 1), :].rearrange("p a f -> p (a f)"), start=True, stop=True).then_inc(h_done, 1)

            def turn_hidden(i, u):
                pe.wait_ge(hid_ready, i + 1)
                for f in range(FC):
                    ins = pe.transpose(t_ps[u][:, f * P:(f + 1) * P], hid[u][:, f * P:(f + 1) * P], ident[:, :])
                ins.then_inc(ht_done, 1)

            def down(i, u, e):
                pe.wait_ge(hT_ready, i + 1)
                for f in range(FC):
                    w2f = w2[:, bass.ds(e, 1), f * D:(f + 1) * D].rearrange("p a d -> p (a d)")
                    ins = pe.matmul(y_ps[u][:, 0:D], hT[u][:, f * P:(f + 1) * P], w2f, start=(f == 0), stop=(f == FC - 1))
                ins.then_inc(y_done, 1)

            for j in range(AHEAD):
                turn_rows(j, j % 2, j % DEEP, j // DEEP)
            up(0, 0, expert_of(pe, 0))
            turn_hidden(0, 0)
            turn_rows(AHEAD, AHEAD % 2, AHEAD % DEEP, AHEAD // DEEP)
            with pe.Fori(0, last // STEP) as n:
                before, e = expert_of(pe, STEP * n), expert_of(pe, STEP * n + 1)
                for s in range(STEP):
                    i = STEP * n + 1 + s
                    u = (1 + s) % 2
                    up(i, u, e)
                    after = expert_of(pe, i + 1) if s < STEP - 1 else None
                    down(i - 1, s % 2, before)
                    turn_rows(i + AHEAD, u, (1 + s + AHEAD) % DEEP, STEP // DEEP * n + (1 + s + AHEAD) // DEEP)
                    turn_hidden(i, u)
                    before, e = e, after
            down(last, last % 2, expert_of(pe, last))


def gate_loop(nc, w, scr, res):
    U = 4
    with ExitStack() as ctx:
        sb, pb, sem = tensors(nc, ctx, "gl")
        each = lambda name, shape, dt=FP32: [sb(f"{name}{u}", shape, dt) for u in range(U)]
        names = ("wq", "wk", "wv", "wa", "wg", "wo")
        W = {n: sb(n, [D, D]) for n in names}
        gamma = sb("gamma", [D, 1])
        mhalf = sb("mhalf", [P, TPS])
        st, mv, rstd = each("st", [P, TPS, 6]), each("mv", [P, TPS, 2]), each("rstd", [P, TPS])
        f, h, o = (each(n, [P, TPS, D]) for n in ("f", "h", "o"))
        xT, k, a, sg, y = (each(n, [D, SEQ]) for n in ("xT", "k", "a", "sg", "y"))
        yk = [each(f"yk{m}", [P, TOPK, TPS, D]) for m in range(2)]
        sl = [each(f"sl{m}", [P, TOPK, TPS], I32) for m in range(2)]
        main, side = ([pb(f"{n}{u}", [P, SEQ]) for u in range(U)] for n in ("main", "side"))
        loaded, consts, own, sums_ready, eps_added, r_ready, h_ready, tp_done, xT_ready, proj_done, k_ready, a_ready, sg_ready, y_ready, o_done, g_ready, kv_ready = (
            sem(n) for n in ("loaded", "consts", "own", "sums_ready", "eps_added", "r_ready", "h_ready", "tp_done", "xT_ready", "proj_done", "k_ready",
                             "a_ready", "sg_ready", "y_ready", "o_done", "g_ready", "kv_ready"))
        pool_waits, dve_waits = sem("pool_waits"), sem("dve_waits")
        rows_in = [[sem(f"rows_in{m}{u}") for u in range(U)] for m in range(2)]
        rows_used, staged = sem("rows_used"), sem("staged")
        block = ctx.enter_context(nc.Block())
        X, ident = res["x"], res["ident"]
        GROUPS = BATCH // U
        NORMS, PROJ = 3, 5
        SCALES = ((1.0, 1e-5), (D + 1e-5, 1e-10), (1.0, 1e-5))

        @block.sync
        def _(sp):
            for n in names:
                sp.dma_start(W[n][:, :], w[f"gl_{n}"]).then_inc(loaded, 16)
            sp.dma_start(gamma[:, :], w["gamma"]).then_inc(loaded, 16)

        @block.gpsimd
        def _(pool):
            pool.memset(mhalf[:, :], -0.5).then_inc(consts, 1)
            pool.wait_ge(consts, 1)

            def stage(i, m):
                pool.wait_ge(rows_used, U * i + U)
                for u in range(U):
                    pool.tensor_copy(sl[m][u][:, :, :], res["slots"][:, :, bass.ds((U * i + u) * TPS, TPS)]).then_inc(staged, 1)
                wait_apart(pool, staged, U * i + U, pool_waits)

            def gather(m, part, parts):
                every = [(u, n, t) for u in range(U) for n in range(TOPK) for t in range(TPS)]
                for u, n, t in every[len(every) * part // parts:len(every) * (part + 1) // parts]:
                    pool.indirect_dma_start(out=yk[m][u][:, n, t, :], out_offset=None, in_=scr["ys"],
                                            in_offset=bass.IndirectOffsetOnAxis(ap=sl[m][u][:, n, t:t + 1], axis=0)).then_inc(rows_in[m][u], 16)

            def powers(i, n):
                for u in range(U):
                    wait_apart(pool, sums_ready, nth(i, u, n, NORMS, U), pool_waits)
                    pool.tensor_scalar(rstd[u][:, :], mv[u][:, :, 1], *SCALES[n], ALU.mult, ALU.add).then_inc(eps_added, 1)
                    pool.wait_ge(eps_added, nth(i, u, n, NORMS, U))
                    pool.tensor_tensor(rstd[u][:, :], rstd[u][:, :], mhalf[:, :], ALU.pow).then_inc(r_ready, 1)

            def group(i, m, more):
                powers(i, 0)
                if more:
                    stage(i + 1, 1 - m)
                    gather(1 - m, 0, 4)
                powers(i, 1)
                if more:
                    for part in range(1, 4):
                        gather(1 - m, part, 4)
                powers(i, 2)

            stage(0, 0)
            gather(0, 0, 1)
            with pool.Fori(0, GROUPS // 2 - 1) as j:
                for m in range(2):
                    group(2 * j + m, m, True)
            group(GROUPS - 2, 0, True)
            group(GROUPS - 1, 1, False)

        @block.vector
        def _(dve):
            dve.wait_ge(loaded, 16 * 7)
            dve.tensor_scalar(gamma[:, :], gamma[:, :], float(D) ** 0.5, None, ALU.mult).then_inc(g_ready, 1)
            dve.sem_inc(rows_used, 2 * U)
            K = 3 * U + 8
            with dve.Fori(0, GROUPS // 2) as j:
                for m in range(2):
                    i = 2 * j + m
                    link = Chain(dve, own, i, K, waits=dve_waits)
                    rows = lambda r, u: [one(r[:, bass.ds((U * i + u) * TPS + t, 1), :]) for t in range(TPS)]
                    for n in range(TOPK):
                        for u in range(U):
                            if n == 0:
                                dve.wait_ge(rows_in[m][u], (j + 1) * (16 * TOPK * TPS))
                            left = rows(res["x2"], u) if n == 0 else tiles_of(f[u])
                            for t in range(TPS):
                                ins = dve.scalar_tensor_tensor(f[u][:, t, :], yk[m][u][:, n, t, :],
                                                               res["gate"][:, n, bass.ds((U * i + u) * TPS + t, 1)], left[t], ALU.mult, ALU.add)
                        link(ins)
                    dve.sem_inc(rows_used, U)
                    pair_stats(dve, link, [lambda u=u: tiles_of(f[u]) for u in range(U)], st, mv, sums_ready)
                    for u in range(U):
                        dve.wait_ge(r_ready, nth(i, u, 0, NORMS, U))
                        ins = row_norm(dve, tiles_of(f[u]), tiles_of(f[u]), mv[u], rstd[u])
                    link(ins)
                    for u in range(U):
                        xs = X[:, bass.ds((U * i + u) * TPS, TPS), :]
                        ins = dve.tensor_tensor(xs, xs, f[u][:, :, :], ALU.add)
                    link.apart(ins)
                    pair_stats(dve, link, [lambda u=u: rows(X, u) for u in range(U)], st, mv, sums_ready)
                    for u in range(U):
                        dve.wait_ge(r_ready, nth(i, u, 1, NORMS, U))
                        row_norm(dve, rows(X, u), tiles_of(h[u]), mv[u], rstd[u]).then_inc(h_ready, 1)
                    for u in range(U):
                        dve.wait_ge(k_ready, nth(i, u, 0, 1, U))
                        dve.wait_ge(proj_done, nth(i, u, 1, PROJ, U))
                        dve.tensor_tensor(k[u][:, :], k[u][:, :], main[u][:, :], ALU.mult).then_inc(kv_ready, 1)
                    for u in range(U):
                        dve.wait_ge(a_ready, nth(i, u, 0, 1, U))
                        dve.wait_ge(kv_ready, nth(i, u, 0, 1, U))
                        ins = dve.tensor_tensor_scan(y[u][:, :], a[u][:, :], k[u][:, :], 0.0, ALU.mult, ALU.add)
                    link(ins)
                    for u in range(U):
                        dve.wait_ge(proj_done, nth(i, u, 3, PROJ, U))
                        ins = dve.tensor_tensor(y[u][:, :], y[u][:, :], main[u][:, :], ALU.mult)
                    link(ins)
                    for u in range(U):
                        dve.wait_ge(sg_ready, nth(i, u, 0, 1, U))
                        dve.tensor_tensor(y[u][:, :], y[u][:, :], sg[u][:, :], ALU.mult).then_inc(y_ready, 1)

                    def projected(u):
                        def rows_of_output():
                            dve.wait_ge(o_done, nth(i, u, 0, 1, U))
                            return [main[u][:, t * D:(t + 1) * D] for t in range(TPS)]
                        return rows_of_output

                    pair_stats(dve, link, [projected(u) for u in range(U)], st, mv, sums_ready)
                    for u in range(U):
                        dve.wait_ge(r_ready, nth(i, u, 2, NORMS, U))
                        ins = row_norm(dve, [main[u][:, t * D:(t + 1) * D] for t in range(TPS)], tiles_of(o[u]), mv[u], rstd[u])
                    link(ins)
                    for u in range(U):
                        xs = X[:, bass.ds((U * i + u) * TPS, TPS), :]
                        ins = dve.tensor_tensor(xs, xs, o[u][:, :, :], ALU.add)
                    ins.then_inc(own, 1)
                    link.n += 1
                    link.end()
            dve.wait_ge(own, K * GROUPS)

        @block.scalar
        def _(act_e):
            act_e.wait_ge(g_ready, 1)
            with act_e.Fori(0, GROUPS) as i:
                for u in range(U):
                    act_e.wait_ge(tp_done, nth(i, u, 0, 1, U))
                    act_e.activation(xT[u][:, :], main[u][:, :], ACT.Copy, scale=gamma[:, 0:1]).then_inc(xT_ready, 1)
                for n, dst, src, func, ready in ((0, k, side, ACT.Copy, k_ready), (2, a, side, ACT.Sigmoid, a_ready), (4, sg, side, ACT.Silu, sg_ready)):
                    for u in range(U):
                        act_e.wait_ge(proj_done, nth(i, u, n, PROJ, U))
                        act_e.activation(dst[u][:, :], src[u][:, :], func).then_inc(ready, 1)

        @block.tensor
        def _(pe):
            pe.wait_ge(loaded, 16 * 7)
            with pe.Fori(0, GROUPS) as i:
                for u in range(U):
                    pe.wait_ge(h_ready, nth(i, u, 0, 1, U))
                    for t in range(TPS):
                        ins = pe.transpose(main[u][:, t * P:(t + 1) * P], h[u][:, t, :], ident[:, :])
                    ins.then_inc(tp_done, 1)
                for n, (name, dst, free) in enumerate((("wk", side, xT_ready), ("wv", main, None), ("wa", side, k_ready), ("wq", main, kv_ready),
                                                       ("wg", side, a_ready))):
                    for u in range(U):
                        if free:
                            pe.wait_ge(free, nth(i, u, 0, 1, U))
                        pe.matmul(dst[u][:, :], W[name][:, :], xT[u][:, :], start=True, stop=True).then_inc(proj_done, 1)
                for u in range(U):
                    pe.wait_ge(y_ready, nth(i, u, 0, 1, U))
                    for t in range(TPS):
                        ins = pe.matmul(main[u][:, t * D:(t + 1) * D], y[u][:, t * P:(t + 1) * P], W["wo"][:, :], start=True, stop=True)
                    ins.then_inc(o_done, 1)


def phase_ffn(nc, w, res, out):
    TWO_PI = 6.283185307179586
    ROUND = 1.5 * 2.0 ** 23
    HI = 6.28125
    MID = 0.0019350051879882812
    LO = TWO_PI - HI - MID
    U = 4
    with ExitStack() as ctx:
        sb, pb, sem = tensors(nc, ctx, "pf")
        w1, w2 = sb("w1", [D, FF]), sb("w2", [P, FC, D])
        cf = sb("cf", [P, 4, FC])
        b2 = sb("b2", [P, D])
        th, nn, sn, cs, c = (sb(n, [P, FC]) for n in ("th", "nn", "sn", "cs", "c"))
        mhalf = sb("mhalf", [P, TPS])
        each = lambda name, shape: [sb(f"{name}{u}", shape) for u in range(U)]
        st, mv, rstd = each("st", [P, TPS, 6]), each("mv", [P, TPS, 2]), each("rstd", [P, TPS])
        h, o = each("h", [P, TPS, D]), each("o", [P, TPS, D])
        xT = each("xT", [D, SEQ])
        hid, turn, near = ([each(f"{n}{f}", [P, SEQ]) for f in range(FC)] for n in ("hid", "turn", "near"))
        bank = [[pb(f"bank{m}{u}", [P, SEQ]) for u in range(U)] for m in range(2)]
        tp = op = bank[0]
        loaded, consts, coef, trig, done, halfpi, own, sums_ready, eps_added, r_ready, h_ready, tp_done, xT_ready = (
            sem(n) for n in ("loaded", "consts", "coef", "trig", "done", "halfpi", "own", "sums_ready", "eps_added", "r_ready", "h_ready", "tp_done", "xT_ready"))
        hp_done, hid_ready, near_ready, frac, sine_ready, sum_ready, relu_ready, o_done, o_ready, x_ready, out_done = (
            sem(n) for n in ("hp_done", "hid_ready", "near_ready", "frac", "sine_ready", "sum_ready", "relu_ready", "o_done", "o_ready", "x_ready", "out_done"))
        pool_waits, dve_waits = sem("pool_waits"), sem("dve_waits")
        block = ctx.enter_context(nc.Block())
        X, ident = res["x"], res["ident"]
        GROUPS = BATCH // U

        def chunk(i, u, f):
            return i * (U * FC) + (u * FC + f + 1)

        steps = [(u, f) for u in range(U) for f in range(FC)]

        @block.sync
        def _(sp):
            sp.dma_start(w1[:, :], w["pf_w1"]).then_inc(loaded, 16)
            sp.dma_start(w2[:, :, :], w["pf_w2"].rearrange("(c f) d -> f c d", f=P)).then_inc(loaded, 16)
            sp.dma_start(cf[:, :, :], w["pf_cols"]).then_inc(loaded, 16)
            sp.dma_start(b2[:, :], w["pf_b2"].partition_broadcast(P)).then_inc(loaded, 16)
            with sp.Fori(0, BATCH) as b:
                sp.wait_ge(x_ready, b + (U + 1))
                sp.dma_start(out[bass.ds(b, 1), :, :].rearrange("a (t p) d -> p (a t) d", p=P), X[:, bass.ds(b * TPS, TPS), :]).then_inc(out_done, 16)
            sp.wait_ge(out_done, 16 * BATCH)

        @block.gpsimd
        def _(pool):
            pool.memset(mhalf[:, :], -0.5).then_inc(consts, 1)
            pool.wait_ge(consts, 1)
            pool.sem_inc(x_ready, U)

            def powers(i, n):
                for u in range(U):
                    wait_apart(pool, sums_ready, nth(i, u, n, 2, U), pool_waits)
                    pool.tensor_scalar(rstd[u][:, :], mv[u][:, :, 1], 1e-5, None, ALU.add).then_inc(eps_added, 1)
                    pool.wait_ge(eps_added, nth(i, u, n, 2, U))
                    pool.tensor_tensor(rstd[u][:, :], rstd[u][:, :], mhalf[:, :], ALU.pow).then_inc(r_ready, 1)

            with pool.Fori(0, GROUPS) as i:
                powers(i, 0)
                for u, f in steps:
                    pool.wait_ge(near_ready, chunk(i, u, f))
                    pool.tensor_tensor(turn[f][u][:, :], turn[f][u][:, :], near[f][u][:, :], ALU.subtract).then_inc(frac, 1)
                powers(i, 1)
                for u in range(U):
                    xs = X[:, bass.ds((U * i + u) * TPS, TPS), :]
                    pool.wait_ge(o_ready, nth(i, u, 0, 1, U))
                    pool.tensor_tensor(xs, xs, o[u][:, :, :], ALU.add).then_inc(x_ready, 1)

        @block.vector
        def _(dve):
            dve.wait_ge(loaded, 64)
            start = Chain(dve, coef, 0, 16)
            b1, phase, real, imag = (cf[:, n, :] for n in range(4))

            def wrap(dst, src):
                start(dve.tensor_scalar(nn[:, :], src, 1.0 / TWO_PI, ROUND, ALU.mult, ALU.add))
                start(dve.tensor_scalar(nn[:, :], nn[:, :], -ROUND, None, ALU.add))
                start(dve.scalar_tensor_tensor(dst, nn[:, :], -HI, src, ALU.mult, ALU.add))
                start(dve.scalar_tensor_tensor(dst, nn[:, :], -MID, dst, ALU.mult, ALU.add))
                start(dve.scalar_tensor_tensor(dst, nn[:, :], -LO, dst, ALU.mult, ALU.add))
                start(dve.tensor_scalar(dst, dst, -3.141592, 3.141592, ALU.max, ALU.min))

            wrap(th[:, :], phase)
            start(dve.tensor_scalar(cs[:, :], th[:, :], TWO_PI / 4, None, ALU.add))
            wrap(cs[:, :], cs[:, :])
            dve.tensor_scalar(nn[:, :], nn[:, :], 0.0, None, ALU.mult).then_inc(halfpi, 1)
            dve.wait_ge(trig, 2)
            start(dve.tensor_tensor(cs[:, :], cs[:, :], real, ALU.mult))
            start(dve.tensor_tensor(sn[:, :], sn[:, :], imag, ALU.mult))
            start(dve.tensor_tensor(c[:, :], cs[:, :], sn[:, :], ALU.add))
            dve.scalar_tensor_tensor(c[:, :], c[:, :], 0.1, imag, ALU.mult, ALU.mult).then_inc(done, 1)
            dve.tensor_scalar(th[:, :], th[:, :], 1.0 / TWO_PI, None, ALU.mult).then_inc(done, 1)
            dve.wait_ge(done, 2)
            start.end()
            K = 4 * U
            with dve.Fori(0, GROUPS) as i:
                link = Chain(dve, own, i, K, waits=dve_waits)
                rows = lambda u: [one(X[:, bass.ds((U * i + u) * TPS + t, 1), :]) for t in range(TPS)]
                pair_stats(dve, link, [lambda u=u: rows(u) for u in range(U)], st, mv, sums_ready)
                for u in range(U):
                    dve.wait_ge(r_ready, nth(i, u, 0, 2, U))
                    row_norm(dve, rows(u), tiles_of(h[u]), mv[u], rstd[u]).then_inc(h_ready, 1)
                for v in range(U + 1):
                    if v < U:
                        for f in range(FC):
                            dve.wait_ge(hid_ready, chunk(i, v, f))
                            ins = dve.tensor_scalar(turn[f][v][:, :], hid[f][v][:, :], 0.1 / TWO_PI, th[:, f:f + 1], ALU.mult, ALU.add)
                        link(ins)
                        for f in range(FC):
                            dve.tensor_scalar(near[f][v][:, :], turn[f][v][:, :], ROUND, -ROUND, ALU.add, ALU.add).then_inc(near_ready, 1)
                    if v > 0:
                        for f in range(FC):
                            dve.wait_ge(sine_ready, chunk(i, v - 1, f))
                            dve.scalar_tensor_tensor(hid[f][v - 1][:, :], turn[f][v - 1][:, :], c[:, f:f + 1], hid[f][v - 1][:, :], ALU.mult, ALU.add).then_inc(sum_ready, 1)
                dve.wait_ge(x_ready, U * i + U)
                for u in range(U):
                    dve.wait_ge(o_done, nth(i, u, 0, 1, U))
                    link(dve.tensor_tensor(o[u][:, :, :], op[u][:, :].rearrange("p (t d) -> p t d", d=D), b2[:, :].unsqueeze(1).to_broadcast([P, TPS, D]), ALU.add))
                pair_stats(dve, link, [lambda u=u: tiles_of(o[u]) for u in range(U)], st, mv, sums_ready)
                for u in range(U):
                    dve.wait_ge(r_ready, nth(i, u, 1, 2, U))
                    row_norm(dve, tiles_of(o[u]), tiles_of(o[u]), mv[u], rstd[u]).then_inc(o_ready, 1)
                link.end()

        @block.scalar
        def _(act_e):
            act_e.wait_ge(halfpi, 1)
            act_e.activation(sn[:, :], th[:, :], ACT.Sin).then_inc(trig, 1)
            act_e.activation(cs[:, :], cs[:, :], ACT.Sin).then_inc(trig, 1)
            with act_e.Fori(0, GROUPS) as i:
                for u in range(U):
                    act_e.wait_ge(tp_done, nth(i, u, 0, 1, U))
                    act_e.activation(xT[u][:, :], tp[u][:, :], ACT.Copy).then_inc(xT_ready, 1)
                SINE, RECTIFY = 6, 9
                for n in range(len(steps) + RECTIFY):
                    if n < len(steps):
                        u, f = steps[n]
                        act_e.wait_ge(hp_done, chunk(i, u, f))
                        act_e.activation(hid[f][u][:, :], bank[(f + 1) % 2][u][:, :], ACT.Identity, bias=cf[:, 0, f:f + 1]).then_inc(hid_ready, 1)
                    if SINE <= n < len(steps) + SINE:
                        u, f = steps[n - SINE]
                        act_e.wait_ge(frac, chunk(i, u, f))
                        act_e.activation(turn[f][u][:, :], turn[f][u][:, :], ACT.Sin, scale=6.283185).then_inc(sine_ready, 1)
                    if n >= RECTIFY:
                        u, f = steps[n - RECTIFY]
                        act_e.wait_ge(sum_ready, chunk(i, u, f))
                        act_e.activation(hid[f][u][:, :], hid[f][u][:, :], ACT.Relu).then_inc(relu_ready, 1)

        @block.tensor
        def _(pe):
            pe.wait_ge(loaded, 64)
            with pe.Fori(0, GROUPS) as i:
                for u in range(U):
                    pe.wait_ge(h_ready, nth(i, u, 0, 1, U))
                    for t in range(TPS):
                        ins = pe.transpose(tp[u][:, t * P:(t + 1) * P], h[u][:, t, :], ident[:, :])
                    ins.then_inc(tp_done, 1)
                for u, f in steps:
                    if f == 0:
                        pe.wait_ge(xT_ready, nth(i, u, 0, 1, U))
                    if f >= 2:
                        pe.wait_ge(hid_ready, chunk(i, u, f - 2))
                    pe.matmul(bank[(f + 1) % 2][u][:, :], w1[:, f * P:(f + 1) * P], xT[u][:, :], start=True, stop=True).then_inc(hp_done, 1)
                for u in range(U):
                    pe.wait_ge(relu_ready, chunk(i, u, FC - 1))
                    for t in range(TPS):
                        for f in range(FC):
                            ins = pe.matmul(op[u][:, t * D:(t + 1) * D], hid[f][u][:, t * P:(t + 1) * P], w2[:, f, :], start=(f == 0), stop=(f == FC - 1))
                    ins.then_inc(o_done, 1)


def build(nc, w, out):
    scr = {name: nc.dram_tensor(f"scratch_{name}", shape, FP32, kind="Internal").ap() for name, shape in (
        ("v", (BATCH, WIN + SEQ, D)), ("k", (BATCH, P, SEQ)), ("kb", (BATCH, P, SEQ)), ("vb", (BATCH, P, SEQ)), ("qT", (BATCH, D, SEQ)),
        ("A", (BATCH, P, SEQ)), ("attnT", (BATCH, P, SEQ)), ("T", (BATCH // 2, P, CH * CH)), ("probs", (BATCH * SEQ, H * NGATE)),
        ("ofir", (BATCH, SEQ, D)), ("o", (BATCH, P, SEQ)), ("c1", (BATCH, P, SEQ)),
        ("xs", ((NTL + DEEP) * P, D)), ("ys", (NTL * P, D)))}
    with ExitStack() as ctx:
        def sb(name, shape):
            return ctx.enter_context(nc.sbuf_tensor(name, shape, FP32))

        res = {"x": sb("x_rows", [P, NT, D]), "ident": sb("ident", [P, P])}
        with ExitStack() as mid:
            for name, shape in (("probs", [P, NT, H * NGATE]), ("eps", [P, H]), ("inv_temp", [P, H]), ("rq", [P, NT, H])):
                res[name] = mid.enter_context(nc.sbuf_tensor(name, shape, FP32))
            with nc.sbuf_tensor("logits", [P, NT, H * NGATE], FP32) as res["logits"]:
                delta_inputs(nc, w["x"], w, scr, res)
                fir_and_inverses(nc, w, scr, res)
            delta_rule(nc, scr, res)
            with ExitStack() as ffn:
                for name, shape, dt in (("x2", [P, NT, D], FP32), ("router", [P, NT, NE], FP32), ("gate", [P, TOPK, NT], FP32),
                                        ("slots", [P, TOPK, NT], I32), ("tile_e", [P, NTL], I32)):
                    res[name] = ffn.enter_context(nc.sbuf_tensor(name, shape, dt))
                attention_output(nc, w, scr, res)
                with ExitStack() as weights:
                    for name, shape in (("w1", [D, NE, FF]), ("w2", [P, NE, FC * D]), ("b1", [P, NE, FF]), ("b2", [P, NE, D]), ("cols", [D, 5])):
                        res["ex_" + name] = weights.enter_context(nc.sbuf_tensor("ex_" + name, shape, FP32))
                    route(nc, w, scr, res)
                    experts(nc, w, scr, res)
                gate_loop(nc, w, scr, res)
        phase_ffn(nc, w, res, out)


def kernel(**inputs):
    import numpy as np
    import concourse.bacc as bacc
    from concourse.bass_utils import run_bass_kernel_spmd

    nc = bacc.Bacc("TRN2", target_bir_lowering=False, num_devices=1)
    a = {k: np.asarray(v) for k, v in inputs.items()}
    L0, F0, L1, F1 = "L0_attn_", "L0_ffn_", "L1_attn_", "L1_ffn_"
    firs = np.zeros((D, len(FIRS), PADW), np.float32)
    for n, (name, k) in enumerate(zip(("fir_s", "fir_m", "fir_l"), FIRS)):
        firs[:, n, 2 * WIN - k:2 * WIN] = a[L0 + name].reshape(D, k)
    laid = {
        "x": a[L0 + "hidden_states"], "wqT": a[L0 + "Wq"].T, "wkT": a[L0 + "Wk"].T, "wvT": a[L0 + "Wv"].T, "woT": a[L0 + "Wo"].T,
        "gatesT": np.concatenate([a[L0 + "gate_w"].reshape(H * NGATE, D), a[L0 + "Wb"]]).T,
        "taps": np.stack([a[L0 + "conv_q"], a[L0 + "conv_k"], a[L0 + "conv_v"]], 1),
        "gate_b": a[L0 + "gate_b"].reshape(-1), "log_temp": a[L0 + "log_temp"].reshape(-1), "eps": a[L0 + "eps_param"].reshape(-1),
        "fir_pad": firs.reshape(D * len(FIRS), PADW),
        "ao_cols": np.stack([np.tile(a[L0 + "norm_w"], H), a[F0 + "g1"], a[F0 + "be1"], a[F0 + "g2"], a[F0 + "be2"]], 1),
        "mix_w": a[F0 + "mix_w"], "mix_b": a[F0 + "mix_b"], "router_w": a[F0 + "router_w"], "w1": a[F0 + "w1"], "w2": a[F0 + "w2"],
        "b1": a[F0 + "b1"], "b2": a[F0 + "b2"],
        "gamma": a[L1 + "gamma"].reshape(D, 1), **{f"gl_{n}": a[L1 + n] for n in ("wq", "wk", "wv", "wa", "wg", "wo")},
        "pf_w1": a[F1 + "W1"], "pf_w2": a[F1 + "W2"], "pf_b2": a[F1 + "b2"],
        "pf_cols": np.stack([a[F1 + n].reshape(FC, P).T for n in ("b1", "quantum_phases", "quantum_weights_real", "quantum_weights_imag")], 1),
    }
    arrays = {f"in_{k}": np.ascontiguousarray(v) for k, v in laid.items()}
    w = {k: nc.dram_tensor(f"in_{k}", arrays[f"in_{k}"].shape, FP32, kind="ExternalInput").ap() for k in laid}
    out = nc.dram_tensor("out", (BATCH, SEQ, D), FP32, kind="ExternalOutput").ap()
    build(nc, w, out)
    return run_bass_kernel_spmd(nc, [arrays], core_ids=[0]).results[0]["out"]
```
